# Optimizing a Trainium2 kernel written in Bass

```python
import numpy as np
import jax
import jax.numpy as jnp

def _softmax(x, axis=-1):
    return jax.nn.softmax(x, axis=axis)

def _gelu(x):
    return jax.nn.gelu(x, approximate=True)

def _silu(x):
    return jax.nn.silu(x)

def _sigmoid(x):
    return jax.nn.sigmoid(x)

def _layernorm(x, axis=-1, eps=1e-05):
    m = jnp.mean(x, axis=axis, keepdims=True)
    v = jnp.var(x, axis=axis, keepdims=True)
    return (x - m) / jnp.sqrt(v + eps)

def _scatter_add(tgt, idx, src, axis=0):
    return tgt.at[idx].add(src)

def _segment_sum(src, seg, n):
    return jax.ops.segment_sum(src, seg, n)
kernel_name = 'mk_xattn_seq_d2_seqx_r8_7dde93'

def setup_inputs(seed: int=0):
    np.random.seed(seed)
    _w = jnp.asarray

    def _rec_inputs():
        import jax
        import jax.numpy as jnp
        _rk = jax.random.key(seed)
        x = -0.0002928 + 1 * jax.random.normal(jax.random.fold_in(_rk, 1), (32, 64, 256), jnp.float32)
        _lenS = 64 - jax.random.randint(jax.random.fold_in(_rk, 7), (32,), 0, max(1, 64 // 4) + 1, jnp.int32)
        _lenS2 = 64 - jax.random.randint(jax.random.fold_in(_rk, 8), (32,), 0, max(1, 64 // 4) + 1, jnp.int32)
        _ctx_2048P = jax.random.normal(jax.random.fold_in(_rk, 11), (32, 16, 256), jnp.float32)
        _ctx_2048c = jax.random.dirichlet(jax.random.fold_in(_rk, 511), 0.3 * jnp.ones((16,), jnp.float32), (32, 64))
        _ctx_2048t = jnp.einsum('bsk,bkd->bsd', _ctx_2048c, _ctx_2048P)
        _ctx_2048t = _ctx_2048t * jax.lax.rsqrt(jnp.mean(jnp.square(_ctx_2048t)) + 1e-12) * 0.953939
        ctx_2048 = -1.39393e-06 + 0.999914 * (_ctx_2048t + 0.3 * jax.random.normal(jax.random.fold_in(_rk, 611), (32, 64, 256), jnp.float32))
        _validS = jnp.arange(64)[None, :] < _lenS[:, None]
        _validS2 = jnp.arange(64)[None, :] < _lenS2[:, None]
        _causal = jnp.tril(jnp.ones((64, 64), dtype=bool))
        mask_1x1xSxS2_fc1 = jnp.where(jnp.broadcast_to(_validS2[0:1, None, None, :], (1, 1, 64, 64)), 1.0, 0.0).astype(jnp.float32)
        mask_Bx1xSxS2_ff1 = jnp.where(jnp.ones((32, 1, 64, 64), dtype=bool), 1.0, 0.0).astype(jnp.float32)
        return (x, ctx_2048, mask_1x1xSxS2_fc1, mask_Bx1xSxS2_ff1)
    x, ctx_2048, mask_1x1xSxS2_fc1, mask_Bx1xSxS2_ff1 = _rec_inputs()

    def _L0_xattn_setup():
        import jax, jax.numpy as jnp
        import numpy as np
        N, C, S, S2, H, CTX = (4, 64, 256, 256, 8, 64)
        EPS = 1e-05
        key = jax.random.key(seed)
        ks = jax.random.split(key, 6)
        sd = lambda fan: 1.0 / np.sqrt(fan)
        return {'input': jax.random.normal(ks[0], (N, C, S), jnp.float32), 'context': jax.random.normal(ks[1], (N, CTX, S2), jnp.float32), 'gamma': jnp.ones((C,), jnp.float32), 'beta': jnp.zeros((C,), jnp.float32), 'Wq': jax.random.normal(ks[2], (C * H, C), jnp.float32) * sd(C), 'bq': jnp.zeros((C * H,), jnp.float32), 'Wkv': jax.random.normal(ks[3], (C * H * 2, CTX), jnp.float32) * sd(CTX), 'bkv': jnp.zeros((C * H * 2,), jnp.float32), 'Wo': jax.random.normal(ks[4], (C, C * H), jnp.float32) * sd(C * H), 'bo': jnp.zeros((C,), jnp.float32)}
    _L0_xattn_all = _L0_xattn_setup()
    _L0_xattn_in = {k: v for k, v in _L0_xattn_all.items() if k in ('gamma', 'beta', 'Wq', 'bq', 'Wkv', 'bkv', 'Wo', 'bo')}
    del _L0_xattn_all

    def _L1_xattn_setup():
        import jax, jax.numpy as jnp
        import numpy as np
        H = 256
        NH = 16
        HD = H // NH
        EPS = 1e-05

        def gelu(x):
            return 0.5 * x * (1.0 + jnp.tanh(0.7978845608028654 * x * (1.0 + 0.044715 * x * x)))

        def layernorm(x, scale, bias):
            m = jnp.mean(x, axis=-1, keepdims=True)
            v = jnp.mean(jnp.square(x - m), axis=-1, keepdims=True)
            return (x - m) * jax.lax.rsqrt(v + EPS) * scale + bias

        def split_heads(x):
            b, s, _ = x.shape
            return x.reshape(b, s, NH, HD).transpose(0, 2, 1, 3)

        def merge_heads(x):
            b, nh, s, hd = x.shape
            return x.transpose(0, 2, 1, 3).reshape(b, s, nh * hd)

        def attention(q, k, v, mask):
            scores = jnp.einsum('bhqd,bhkd->bhqk', q, k) / jnp.sqrt(jnp.float32(HD))
            scores = scores * mask - 10000.0 * (1.0 - mask)
            probs = jax.nn.softmax(scores, axis=-1)
            return jnp.einsum('bhqk,bhkd->bhqd', probs, v)
        key = jax.random.key(seed)
        ks = jax.random.split(key, 16)
        b, s, t = (2, 128, 128)
        w = lambda k, i, o: jax.random.normal(k, (i, o), jnp.float32) * 0.02
        inp = {'hidden_states': jax.random.normal(ks[0], (b, s, H), jnp.float32), 'encoder_states': jax.random.normal(ks[1], (b, t, H), jnp.float32), 'ltor_mask': jnp.tril(jnp.ones((1, 1, s, s), jnp.float32)), 'cross_mask': jnp.ones((b, 1, s, t), jnp.float32), 'ln1_s': jnp.ones((H,), jnp.float32), 'ln1_b': jnp.zeros((H,), jnp.float32), 'w_qkv': w(ks[2], H, 3 * H), 'b_qkv': jnp.zeros((3 * H,), jnp.float32), 'w_ao': w(ks[3], H, H), 'b_ao': jnp.zeros((H,), jnp.float32), 'ln2_s': jnp.ones((H,), jnp.float32), 'ln2_b': jnp.zeros((H,), jnp.float32), 'w_q': w(ks[4], H, H), 'b_q': jnp.zeros((H,), jnp.float32), 'w_kv': w(ks[5], H, 2 * H), 'b_kv': jnp.zeros((2 * H,), jnp.float32), 'w_co': w(ks[6], H, H), 'b_co': jnp.zeros((H,), jnp.float32), 'ln3_s': jnp.ones((H,), jnp.float32), 'ln3_b': jnp.zeros((H,), jnp.float32), 'w1': w(ks[7], H, 4 * H), 'b1': jnp.zeros((4 * H,), jnp.float32), 'w2': w(ks[8], 4 * H, H), 'b2': jnp.zeros((H,), jnp.float32)}
        return inp
    _L1_xattn_all = _L1_xattn_setup()
    _L1_xattn_in = {k: v for k, v in _L1_xattn_all.items() if k in ('ln1_s', 'ln1_b', 'w_qkv', 'b_qkv', 'w_ao', 'b_ao', 'ln2_s', 'ln2_b', 'w_q', 'b_q', 'w_kv', 'b_kv', 'w_co', 'b_co', 'ln3_s', 'ln3_b', 'w1', 'b1', 'w2', 'b2')}
    del _L1_xattn_all
    return {'x': x, 'ctx_2048': ctx_2048, 'mask_1x1xSxS2_fc1': mask_1x1xSxS2_fc1, 'mask_Bx1xSxS2_ff1': mask_Bx1xSxS2_ff1, 'L0_xattn_gamma': _L0_xattn_in['gamma'], 'L0_xattn_beta': _L0_xattn_in['beta'], 'L0_xattn_Wq': _L0_xattn_in['Wq'], 'L0_xattn_bq': _L0_xattn_in['bq'], 'L0_xattn_Wkv': _L0_xattn_in['Wkv'], 'L0_xattn_bkv': _L0_xattn_in['bkv'], 'L0_xattn_Wo': _L0_xattn_in['Wo'], 'L0_xattn_bo': _L0_xattn_in['bo'], 'L1_xattn_ln1_s': _L1_xattn_in['ln1_s'], 'L1_xattn_ln1_b': _L1_xattn_in['ln1_b'], 'L1_xattn_w_qkv': _L1_xattn_in['w_qkv'], 'L1_xattn_b_qkv': _L1_xattn_in['b_qkv'], 'L1_xattn_w_ao': _L1_xattn_in['w_ao'], 'L1_xattn_b_ao': _L1_xattn_in['b_ao'], 'L1_xattn_ln2_s': _L1_xattn_in['ln2_s'], 'L1_xattn_ln2_b': _L1_xattn_in['ln2_b'], 'L1_xattn_w_q': _L1_xattn_in['w_q'], 'L1_xattn_b_q': _L1_xattn_in['b_q'], 'L1_xattn_w_kv': _L1_xattn_in['w_kv'], 'L1_xattn_b_kv': _L1_xattn_in['b_kv'], 'L1_xattn_w_co': _L1_xattn_in['w_co'], 'L1_xattn_b_co': _L1_xattn_in['b_co'], 'L1_xattn_ln3_s': _L1_xattn_in['ln3_s'], 'L1_xattn_ln3_b': _L1_xattn_in['ln3_b'], 'L1_xattn_w1': _L1_xattn_in['w1'], 'L1_xattn_b1': _L1_xattn_in['b1'], 'L1_xattn_w2': _L1_xattn_in['w2'], 'L1_xattn_b2': _L1_xattn_in['b2']}

def reference(x, ctx_2048, mask_1x1xSxS2_fc1, mask_Bx1xSxS2_ff1, L0_xattn_gamma, L0_xattn_beta, L0_xattn_Wq, L0_xattn_bq, L0_xattn_Wkv, L0_xattn_bkv, L0_xattn_Wo, L0_xattn_bo, L1_xattn_ln1_s, L1_xattn_ln1_b, L1_xattn_w_qkv, L1_xattn_b_qkv, L1_xattn_w_ao, L1_xattn_b_ao, L1_xattn_ln2_s, L1_xattn_ln2_b, L1_xattn_w_q, L1_xattn_b_q, L1_xattn_w_kv, L1_xattn_b_kv, L1_xattn_w_co, L1_xattn_b_co, L1_xattn_ln3_s, L1_xattn_ln3_b, L1_xattn_w1, L1_xattn_b1, L1_xattn_w2, L1_xattn_b2):
    import jax
    import jax.numpy as jnp

    def _L0_xattn_ref(input, context, gamma, beta, Wq, bq, Wkv, bkv, Wo, bo):
        import jax, jax.numpy as jnp
        import numpy as np
        N, C, S, S2, H, CTX = (4, 64, 256, 256, 8, 64)
        EPS = 1e-05
        n, c, s = input.shape
        h = H
        mu = jnp.mean(input, axis=(1, 2), keepdims=True)
        var = jnp.var(input, axis=(1, 2), keepdims=True)
        xn = (input - mu) * jax.lax.rsqrt(var + EPS)
        xn = xn * gamma[None, :, None] + beta[None, :, None]
        q = jnp.einsum('oc,ncs->nos', Wq, xn) + bq[None, :, None]
        kv = jnp.einsum('od,nds->nos', Wkv, context) + bkv[None, :, None]
        q = q.reshape(n, h, c, s).transpose(0, 1, 3, 2)
        kv = kv.reshape(n, 2 * h, c, -1).transpose(0, 1, 3, 2)
        k, v = (kv[:, :h], kv[:, h:])
        scale = c ** (-0.25)
        att = jax.nn.softmax(jnp.einsum('nhqc,nhkc->nhqk', q * scale, k * scale), axis=-1)
        y = jnp.einsum('nhqk,nhkc->nhqc', att, v)
        y = y.transpose(0, 1, 3, 2).reshape(n, h * c, s)
        out = jnp.einsum('co,nos->ncs', Wo, y) + bo[None, :, None]
        return input + out

    def _L1_xattn_ref(hidden_states, encoder_states, ltor_mask, cross_mask, ln1_s, ln1_b, w_qkv, b_qkv, w_ao, b_ao, ln2_s, ln2_b, w_q, b_q, w_kv, b_kv, w_co, b_co, ln3_s, ln3_b, w1, b1, w2, b2):
        import jax, jax.numpy as jnp
        import numpy as np
        H = 256
        NH = 16
        HD = H // NH
        EPS = 1e-05

        def gelu(x):
            return 0.5 * x * (1.0 + jnp.tanh(0.7978845608028654 * x * (1.0 + 0.044715 * x * x)))

        def layernorm(x, scale, bias):
            m = jnp.mean(x, axis=-1, keepdims=True)
            v = jnp.mean(jnp.square(x - m), axis=-1, keepdims=True)
            return (x - m) * jax.lax.rsqrt(v + EPS) * scale + bias

        def split_heads(x):
            b, s, _ = x.shape
            return x.reshape(b, s, NH, HD).transpose(0, 2, 1, 3)

        def merge_heads(x):
            b, nh, s, hd = x.shape
            return x.transpose(0, 2, 1, 3).reshape(b, s, nh * hd)

        def attention(q, k, v, mask):
            scores = jnp.einsum('bhqd,bhkd->bhqk', q, k) / jnp.sqrt(jnp.float32(HD))
            scores = scores * mask - 10000.0 * (1.0 - mask)
            probs = jax.nn.softmax(scores, axis=-1)
            return jnp.einsum('bhqk,bhkd->bhqd', probs, v)
        ln_out = layernorm(hidden_states, ln1_s, ln1_b)
        qkv = ln_out @ w_qkv + b_qkv
        q, k, v = jnp.split(qkv, 3, axis=-1)
        ctx = merge_heads(attention(split_heads(q), split_heads(k), split_heads(v), ltor_mask))
        attn_out = ctx @ w_ao + b_ao
        x = hidden_states + attn_out
        ln_out = layernorm(x, ln2_s, ln2_b)
        q = ln_out @ w_q + b_q
        kv = encoder_states @ w_kv + b_kv
        k, v = jnp.split(kv, 2, axis=-1)
        ctx = merge_heads(attention(split_heads(q), split_heads(k), split_heads(v), cross_mask))
        cross_out = ctx @ w_co + b_co
        x = x + cross_out
        ln_out = layernorm(x, ln3_s, ln3_b)
        mlp_out = gelu(ln_out @ w1 + b1) @ w2 + b2
        return x + mlp_out
    x = _L0_xattn_ref(x, ctx_2048, L0_xattn_gamma, L0_xattn_beta, L0_xattn_Wq, L0_xattn_bq, L0_xattn_Wkv, L0_xattn_bkv, L0_xattn_Wo, L0_xattn_bo)
    x = _L1_xattn_ref(x, ctx_2048, mask_1x1xSxS2_fc1, mask_Bx1xSxS2_ff1, L1_xattn_ln1_s, L1_xattn_ln1_b, L1_xattn_w_qkv, L1_xattn_b_qkv, L1_xattn_w_ao, L1_xattn_b_ao, L1_xattn_ln2_s, L1_xattn_ln2_b, L1_xattn_w_q, L1_xattn_b_q, L1_xattn_w_kv, L1_xattn_b_kv, L1_xattn_w_co, L1_xattn_b_co, L1_xattn_ln3_s, L1_xattn_ln3_b, L1_xattn_w1, L1_xattn_b1, L1_xattn_w2, L1_xattn_b2)
    return x

_drawn_inputs = setup_inputs


def setup_inputs(seed=0):
    import zlib

    import numpy as np

    out = dict(_drawn_inputs(seed))
    spreads = {'L0_xattn_gamma': (1.0, 0.2),
     'L0_xattn_beta': (0.0, 0.279),
     'L0_xattn_bq': (0.0, 0.272),
     'L0_xattn_bkv': (0.0, 0.1),
     'L0_xattn_bo': (0.0, 0.1),
     'L1_xattn_ln1_s': (1.0, 0.6),
     'L1_xattn_ln1_b': (0.0, 0.8),
     'L1_xattn_b_qkv': (0.0, 0.277),
     'L1_xattn_b_ao': (0.0, 0.1),
     'L1_xattn_ln2_s': (1.0, 0.6),
     'L1_xattn_ln2_b': (0.0, 2.0),
     'L1_xattn_b_q': (0.0, 2.0),
     'L1_xattn_b_kv': (0.0, 0.279),
     'L1_xattn_b_co': (0.0, 0.1),
     'L1_xattn_ln3_s': (1.0, 0.6),
     'L1_xattn_ln3_b': (0.0, 0.78),
     'L1_xattn_b1': (0.0, 0.1),
     'L1_xattn_b2': (0.0, 0.1)}
    factors = {'L1_xattn_w_qkv': 3.291, 'L1_xattn_w_q': 8.0}
    for name, (base, spread) in spreads.items():
        noise = np.random.default_rng([zlib.crc32(name.encode()), seed]).standard_normal(out[name].shape)
        drawn = base * np.exp(spread * noise) if base else spread * noise
        out[name] = jnp.asarray(drawn.astype(out[name].dtype))
    for name, factor in factors.items():
        out[name] = (out[name] * factor).astype(out[name].dtype)
    return out
```

```python
from contextlib import ExitStack

import concourse.bass as bass
from concourse import mybir

F32 = mybir.dt.float32
F32R = mybir.dt.float32r
ALU = mybir.AluOpType
ACT = mybir.ActivationFunctionType
AX = mybir.AxisListType

P = 128
B, S, D = 32, 64, 256
NP = B // 2
H0, C0 = 8, 64
QT, KT = D // P, D // P
SCALE0 = float(C0) ** -0.5
EPS = 1e-5


class Pair:

    def __init__(self, idx, par, before):
        self.idx, self.par, self.before = idx, par, before

    def next(self, n=1):
        off = self.par + n
        return Pair(self.idx + n, off % 2, self.before + off // 2)


def run_steps(eng, step, first, last, loop_first, loop_last):
    idx = first
    while idx <= last:
        if idx == loop_first:
            turns = (loop_last + 1 - loop_first) // 2
            with eng.Fori(0, turns) as t:
                step(Pair(t * 2 + loop_first, 0, t + loop_first // 2))
                step(Pair(t * 2 + loop_first + 1, 1, t + loop_first // 2))
            idx += 2 * turns
        else:
            step(Pair(idx, idx % 2, idx // 2))
            idx += 1


def exists(pair, off, count=NP):
    return not isinstance(pair.idx, int) or 0 <= pair.idx + off < count


def wait(eng, sem, value):
    if not isinstance(value, int) or value > 0:
        eng.wait_ge(sem, value)


def bc(ap, dim, n):
    shape = list(ap.shape)
    return ap.unsqueeze(dim).broadcast_to(shape[:dim] + [n] + shape[dim:])


def layer0(nc, sb, psum, sem, block, x, ctx, gamma, beta, Wq, bq, Wkv, bkv, Wo, bo, x1):
    wq2 = sb("wq2", [C0, H0, 2, C0], F32)
    wk2 = sb("wk2", [C0, H0, 2, C0], F32)
    wv2 = sb("wv2", [C0, H0, 2, C0], F32)
    wo_nat = sb("wo_nat", [C0, H0 * C0], F32)
    wo2 = sb("wo2", [C0, H0, 2, C0], F32)
    bq_sb = sb("bq_sb", [C0, H0], F32)
    bv_sb = sb("bv_sb", [C0, H0], F32)
    gamma2 = sb("gamma2", [P, 1], F32)
    beta2 = sb("beta2", [P, 1], F32)
    bo2 = sb("bo2", [P, 1], F32)
    a_st = sb("a_st", [P, H0, P], F32R)
    qbias = sb("qbias", [P, H0], F32)
    wvo_hi = sb("wvo_hi", [P, H0 * C0], F32R)
    wvo_lo = sb("wvo_lo", [P, H0 * C0], F32R)
    obias = sb("obias", [P, 1], F32)
    ident = sb("ident", [P, P], F32)
    mean64 = sb("mean64", [C0, P], F32)
    neghalf = sb("neghalf", [P, 2], F32)
    xd = sb("xd", [P, 2, 2, D], F32)
    cd = sb("cd", [P, 2, 2, D], F32)
    xp = sb("xp", [P, 2, D], F32)
    bnst = sb("bnst", [P, 2, 6], F32)
    mv = sb("mv", [P, 2, 2], F32)
    mvm = sb("mvm", [P, 2, 2], F32)
    dev = sb("dev", [P, 2], F32)
    dev2 = sb("dev2", [P, 2], F32)
    veps = sb("veps", [P, 2], F32)
    rstd = sb("rstd", [P, 2], F32)
    s1 = sb("s1", [P, 2], F32)
    ms1 = sb("ms1", [P, 2], F32)
    s2 = sb("s2", [P, 2], F32)
    xh = sb("xh", [P, 2, 2, D], F32R)
    xn = sb("xn", [P, 2, D], F32)
    xl = sb("xl", [P, 2, 2, D], F32R)
    cs = sb("cs", [P, 2, 2, D], F32R)
    c1 = sb("c1", [P, 2, 2, D], F32R)
    qh = sb("qh", [P, 2, H0, 2, D], F32R)
    ql = sb("ql", [P, 2, 2, H0, D], F32R)
    vw = sb("vw", [P, 2, 2, KT, H0, C0 + 1], F32)
    pt = sb("pt", [P, 2, KT, D], F32)
    nmax = sb("nmax", [P, 2, H0, QT], F32)
    nmaxt = sb("nmaxt", [H0 * QT, 2, P], F32R)
    rden = sb("rden", [P, 2, 2, QT], F32)
    yn = sb("yn", [P, 2, 4, 2, QT, C0], F32)
    ysum = sb("ysum", [P, 2, 4, QT, C0], F32)
    ot = sb("ot", [P, 2, QT, 2, C0], F32)

    T = [psum[:, 0], psum[:, 1]]
    M = [psum[:, 2], psum[:, 3]]
    J = [psum[:, 4], psum[:, 5]]
    Y = [psum[:, 6], psum[:, 7]]

    s_w, s_const, s_ones = sem("w_loaded"), sem("const_set"), sem("ones_set")
    s_wot, s_wot_ev = sem("wo_transposed"), sem("wo_copied")
    s_fold, s_fold_ev, s_fold_lo = sem("folded"), sem("fold_high"), sem("fold_low")
    s_x = [sem("x_loaded0"), sem("x_loaded1")]
    s_c = [sem("ctx_loaded0"), sem("ctx_loaded1")]
    s_xp = [sem("xres_loaded0"), sem("xres_loaded1")]
    s_bn, s_mv, s_st = sem("bn_done"), sem("row_stats"), sem("sample_stats")
    s_dev, s_dev2, s_veps = sem("dev_done"), sem("dev2_done"), sem("var_eps")
    s_aff, s_xh, s_xn, s_xl = sem("affine"), sem("x_high"), sem("x_norm"), sem("x_low")
    s_cs, s_c1, s_csl = sem("ctx_high"), sem("ctx_high_ones"), sem("ctx_low")
    s_q, s_qh, s_ql = sem("q_projected"), sem("q_high"), sem("q_low")
    s_s, s_max = sem("scores_for_max"), sem("max_taken")
    s_mt, s_mtc, s_row = sem("max_transposed"), sem("max_rounded"), [sem("max_row0"), sem("max_row1")]
    s_v, s_vw = sem("v_projected"), sem("v_copied")
    s_t, s_exp, s_pv = sem("scores"), sem("probs"), sem("weighted")
    s_rden, s_yn, s_ysum = sem("denominators"), sem("normalised"), sem("heads_summed")
    s_tick = sem("wait_carrier")
    s_ot, s_x1 = sem("out_transposed"), sem("x1_ready")

    @block.sync
    def _(sp):
        for copy in range(2):
            sp.dma_start(wq2[:, :, copy], Wq.rearrange("(h o) c -> o h c", o=C0)).then_inc(s_w, 16)
            sp.dma_start(wk2[:, :, copy], Wkv[0:H0 * C0].rearrange("(h o) c -> o h c", o=C0)).then_inc(s_w, 16)
            sp.dma_start(wv2[:, :, copy], Wkv[H0 * C0:].rearrange("(h o) c -> o h c", o=C0)).then_inc(s_w, 16)
            half = slice(64 * copy, 64 * copy + 64)
            sp.dma_start(gamma2[half], gamma.rearrange("(c a) -> c a", a=1)).then_inc(s_w, 16)
            sp.dma_start(beta2[half], beta.rearrange("(c a) -> c a", a=1)).then_inc(s_w, 16)
            sp.dma_start(bo2[half], bo.rearrange("(c a) -> c a", a=1)).then_inc(s_w, 16)
        sp.dma_start(wo_nat[:], Wo).then_inc(s_w, 16)
        sp.dma_start(bq_sb[:], bq.rearrange("(h o) -> o h", o=C0), allow_slow_non_contiguous=True).then_inc(s_w, 16)
        sp.dma_start(bv_sb[:], bkv[H0 * C0:].rearrange("(h o) -> o h", o=C0), allow_slow_non_contiguous=True).then_inc(s_w, 16)

        def load(p):
            for copy in range(2):
                half = slice(64 * copy, 64 * copy + 64)
                sp.dma_start(xd[half, p.par], x[bass.ds(p.idx * 2, 2)].rearrange("n c s -> c n s")
                             ).then_inc(s_x[p.par], 16)
            for copy in range(2):
                half = slice(64 * copy, 64 * copy + 64)
                sp.dma_start(cd[half, p.par], ctx[bass.ds(p.idx * 2, 2)].rearrange("n c s -> c n s")
                             ).then_inc(s_c[p.par], 16)

        def max_row(p, n):
            sp.wait_ge(s_mtc, p.idx * 2 + n + 1)
            sp.dma_start(ql[C0:C0 + 1, p.par, n].rearrange("a h (t q) -> a (h t) q", t=QT).bitcast(F32),
                         nmaxt[:, n].bitcast(F32)).then_inc(s_row[n], 16)

        def step(p):
            if exists(p, 3):
                p3 = p.next(3)
                wait(sp, s_xh, 2 * (p3.idx - 1))
                wait(sp, s_xl, p3.idx - 1)
                wait(sp, s_csl, p3.idx - 1)
                wait(sp, s_c1, p3.idx - 1)
                load(p3)
            if exists(p, 0):
                max_row(p, 1)
                wait(sp, s_x1, p.idx - 1)
                sp.dma_start(xp[:, p.par], x[bass.ds(p.idx * 2, 2)].rearrange("n c s -> (n c) s")
                             ).then_inc(s_xp[p.par], 16)
            if exists(p, 1):
                max_row(p.next(), 0)

        load(Pair(0, 0, 0))
        load(Pair(1, 1, 0))
        step(Pair(-1, 1, -1))
        run_steps(sp, step, 0, NP - 1, 2, NP - 5)

    @block.gpsimd
    def _(pool):
        nc.gpsimd.memset(ident[:], 0.0).then_inc(s_const, 1)
        nc.gpsimd.memset(mean64[:], 1.0 / C0).then_inc(s_const, 1)
        nc.gpsimd.memset(neghalf[:], -0.5).then_inc(s_const, 1)
        nc.gpsimd.memset(vw[:, :, :, :, :, C0:C0 + 1], 1.0).then_inc(s_const, 1)
        pool.wait_ge(s_const, 1)
        nc.gpsimd.affine_select(out=ident[:], in_=ident[:], compare_op=ALU.not_equal, fill=1.0, base=0,
                                pattern=[[-1, P]], channel_multiplier=1).then_inc(s_const, 1)
        pool.wait_ge(s_w, 16 * 15)
        pool.wait_ge(s_const, 5)

        def prepare_x(p):
            pool.wait_ge(s_veps, p.idx + 1)
            wait(pool, s_xh, 2 * p.idx)
            wait(pool, s_xn, 2 * p.idx)
            wait(pool, s_xl, p.idx)
            nc.gpsimd.tensor_tensor(rstd[:], veps[:], neghalf[:], ALU.pow).then_inc(s_aff, 1)
            pool.wait_ge(s_aff, 4 * p.idx + 1)
            nc.gpsimd.tensor_tensor(s1[:], rstd[:], gamma2[:].broadcast_to([P, 2]), ALU.mult).then_inc(s_aff, 1)
            pool.wait_ge(s_aff, 4 * p.idx + 2)
            nc.gpsimd.tensor_tensor(ms1[:], s1[:], mvm[:, :, 0], ALU.mult).then_inc(s_aff, 1)
            pool.wait_ge(s_aff, 4 * p.idx + 3)
            nc.gpsimd.tensor_tensor(s2[:], beta2[:].broadcast_to([P, 2]), ms1[:], ALU.subtract).then_inc(s_aff, 1)
            pool.wait_ge(s_aff, 4 * p.idx + 4)
            pool.sem_inc(s_tick, 1)
            for n in range(2):
                nc.gpsimd.tensor_scalar(xn[:, n], xd[:, p.par, n], s1[:, n:n + 1], s2[:, n:n + 1],
                                        ALU.mult, ALU.add).then_inc(s_xn, 1)
            pool.wait_ge(s_xn, 2 * p.idx + 2)
            pool.wait_ge(s_xh, 2 * p.idx + 2)
            wait(pool, s_q, H0 * (p.idx - 1))
            nc.gpsimd.tensor_tensor(xl[:, p.par], xn[:], xh[:, p.par].bitcast(F32), ALU.subtract).then_inc(s_xl, 1)

        def prepare_context(p):
            pool.wait_ge(s_xl, p.idx + 1)
            pool.wait_ge(s_cs, p.idx + 1)
            nc.gpsimd.tensor_tensor(cs[C0:P, p.par], cd[C0:P, p.par], cs[C0:P, p.par].bitcast(F32),
                                    ALU.subtract).then_inc(s_csl, 1)

        def sum_heads(p, n):
            pool.wait_ge(s_yn, 8 * p.idx + 4 * n + 4)
            c = 6 * p.idx + 3 * n
            yv = yn[:, n].rearrange("p a b t c -> p (a b) t c")
            a = ysum[:, n]
            wait(pool, s_ysum, c)
            nc.gpsimd.tensor_tensor(a, yv[:, 0:4], yv[:, 4:8], ALU.add).then_inc(s_ysum, 1)
            pool.wait_ge(s_ysum, c + 1)
            nc.gpsimd.tensor_tensor(a[:, 0:2], a[:, 0:2], a[:, 2:4], ALU.add).then_inc(s_ysum, 1)
            pool.wait_ge(s_ysum, c + 2)
            wait(pool, s_ot, p.idx - 1)
            nc.gpsimd.tensor_tensor(ot[:, p.par, :, n], a[:, 0], a[:, 1], ALU.add).then_inc(s_ysum, 1)

        def step(p):
            if exists(p, 0):
                sum_heads(p, 0)
            if exists(p, 2):
                prepare_x(p.next(2))
                prepare_context(p.next(2))
                pool.wait_ge(s_csl, p.idx + 3)
            if exists(p, 0):
                sum_heads(p, 1)

        step(Pair(-2, 0, -1))
        step(Pair(-1, 1, -1))
        run_steps(pool, step, 0, NP - 1, 2, NP - 3)

    @block.scalar
    def _(act):
        act.wait_ge(s_fold, 1)
        for b in range(2):
            nc.scalar.activation(a_st[:, 4 * b:4 * b + 4], T[b].rearrange("p (h c) -> p h c", c=P), ACT.Copy,
                                 scale=SCALE0).then_inc(s_fold_ev, 1)
        nc.scalar.copy(wvo_hi[:], M[0]).then_inc(s_fold_ev, 1)
        nc.scalar.activation(qbias[:], M[1][:, 0:H0], ACT.Copy, scale=SCALE0).then_inc(s_fold_ev, 1)

        def prepare_x(p):
            act.wait_ge(s_aff, 4 * p.idx + 4)
            wait(act, s_q, H0 * (p.idx - 1))
            for n in range(2):
                nc.scalar.activation(xh[:, p.par, n], xd[:, p.par, n], ACT.Identity, bias=s2[:, n:n + 1],
                                     scale=s1[:, n:n + 1]).then_inc(s_xh, 1)

        def prepare_context(p):
            act.wait_ge(s_c[p.par], 32 * (p.before + 1))
            wait(act, s_v, 4 * (p.idx - 1))
            wait(act, s_s, 16 * (p.idx - 1))
            wait(act, s_t, 16 * (p.idx - 1))
            nc.scalar.copy(cs[:, p.par], cd[:, p.par]).then_inc(s_cs, 1)
            nc.scalar.copy(c1[0:C0, p.par], cd[0:C0, p.par]).then_inc(s_c1, 1)

        def q_high(p, h):
            act.wait_ge(s_q, H0 * p.idx + h + 1)
            if h == 0:
                wait(act, s_s, 16 * (p.idx - 1))
                wait(act, s_t, 16 * (p.idx - 1))
            nc.scalar.activation(qh[:, p.par, h].rearrange("p n s -> p (n s)"), J[h % 2], ACT.Identity,
                                 bias=qbias[:, h:h + 1]).then_inc(s_qh, 1)

        def v_copy(p, n, kt):
            act.wait_ge(s_v, 4 * p.idx + 2 * n + kt + 1)
            if n == 0 and kt == 0:
                wait(act, s_pv, 16 * (p.idx - 1))
            nc.scalar.copy(vw[:, p.par, n, kt, :, 0:C0], J[kt].rearrange("p (h c) -> p h c", c=C0)
                           ).then_inc(s_vw, 1)

        def exp(p, u):
            act.wait_ge(s_t, 16 * p.idx + u + 1)
            wait(act, s_pv, 16 * p.idx + u - 1)
            nc.scalar.activation(pt[:, u % 2].rearrange("p t q -> p (t q)"), T[u % 2], ACT.Exp
                                 ).then_inc(s_exp, 1)

        def step(p):
            for u in range(16):
                if u < H0 and exists(p, 1):
                    q_high(p.next(), u)
                if exists(p, 0):
                    exp(p, u)
                if u in (11, 12, 13, 14) and exists(p, 1):
                    v_copy(p.next(), (u - 11) // 2, (u - 11) % 2)
                if u == 11 and exists(p, 2):
                    prepare_x(p.next(2))
            if exists(p, 2):
                prepare_context(p.next(2))

        step(Pair(-2, 0, -1))
        step(Pair(-1, 1, -1))
        run_steps(act, step, 0, NP - 1, 2, NP - 3)

    @block.vector
    def _(dve):
        nc.vector.memset(c1[C0:P].bitcast(F32), 0.0).then_inc(s_ones, 1)
        dve.wait_ge(s_ones, 1)
        nc.vector.memset(c1[C0:C0 + 1].bitcast(F32), 1.0).then_inc(s_ones, 1)
        nc.vector.memset(ql[C0:P].bitcast(F32), 0.0).then_inc(s_ones, 1)
        dve.wait_ge(s_wot, 1)
        for copy in range(2):
            nc.vector.tensor_copy(wo2[:, :, copy], J[0][0:C0].rearrange("o (h c) -> o h c", c=C0)).then_inc(s_wot_ev, 1)
        dve.wait_ge(s_fold_ev, 4)
        for b in range(2):
            hi = a_st[C0:P, 4 * b:4 * b + 4]
            nc.vector.scalar_tensor_tensor(hi, T[b][C0:P].rearrange("p (h c) -> p h c", c=P), SCALE0,
                                           hi.bitcast(F32), ALU.mult, ALU.subtract).then_inc(s_fold_lo, 1)
        nc.vector.tensor_tensor(wvo_lo[:], M[0], wvo_hi[:].bitcast(F32), ALU.subtract).then_inc(s_fold_lo, 1)
        nc.vector.tensor_tensor(obias[:], M[1][:, 32:33], bo2[:], ALU.add).then_inc(s_fold_lo, 1)

        def row_stats(p):
            dve.wait_ge(s_x[p.par], 32 * (p.before + 1))
            wait(dve, s_mv, 2 * p.idx)
            for n in range(2):
                nc.vector.bn_stats(bnst[:, n], xd[:, p.par, n]).then_inc(s_bn, 1)
            dve.wait_ge(s_bn, 2 * p.idx + 2)
            wait(dve, s_st, 2 * p.idx)
            wait(dve, s_dev, 2 * p.idx)
            dve.sem_inc(s_tick, 1)
            for n in range(2):
                nc.vector.bn_aggr(mv[:, n], bnst[:, n]).then_inc(s_mv, 1)

        def deviation(p):
            dve.wait_ge(s_st, 2 * p.idx + 1)
            wait(dve, s_aff, 4 * p.idx)
            wait(dve, s_veps, p.idx)
            wait(dve, s_dev2, p.idx)
            nc.vector.tensor_copy(mvm[:], J[0][:, 0:4].rearrange("p (n k) -> p n k", k=2)).then_inc(s_dev, 1)
            dve.wait_ge(s_dev, 2 * p.idx + 1)
            dve.wait_ge(s_mv, 2 * p.idx + 2)
            nc.vector.tensor_tensor(dev[:], mv[:, :, 0], mvm[:, :, 0], ALU.subtract).then_inc(s_dev, 1)
            dve.wait_ge(s_dev, 2 * p.idx + 2)
            nc.vector.tensor_tensor(dev2[:], dev[:], dev[:], ALU.mult).then_inc(s_dev2, 1)

        def variance(p):
            dve.wait_ge(s_st, 2 * p.idx + 2)
            nc.vector.scalar_tensor_tensor(veps[:], J[1][:, 0:2], EPS, mvm[:, :, 1], ALU.add, ALU.add
                                           ).then_inc(s_veps, 1)

        def q_low(p, h):
            dve.wait_ge(s_qh, H0 * p.idx + h + 1)
            if h == 0:
                wait(dve, s_t, 16 * (p.idx - 1))
            nc.vector.scalar_tensor_tensor(ql[0:C0, p.par, :, h], J[h % 2][0:C0].rearrange("p (n s) -> p n s", n=2),
                                           qbias[0:C0, h:h + 1], qh[0:C0, p.par, h].bitcast(F32),
                                           ALU.add, ALU.subtract).then_inc(s_ql, 1)

        def maximum(p, k):
            n, h = k // H0, k % H0
            dve.wait_ge(s_s, 16 * p.idx + k + 1)
            if k % H0 == 0:
                wait(dve, s_mt, 2 * (p.idx - 1) + n + 1)
            nc.vector.tensor_reduce(out=nmax[:, n, h], in_=M[k % 2].rearrange("p (t k) -> p t k", t=QT),
                                    op=ALU.max, axis=AX.X, negate=True).then_inc(s_max, 1)

        def round_max(p, n):
            dve.wait_ge(s_mt, 2 * p.idx + n + 1)
            wait(dve, s_row[n], 16 * p.idx)
            nc.vector.tensor_copy(nmaxt[:, n], J[0][0:H0 * QT, 0:P]).then_inc(s_mtc, 1)

        def normalise(p, g):
            n, a = g // 4, g % 4
            dve.wait_ge(s_pv, 16 * p.idx + 2 * g + 2)
            wait(dve, s_yn, 8 * p.idx + g - 1)
            yb = Y[g % 2][:, 0:2 * QT * (C0 + 1)].rearrange("p (b t c) -> p b t c", t=QT, c=C0 + 1)
            nc.vector.reciprocal(rden[:, g % 2], yb[:, :, :, C0]).then_inc(s_rden, 1)
            dve.wait_ge(s_rden, 8 * p.idx + g + 1)
            if a == 0:
                wait(dve, s_ysum, 6 * (p.idx - 1) + 3 * n + 1)
            nc.vector.tensor_tensor(yn[:, n, a], yb[:, :, :, 0:C0], bc(rden[:, g % 2], 3, C0), ALU.mult
                                    ).then_inc(s_yn, 1)

        def residual(p):
            dve.wait_ge(s_ot, p.idx + 1)
            dve.wait_ge(s_xp[p.par], 16 * (p.before + 1))
            nc.vector.scalar_tensor_tensor(x1[:, p.idx], J[1][:, 0:D], obias[:], xp[:, p.par], ALU.add, ALU.add
                                           ).then_inc(s_x1, 1)

        def step(p):
            for u in range(16):
                if u < H0 and exists(p, 1):
                    q_low(p.next(), u)
                if u == 1 and exists(p, 0):
                    round_max(p, 1)
                if u == 4 and exists(p, -1):
                    residual(p.next(-1))
                if u % 2 == 1 and u > 1 and exists(p, 0):
                    normalise(p, u // 2 - 1)
                if u >= 1 and u <= 8 and exists(p, 1):
                    maximum(p.next(), u - 1)
                if u >= 8 and exists(p, 1):
                    maximum(p.next(), u)
                if u == 8 and exists(p, 2):
                    row_stats(p.next(2))
                    deviation(p.next(2))
                if u == 9 and exists(p, 2):
                    variance(p.next(2))
                if u == 10 and exists(p, 1):
                    round_max(p.next(), 0)
            if exists(p, 0):
                normalise(p, 7)

        step(Pair(-2, 0, -1))
        step(Pair(-1, 1, -1))
        run_steps(dve, step, 0, NP - 1, 2, NP - 3)
        residual(Pair(NP - 1, (NP - 1) % 2, (NP - 1) // 2))

    @block.tensor
    def _(pe):
        mm = nc.tensor.matmul
        pe.wait_ge(s_w, 16 * 15)
        pe.wait_ge(s_const, 5)
        for h in range(H0):
            last = nc.tensor.transpose(J[0][0:C0, h * C0:(h + 1) * C0], wo_nat[:, h * C0:(h + 1) * C0], ident[0:C0, 0:C0])
        last.then_inc(s_wot, 1)
        for h in range(H0):
            mm(T[h // 4][:, h % 4 * P:(h % 4 + 1) * P], wq2[:, h].rearrange("o a c -> o (a c)"),
               wk2[:, h].rearrange("o a c -> o (a c)"), start=True, stop=True)
            mm(M[1][:, h:h + 1], wk2[:, h].rearrange("o a c -> o (a c)"), bq_sb[:, h:h + 1], start=True, stop=True)
        pe.wait_ge(s_wot_ev, 2)
        for h in range(H0):
            mm(M[0][:, h * C0:(h + 1) * C0], wv2[:, h].rearrange("o a c -> o (a c)"), wo2[:, h, 0], start=True, stop=True)
        for h in range(H0):
            last = mm(M[1][:, 32:33], wo2[:, h].rearrange("o a c -> o (a c)"), bv_sb[:, h:h + 1],
                      start=(h == 0), stop=(h == H0 - 1))
        last.then_inc(s_fold, 1)
        pe.wait_ge(s_fold_lo, 4)
        pe.wait_ge(s_ones, 3)

        def stats(p, k):
            if k == 0:
                pe.wait_ge(s_mv, 2 * p.idx + 2)
                wait(pe, s_ql, H0 * p.idx)
                mm(J[0][:, 0:4], mean64[:], mv[0:C0].rearrange("p n k -> p (n k)"), start=True, stop=True
                   ).then_inc(s_st, 1)
            else:
                pe.wait_ge(s_dev2, p.idx + 1)
                mm(J[1][:, 0:2], mean64[:], dev2[0:C0], start=True, stop=True).then_inc(s_st, 1)

        def project_q(p, h):
            if h == 0:
                pe.wait_ge(s_xl, p.idx + 1)
                pe.wait_ge(s_xh, 2 * p.idx + 2)
                wait(pe, s_vw, 4 * p.idx)
                wait(pe, s_veps, p.idx + 1)
            else:
                wait(pe, s_ql, H0 * p.idx + h - 1)
            if h == 2:
                wait(pe, s_mtc, 2 * p.idx)
            if h == 5:
                wait(pe, s_x1, p.idx - 1)
            mm(J[h % 2], a_st[:, h], xh[:, p.par].rearrange("p n s -> p (n s)"), start=True, stop=False)
            mm(J[h % 2], a_st[:, h], xl[:, p.par].rearrange("p n s -> p (n s)"), start=False, stop=True
               ).then_inc(s_q, 1)

        def scores_for_max(p, k):
            n, h = k // H0, k % H0
            if k == 0:
                pe.wait_ge(s_csl, p.idx + 1)
            if n == 0:
                pe.wait_ge(s_qh, H0 * p.idx + h + 1)
            wait(pe, s_max, 16 * p.idx + k - 1)
            for qt in range(QT):
                last = mm(M[k % 2][:, qt * D:(qt + 1) * D], qh[:, p.par, h, n, qt * P:(qt + 1) * P], cs[:, p.par, n],
                          start=True, stop=True)
            last.then_inc(s_s, 1)

        def transpose_max(p, n):
            pe.wait_ge(s_max, 16 * p.idx + 8 * n + 8)
            nc.tensor.transpose(J[0][0:H0 * QT, 0:P], nmax[:, n].rearrange("p h t -> p (h t)"), ident[:]
                                ).then_inc(s_mt, 1)

        def project_v(p, n, kt):
            if n == 0 and kt == 0:
                wait(pe, s_mtc, 2 * p.idx + 1)
            if n == 0 and kt == 1:
                wait(pe, s_ql, H0 * p.idx + H0)
            if n == 1:
                pe.wait_ge(s_vw, 4 * p.idx + kt + 1)
            keys = slice(kt * P, (kt + 1) * P)
            mm(J[kt], cs[:, p.par, n, keys], wvo_hi[:], start=True, stop=False)
            mm(J[kt], cs[:, p.par, n, keys], wvo_lo[:], start=False, stop=True).then_inc(s_v, 1)

        def scores(p, u):
            n, h = u // H0, u % H0
            if h == 0:
                pe.wait_ge(s_row[n], 16 * (p.idx + 1))
            if u == 0:
                pe.wait_ge(s_c1, p.idx + 1)
                pe.wait_ge(s_ql, H0 * (p.idx + 1))
            wait(pe, s_exp, 16 * p.idx + u - 1)
            for kt in range(KT):
                keys = slice(kt * P, (kt + 1) * P)
                out = T[u % 2][:, kt * D:(kt + 1) * D]
                mm(out, cs[:, p.par, n, keys], qh[:, p.par, h, n], start=True, stop=False)
                last = mm(out, c1[:, p.par, n, keys], ql[:, p.par, n, h], start=False, stop=True)
            last.then_inc(s_t, 1)

        def weigh(p, u):
            n, h = u // H0, u % H0
            pe.wait_ge(s_exp, 16 * p.idx + u + 1)
            if u == 0:
                pe.wait_ge(s_vw, 4 * p.idx + 4)
            if u % 2 == 0:
                wait(pe, s_yn, 8 * p.idx + u // 2 - 1)
            for qt in range(QT):
                at = (u % 2 * QT + qt) * (C0 + 1)
                out = Y[u // 2 % 2][:, at:at + C0 + 1]
                for kt in range(KT):
                    last = mm(out, pt[:, u % 2, kt, qt * P:(qt + 1) * P], vw[:, p.par, n, kt, h],
                              start=(kt == 0), stop=(kt == KT - 1))
            last.then_inc(s_pv, 1)

        def transpose_out(p):
            pe.wait_ge(s_ysum, 6 * p.idx + 6)
            for qt in range(QT):
                last = nc.tensor.transpose(J[1][:, qt * P:(qt + 1) * P],
                                           ot[:, p.par, qt].rearrange("q n c -> q (n c)"), ident[:])
            last.then_inc(s_ot, 1)

        def step(p):
            for u in range(16):
                if u < H0 and exists(p, 1):
                    project_q(p.next(), u)
                if u == 1 and exists(p, 0):
                    if exists(p, 1):
                        pe.wait_ge(s_ql, H0 * (p.idx + 1) + 1)
                    pe.wait_ge(s_vw, 4 * (p.idx + 1))
                    transpose_max(p, 1)
                if u == 4 and exists(p, -1):
                    if exists(p, 1):
                        pe.wait_ge(s_ql, H0 * (p.idx + 1) + 4)
                    pe.wait_ge(s_vw, 4 * (p.idx + 1))
                    transpose_out(p.next(-1))
                if exists(p, 0):
                    scores(p, u)
                    if u > 0:
                        weigh(p, u - 1)
                if u >= 1 and u <= 8 and exists(p, 1):
                    scores_for_max(p.next(), u - 1)
                if u >= 8 and exists(p, 1):
                    scores_for_max(p.next(), u)
                if u == 8 and exists(p, 2):
                    stats(p.next(2), 0)
                if u == 9 and exists(p, 2):
                    stats(p.next(2), 1)
                if u == 10 and exists(p, 1):
                    if exists(p, 2):
                        pe.wait_ge(s_dev, 2 * (p.idx + 2) + 2)
                    pe.wait_ge(s_ql, H0 * (p.idx + 2))
                    transpose_max(p.next(), 0)
                if u in (11, 12, 13, 14) and exists(p, 1):
                    if u == 12 and exists(p, 2):
                        pe.wait_ge(s_veps, p.idx + 3)
                    project_v(p.next(), (u - 11) // 2, (u - 11) % 2)
            if exists(p, 0):
                weigh(p, 15)

        step(Pair(-2, 0, -1))
        step(Pair(-1, 1, -1))
        run_steps(pe, step, 0, NP - 1, 2, NP - 3)
        pe.wait_ge(s_x1, NP - 1)
        transpose_out(Pair(NP - 1, (NP - 1) % 2, (NP - 1) // 2))
    return s_x1


NH, HD = 16, D // 16
G = D // P
FF = 4 * D
SCALE1 = float(HD) ** -0.5
TOK = 2 * S


class Attention:

    def __init__(self, name, sb, sem, cross):
        cols = 2 * D if cross else D
        self.cross = cross
        self.bnst = sb(name + "_bnst", [P, 6], F32)
        self.mv = sb(name + "_mv", [P, 2], F32)
        self.veps = sb(name + "_veps", [P, 1], F32)
        self.rstd = sb(name + "_rstd", [P, 1], F32)
        self.xc = sb(name + "_xc", [P, D], F32)
        self.hh = sb(name + "_hh", [P, cols], F32R)
        self.hl = sb(name + "_hl", [P, cols], F32R)
        self.qs = sb(name + "_qs", [P, G, TOK], F32)
        self.q8 = sb(name + "_q8", [P, G, 2, 8, S], F32)
        self.kT = sb(name + "_kT", [P, G, TOK], F32)
        self.vz = sb(name + "_vz", [P, 2, 2, D], F32)
        self.t = sb(name + "_t", [P, 2, 8, S], F32)
        self.nmax = sb(name + "_nmax", [P, 16], F32)
        self.den = sb(name + "_den", [P, 16], F32)
        self.rden = sb(name + "_rden", [P, 16], F32)
        self.pT = sb(name + "_pT", [P, 8, P], F32)
        self.yh = sb(name + "_yh", [P, G, TOK], F32R)
        self.yl = sb(name + "_yl", [P, G, TOK], F32R)
        self.xb = sb(name + "_xb", [P, D], F32)
        self.done = {what: sem(name + "_" + what) for what in (
            "bnst", "mv", "veps", "rstd", "xc", "transposed", "hh", "hl", "qk", "qs", "q8_g0", "q8_g1", "kT", "v",
            "vz", "s", "masked", "mask_added", "nmax", "shifted", "exp", "den", "rden", "probs", "p_transposed",
            "pT", "y", "yh", "yl", "o", "xb", "x")}


def split_weight(nc, sb, name, shape):
    return (sb(name + "_raw", shape, F32), sb(name + "_high", shape, F32R), sb(name + "_low", shape, F32R))


def layer1_attentions(nc, sb, psum, sem, block, ctx, self_mask, cross_mask, ln1_s, ln1_b, w_qkv, b_qkv, w_ao, b_ao,
                      ln2_s, ln2_b, w_q, b_q, w_kv, b_kv, w_co, b_co, x1):
    SELF = Attention("self", sb, sem, False)
    CROSS = Attention("cross", sb, sem, True)
    wqkv_raw, wqkv_hi, wqkv_lo = split_weight(nc, sb, "w_qkv", [P, G, 3 * D])
    wao_raw, wao_hi, wao_lo = split_weight(nc, sb, "w_ao", [P, G, D])
    wcq_raw, wcq_hi, wcq_lo = split_weight(nc, sb, "w_q", [P, G, D])
    wkv_raw, wkv_hi, wkv_lo = split_weight(nc, sb, "w_kv", [P, G, 2 * D])
    wco_raw, wco_hi, wco_lo = split_weight(nc, sb, "w_co", [P, G, D])
    lns = sb("ln_scales", [P, 2, G], F32)
    lnb = sb("ln_biases", [P, 2, G], F32)
    b1 = sb("bias_self", [P, 3 * G], F32)
    b2 = sb("bias_cross", [P, 3 * G], F32)
    bias_out = sb("bias_out", [P, 2, D], F32)
    ident = sb("ident1", [P, P], F32)
    mask8 = sb("mask8", [P, 8], F32)
    m_self = sb("m_self", [P, S], F32)
    ma_self = sb("ma_self", [P, S], F32)
    m_cross = sb("m_cross", [P, 2, S], F32)
    ma_cross = sb("ma_cross", [P, 2, S], F32)
    ctok = sb("ctx_tokens", [P, D], F32)
    neghalf = sb("neghalf1", [P, 1], F32)

    SB = psum[:, 0:2]
    PB = psum[:, 2:4]
    QK, V, T = psum[:, 4], psum[:, 5], psum[:, 6]
    YO = psum[:, 7]

    s_w, s_const = sem("w1_loaded"), sem("const1_set")
    s_lnf, s_hi, s_lo = sem("ln_folded"), sem("w1_high"), sem("w1_low")
    s_b, s_bf = sem("bias_product"), sem("bias_folded")
    s_ctx, s_cm, s_ma = sem("ctx_tokens_loaded"), sem("cross_mask_loaded"), sem("cross_mask_term")
    s_tick = sem("wait_carrier1")
    W_LOADS = 5 + 4 + 3 + 2 + 2

    def columns(v):
        return v.rearrange("(m p) -> p m", p=P)

    def in_steps(eng, half):
        def step(i):
            half(SELF, at(i, 1), at(i, 0), at(i, -1))
            half(CROSS, at(i, 0), at(i, -1), at(i, 1))
        for i in range(-1, 2):
            step(i)
        with eng.Fori(2, NP - 1) as i:
            step(i)
        for i in range(NP - 1, NP + 1):
            step(i)

    def at(i, off):
        if isinstance(i, int) and not 0 <= i + off < NP:
            return None
        return i + off

    def before_front(a, p):
        n = p - 1 if not a.cross else p + 2
        return n if not isinstance(n, int) else max(0, min(n, NP))

    before_back = before_front

    def other(a):
        return SELF if a.cross else CROSS

    @block.sync
    def _(sp):
        for dst, src in ((wqkv_raw, w_qkv), (wao_raw, w_ao), (wcq_raw, w_q), (wkv_raw, w_kv), (wco_raw, w_co)):
            sp.dma_start(dst[:], src.rearrange("(k p) n -> p k n", p=P)).then_inc(s_w, 16)
        for n, (s_in, b_in) in enumerate(((ln1_s, ln1_b), (ln2_s, ln2_b))):
            sp.dma_start(lns[:, n], columns(s_in), allow_slow_non_contiguous=True).then_inc(s_w, 16)
            sp.dma_start(lnb[:, n], columns(b_in), allow_slow_non_contiguous=True).then_inc(s_w, 16)
        sp.dma_start(b1[:], columns(b_qkv), allow_slow_non_contiguous=True).then_inc(s_w, 16)
        sp.dma_start(b2[:, 0:G], columns(b_q), allow_slow_non_contiguous=True).then_inc(s_w, 16)
        sp.dma_start(b2[:, G:3 * G], columns(b_kv), allow_slow_non_contiguous=True).then_inc(s_w, 16)
        for n, bias in enumerate((b_ao, b_co)):
            sp.dma_start(bias_out[:, n], bias.partition_broadcast(P)).then_inc(s_w, 16)
        for h2 in range(2):
            sp.dma_start(m_self[S * h2:S * h2 + S], self_mask[0, 0]).then_inc(s_w, 16)

        def load(p):
            wait(sp, CROSS.done["transposed"], p)
            sp.dma_start(ctok[:], ctx[bass.ds(p * 2, 2)].rearrange("n t f -> (n t) f")).then_inc(s_ctx, 16)
            wait(sp, CROSS.done["masked"], p)
            wait(sp, s_ma, p)
            for h2 in range(2):
                sp.dma_start(m_cross[S * h2:S * h2 + S],
                             cross_mask[bass.ds(p * 2, 2), 0].rearrange("n q k -> q n k")).then_inc(s_cm, 16)
        load(0)
        load(1)
        with sp.Fori(2, NP) as p:
            load(p)

    @block.gpsimd
    def _(pool):
        nc.gpsimd.memset(ident[:], 0.0).then_inc(s_const, 1)
        nc.gpsimd.memset(mask8[:], 1.0).then_inc(s_const, 1)
        nc.gpsimd.memset(neghalf[:], -0.5).then_inc(s_const, 1)
        for a in (SELF, CROSS):
            nc.gpsimd.memset(a.vz[:], 0.0).then_inc(s_const, 1)
        pool.wait_ge(s_const, 5)
        nc.gpsimd.affine_select(out=ident[:], in_=ident[:], compare_op=ALU.not_equal, fill=1.0, base=0,
                                pattern=[[-1, P]], channel_multiplier=1).then_inc(s_const, 1)
        nc.gpsimd.affine_select(out=mask8[:], in_=mask8[:], compare_op=ALU.is_ge, fill=0.0, base=0,
                                pattern=[[-HD, 8]], channel_multiplier=1).then_inc(s_const, 1)
        pool.wait_ge(s_const, 7)
        nc.gpsimd.affine_select(out=mask8[:], in_=mask8[:], compare_op=ALU.is_ge, fill=0.0, base=HD - 1,
                                pattern=[[HD, 8]], channel_multiplier=-1).then_inc(s_const, 1)
        pool.wait_ge(s_const, 8)
        pool.wait_ge(s_w, 16 * W_LOADS)
        nc.gpsimd.tensor_scalar(ma_self[:], m_self[:], 1e4, -1e4, ALU.mult, ALU.add).then_inc(s_const, 1)
        pool.wait_ge(s_const, 9)

        def half(a, f, b, prev):
            done = a.done
            if f is not None:
                pool.wait_ge(done["veps"], f + 1)
                wait(pool, done["xc"], f)
                nc.gpsimd.tensor_tensor(a.rstd[:], a.veps[:], neghalf[:], ALU.pow).then_inc(done["rstd"], 1)
            if b is not None:
                wait(pool, done["x"], b)
                if a.cross:
                    pool.wait_ge(SELF.done["x"], b + 1)
                nc.gpsimd.tensor_tensor(a.xb[:], x1[:, b], bias_out[:, 1 if a.cross else 0], ALU.add
                                        ).then_inc(done["xb"], 1)
            if f is not None:
                if a.cross:
                    pool.wait_ge(s_cm, 32 * (f + 1))
                    wait(pool, done["mask_added"], f)
                    pool.sem_inc(s_tick, 1)
                    nc.gpsimd.tensor_scalar(ma_cross[:], m_cross[:], 1e4, -1e4, ALU.mult, ALU.add).then_inc(s_ma, 1)
                pool.wait_ge(done["qs"], 2 * f + 2)
                wait(pool, done["s"], f)
                for n in range(2):
                    q_n = bc(a.qs[:, 1, S * n:S * n + S], 1, 8)
                    nc.gpsimd.tensor_tensor(a.q8[:, 1, n], q_n, bc(mask8[:], 2, S), ALU.mult).then_inc(done["q8_g1"], 1)
                pool.wait_ge(done["masked"], f + 1)
                if a.cross:
                    pool.wait_ge(s_ma, f + 1)
                    madd = bc(ma_cross[:], 2, 8)
                    nc.gpsimd.tensor_tensor(a.t[:], a.t[:], madd, ALU.add).then_inc(done["mask_added"], 1)
                else:
                    tv = a.t[:].rearrange("p n h k -> p (n h) k")
                    nc.gpsimd.tensor_tensor(tv, tv, bc(ma_self[:], 1, 16), ALU.add).then_inc(done["mask_added"], 1)

        in_steps(pool, half)

    @block.scalar
    def _(act):
        act.wait_ge(s_lnf, 4)
        for src, hi in ((wqkv_raw, wqkv_hi), (wao_raw, wao_hi), (wcq_raw, wcq_hi), (wkv_raw, wkv_hi), (wco_raw, wco_hi)):
            nc.scalar.copy(hi[:], src[:]).then_inc(s_hi, 1)
        act.wait_ge(s_bf, 4)
        act.wait_ge(s_const, 9)

        def exponent(a, p):
            act.wait_ge(a.done["shifted"], p + 1)
            nc.scalar.activation(a.t[:], a.t[:], ACT.Exp).then_inc(a.done["exp"], 1)

        def half(a, f, b, prev):
            done, bias = a.done, (b2 if a.cross else b1)
            if b is not None:
                for n in range(2):
                    act.wait_ge(done["p_transposed"], 2 * b + n + 1)
                    if n == 0:
                        wait(act, done["y"], b)
                    nc.scalar.copy(a.pT[:, 4 * n:4 * n + 4].rearrange("p a q -> p (a q)"), PB[:, n]).then_inc(done["pT"], 1)
            if f is not None:
                act.wait_ge(done["transposed"], f + 1)
                wait(act, done["v"], f)
                nc.scalar.copy(a.hh[:], T[:, 0:a.hh.shape[1]]).then_inc(done["hh"], 1)
                act.wait_ge(done["qk"], f + 1)
                wait(act, done["q8_g0"], 2 * f)
                wait(act, done["q8_g1"], 2 * f)
                for g in range(G):
                    nc.scalar.activation(a.qs[:, g], QK[:, g * TOK:(g + 1) * TOK], ACT.Identity, bias=bias[:, g:g + 1],
                                         scale=SCALE1).then_inc(done["qs"], 1)
                wait(act, done["s"], f)
                for g in range(G):
                    nc.scalar.activation(a.kT[:, g], QK[:, (G + g) * TOK:(G + g + 1) * TOK], ACT.Identity,
                                         bias=bias[:, G + g:G + g + 1]).then_inc(done["kT"], 1)
            if prev is not None:
                exponent(other(a), prev)
            if b is not None:
                act.wait_ge(done["y"], b + 1)
                wait(act, done["o"], b)
                wait(act, done["yl"], 2 * b)
                for g in range(G):
                    nc.scalar.activation(a.yh[:, g], YO[:, g * TOK:(g + 1) * TOK], ACT.Identity,
                                         bias=bias[:, 2 * G + g:2 * G + g + 1]).then_inc(done["yh"], 1)
            if f is not None:
                act.wait_ge(done["v"], f + 1)
                wait(act, done["y"], f)
                for n in range(2):
                    for hp2 in range(2):
                        src = V[S * n:S * n + S, 0:D].rearrange("k (gj a h d) -> k gj a h d", a=2, h=2, d=HD)[:, :, hp2]
                        dst = a.vz[S * hp2:S * hp2 + S, n].rearrange("k h (gj a c d) -> k gj a c h d", a=2, c=2, d=HD)
                        for h2 in range(2):
                            nc.scalar.copy(dst[:, :, hp2, h2, h2], src[:, :, h2]).then_inc(done["vz"], 1)

        in_steps(act, half)

    @block.vector
    def _(dve):
        dve.wait_ge(s_w, 16 * W_LOADS)
        dve.wait_ge(s_b, 1)
        nc.vector.tensor_tensor(b1[:], T[:, 0:3 * G], b1[:], ALU.add).then_inc(s_bf, 1)
        nc.vector.tensor_tensor(b2[:, 0:G], T[:, 16:16 + G], b2[:, 0:G], ALU.add).then_inc(s_bf, 1)
        dve.wait_ge(s_bf, 2)
        nc.vector.tensor_scalar(b1[:, 0:G], b1[:, 0:G], SCALE1, None, ALU.mult).then_inc(s_bf, 1)
        nc.vector.tensor_scalar(b2[:, 0:G], b2[:, 0:G], SCALE1, None, ALU.mult).then_inc(s_bf, 1)
        for n, w in enumerate((wqkv_raw, wcq_raw)):
            for kt in range(G):
                nc.vector.tensor_scalar(w[:, kt], w[:, kt], lns[:, n, kt:kt + 1], None, ALU.mult).then_inc(s_lnf, 1)
        for n, (src, hi, lo) in enumerate(((wqkv_raw, wqkv_hi, wqkv_lo), (wao_raw, wao_hi, wao_lo),
                                           (wcq_raw, wcq_hi, wcq_lo), (wkv_raw, wkv_hi, wkv_lo),
                                           (wco_raw, wco_hi, wco_lo))):
            dve.wait_ge(s_hi, n + 1)
            nc.vector.tensor_tensor(lo[:], src[:], hi[:].bitcast(F32), ALU.subtract).then_inc(s_lo, 1)
        dve.wait_ge(s_const, 9)

        def softmax_shift(a, p):
            t = a.t[:].rearrange("p n h k -> p (n h) k")
            dve.wait_ge(a.done["nmax"], p + 1)
            nc.vector.tensor_tensor(t, t, bc(a.nmax[:], 2, S), ALU.add).then_inc(a.done["shifted"], 1)

        def softmax_max(a, p):
            dve.wait_ge(a.done["mask_added"], p + 1)
            wait(dve, a.done["shifted"], p)
            nc.vector.tensor_reduce(out=a.nmax[:], in_=a.t[:].rearrange("p n h k -> p (n h) k"), op=ALU.max, axis=AX.X,
                                    negate=True).then_inc(a.done["nmax"], 1)

        def softmax_sum(a, p):
            t = a.t[:].rearrange("p n h k -> p (n h) k")
            dve.wait_ge(a.done["exp"], p + 1)
            wait(dve, a.done["rden"], p)
            nc.vector.tensor_reduce(out=a.den[:], in_=t, op=ALU.add, axis=AX.X).then_inc(a.done["den"], 1)
            dve.wait_ge(a.done["den"], p + 1)
            wait(dve, a.done["probs"], p)
            nc.vector.reciprocal(a.rden[:], a.den[:]).then_inc(a.done["rden"], 1)
            dve.wait_ge(a.done["rden"], p + 1)
            nc.vector.tensor_tensor(t, t, bc(a.rden[:], 2, S), ALU.mult).then_inc(a.done["probs"], 1)

        def half(a, f, b, prev):
            done, bias = a.done, (b2 if a.cross else b1)
            if f is not None:
                if a.cross:
                    dve.wait_ge(SELF.done["x"], f + 1)
                wait(dve, done["mv"], f)
                dve.sem_inc(s_tick, 1)
                nc.vector.bn_stats(a.bnst[:], x1[:, f]).then_inc(done["bnst"], 1)
                dve.wait_ge(done["bnst"], f + 1)
                wait(dve, done["xc"], f)
                dve.sem_inc(s_tick, 1)
                nc.vector.bn_aggr(a.mv[:], a.bnst[:]).then_inc(done["mv"], 1)
                dve.wait_ge(done["mv"], f + 1)
                wait(dve, done["rstd"], f)
                nc.vector.tensor_scalar(a.veps[:], a.mv[:, 1:2], EPS, None, ALU.add).then_inc(done["veps"], 1)
            if prev is not None:
                softmax_max(other(a), prev)
            if f is not None:
                dve.wait_ge(done["rstd"], f + 1)
                wait(dve, done["transposed"], f)
                nc.vector.tensor_scalar(a.xc[:], x1[:, f], a.mv[:, 0:1], a.rstd[:], ALU.subtract, ALU.mult
                                        ).then_inc(done["xc"], 1)
            if prev is not None:
                softmax_shift(other(a), prev)
            if f is not None:
                dve.wait_ge(done["hh"], f + 1)
                wait(dve, done["v"], f)
                nc.vector.tensor_tensor(a.hl[:], T[:, 0:a.hl.shape[1]], a.hh[:].bitcast(F32), ALU.subtract
                                        ).then_inc(done["hl"], 1)
                dve.wait_ge(done["qs"], 2 * f + 1)
                wait(dve, done["s"], f)
                for n in range(2):
                    q_n = bc(a.qs[:, 0, S * n:S * n + S], 1, 8)
                    nc.vector.tensor_tensor(a.q8[:, 0, n], q_n, bc(mask8[:], 2, S), ALU.mult).then_inc(done["q8_g0"], 1)
            if b is not None:
                for g in range(G):
                    dve.wait_ge(done["yh"], 2 * b + 2)
                    wait(dve, done["o"], b)
                    nc.vector.scalar_tensor_tensor(a.yl[:, g], YO[:, g * TOK:(g + 1) * TOK],
                                                   bias[:, 2 * G + g:2 * G + g + 1], a.yh[:, g].bitcast(F32),
                                                   ALU.add, ALU.subtract).then_inc(done["yl"], 1)
            if prev is not None:
                softmax_sum(other(a), prev)
            if f is not None:
                dve.wait_ge(done["s"], f + 1)
                wait(dve, done["p_transposed"], 2 * f)
                if a.cross:
                    dve.wait_ge(s_cm, 32 * (f + 1))
                    for n in range(2):
                        last = nc.vector.tensor_tensor(a.t[:, n], SB[:, n].rearrange("p (h k) -> p h k", k=S),
                                                       bc(m_cross[:, n], 1, 8), ALU.mult)
                    last.then_inc(done["masked"], 1)
                else:
                    for n in range(2):
                        last = nc.vector.tensor_tensor(a.t[:, n], SB[:, n].rearrange("p (h k) -> p h k", k=S),
                                                       bc(m_self[:], 1, 8), ALU.mult)
                    last.then_inc(done["masked"], 1)
            if b is not None:
                dve.wait_ge(done["o"], b + 1)
                dve.wait_ge(done["xb"], b + 1)
                nc.vector.tensor_tensor(x1[:, b], YO[:, D:2 * D], a.xb[:], ALU.add).then_inc(done["x"], 1)

        in_steps(dve, half)

    @block.tensor
    def _(pe):
        mm = nc.tensor.matmul
        pe.wait_ge(s_w, 16 * W_LOADS)
        pe.wait_ge(s_const, 9)
        for m in range(3 * G):
            for kt in range(G):
                mm(T[:, m:m + 1], wqkv_raw[:, kt, m * P:(m + 1) * P], lnb[:, 0, kt:kt + 1], start=(kt == 0), stop=(kt == G - 1))
        for m in range(G):
            for kt in range(G):
                last = mm(T[:, 16 + m:17 + m], wcq_raw[:, kt, m * P:(m + 1) * P], lnb[:, 1, kt:kt + 1],
                          start=(kt == 0), stop=(kt == G - 1))
        last.then_inc(s_b, 1)
        pe.wait_ge(s_lo, 5)
        pe.wait_ge(s_bf, 4)

        def three(out, pairs):
            n = len(pairs)
            for k, ((lh, ll), (rh, rl)) in enumerate(pairs):
                mm(out, lh, rh, start=(k == 0), stop=False)
                mm(out, ll, rh, start=False, stop=False)
                last = mm(out, lh, rl, start=False, stop=(k == n - 1))
            return last

        def half(a, f, b, prev):
            done, o = a.done, other(a)
            if b is not None:
                pe.wait_ge(done["probs"], b + 1)
                wait(pe, o.done["pT"], 2 * before_back(a, b))
                wait(pe, done["pT"], 2 * b)
                for n in range(2):
                    for k in range(4):
                        last = nc.tensor.transpose(PB[:, n, k * P:(k + 1) * P],
                                                   a.t[:, n, 2 * k:2 * k + 2].rearrange("p h k -> p (h k)"), ident[:])
                    last.then_inc(done["p_transposed"], 1)
            if f is not None:
                pe.wait_ge(done["xc"], f + 1)
                wait(pe, o.done["hl"], before_front(a, f))
                wait(pe, done["hl"], f)
                if a.cross:
                    pe.wait_ge(s_ctx, 16 * (f + 1))
                    for kt in range(G):
                        nc.tensor.transpose(T[:, D + kt * TOK:D + (kt + 1) * TOK], ctok[:, kt * P:(kt + 1) * P], ident[:])
                for kt in range(G):
                    last = nc.tensor.transpose(T[:, kt * TOK:(kt + 1) * TOK], a.xc[:, kt * P:(kt + 1) * P], ident[:])
                last.then_inc(done["transposed"], 1)
            if b is not None:
                pe.wait_ge(done["pT"], 2 * b + 2)
                pe.wait_ge(done["vz"], 8 * b + 8)
                wait(pe, o.done["x"], before_back(a, b))
                wait(pe, done["x"], b)
                for n in range(2):
                    for g in range(G):
                        for jj in range(2):
                            for h2 in range(2):
                                at_f = g * P + jj * S
                                last = mm(YO[S * jj:S * jj + S, g * TOK + n * S:g * TOK + (n + 1) * S],
                                          a.vz[:, n, h2, at_f:at_f + S], a.pT[:, 4 * n + 2 * g + jj, h2 * S:(h2 + 1) * S],
                                          start=(h2 == 0), stop=(h2 == 1))
                last.then_inc(done["y"], 1)
            if f is not None:
                pe.wait_ge(done["hl"], f + 1)
                wait(pe, o.done["kT"], 2 * before_front(a, f))
                wait(pe, done["kT"], 2 * f)
                for m in range(2 * G):
                    pairs = []
                    for kt in range(G):
                        src = D if a.cross and m >= G else 0
                        cols = slice(src + kt * TOK, src + (kt + 1) * TOK)
                        if not a.cross:
                            w = (wqkv_hi[:, kt, m * P:(m + 1) * P], wqkv_lo[:, kt, m * P:(m + 1) * P])
                        elif m < G:
                            w = (wcq_hi[:, kt, m * P:(m + 1) * P], wcq_lo[:, kt, m * P:(m + 1) * P])
                        else:
                            w = (wkv_hi[:, kt, (m - G) * P:(m - G + 1) * P], wkv_lo[:, kt, (m - G) * P:(m - G + 1) * P])
                        pairs.append((w, (a.hh[:, cols], a.hl[:, cols])))
                    last = three(QK[:, m * TOK:(m + 1) * TOK], pairs)
                last.then_inc(done["qk"], 1)
                wait(pe, o.done["vz"], 8 * before_front(a, f))
                wait(pe, done["vz"], 8 * f)
                pairs = []
                for kt in range(G):
                    src = D if a.cross else 0
                    cols = slice(src + kt * TOK, src + (kt + 1) * TOK)
                    w = (wkv_hi[:, kt, D:2 * D], wkv_lo[:, kt, D:2 * D]) if a.cross else \
                        (wqkv_hi[:, kt, 2 * D:3 * D], wqkv_lo[:, kt, 2 * D:3 * D])
                    pairs.append(((a.hh[:, cols], a.hl[:, cols]), w))
                three(V[:, 0:D], pairs).then_inc(done["v"], 1)
            if b is not None:
                pe.wait_ge(done["yl"], 2 * b + 2)
                hi, lo = (wco_hi, wco_lo) if a.cross else (wao_hi, wao_lo)
                pairs = [((a.yh[:, g], a.yl[:, g]), (hi[:, g], lo[:, g])) for g in range(G)]
                three(YO[:, D:2 * D], pairs).then_inc(done["o"], 1)
            if f is not None:
                pe.wait_ge(done["kT"], 2 * f + 2)
                pe.wait_ge(done["q8_g0"], 2 * f + 2)
                pe.wait_ge(done["q8_g1"], 2 * f + 2)
                wait(pe, o.done["masked"], before_front(a, f))
                wait(pe, done["masked"], f)
                for n in range(2):
                    for g in range(G):
                        for r in range(4):
                            hp = 4 * g + r
                            last = mm(SB[:, n, hp * S:(hp + 1) * S],
                                      a.q8[:, g, n, 2 * r:2 * r + 2].rearrange("p h q -> p (h q)"),
                                      a.kT[:, g, n * S:(n + 1) * S], start=True, stop=True)
                last.then_inc(done["s"], 1)

        in_steps(pe, half)


def layer1_mlp(nc, sb, psum, sem, block, ln3_s, ln3_b, w1, b1, w2, b2, x1, out):
    NG, GT = NP // 2, 2 * TOK
    M = FF // P
    w1_raw, w1_hi, w1_lo = split_weight(nc, sb, "w1", [P, G, FF])
    w2_raw, w2_hi, w2_lo = split_weight(nc, sb, "w2", [P, M, D])
    lns = sb("ln3_scale", [P, G], F32)
    lnb = sb("ln3_bias", [P, G], F32)
    bias1 = sb("bias_hidden", [P, M], F32)
    bias2 = sb("bias_mlp", [P, D], F32)
    ident = sb("ident2", [P, P], F32)
    neghalf = sb("neghalf2", [P, 2], F32)
    bnst = sb("mlp_bnst", [P, 2, 6], F32)
    mv = sb("mlp_mv", [P, 2, 2], F32)
    veps = sb("mlp_veps", [P, 2], F32)
    rstd = sb("mlp_rstd", [P, 2], F32)
    xc = sb("mlp_xc", [P, 2, D], F32)
    xb = sb("mlp_xb", [P, 2, D], F32)
    hh = sb("mlp_hh", [P, G, GT], F32R)
    hl = sb("mlp_hl", [P, G, GT], F32R)
    gf = sb("mlp_gelu", [P, M, GT], F32)
    gh = sb("mlp_gelu_high", [P, 2, M, GT], F32R)
    gl = sb("mlp_gelu_low", [P, 2, M, GT], F32R)
    res = sb("mlp_result", [P, 2, 2, D], F32)

    H = psum[:, 0:4]
    T, O = psum[:, 4], psum[:, 5]

    s_w, s_const = sem("w2_loaded"), sem("const2_set")
    s_b, s_bf, s_lnf, s_hi, s_lo = (sem("bias1_product"), sem("bias1_folded"), sem("ln3_folded"), sem("w2_high"),
                                    sem("w2_low"))
    s_bn, s_mv, s_veps, s_rstd, s_xc = (sem("mlp_bn"), sem("mlp_mean_var"), sem("mlp_var_eps"), sem("mlp_rstd_done"),
                                        sem("mlp_centred"))
    s_t, s_hh, s_hl, s_h, s_g = (sem("mlp_transposed"), sem("mlp_high"), sem("mlp_low"), sem("mlp_hidden"),
                                 sem("mlp_gelu_done"))
    s_gh, s_gl, s_xb, s_o, s_res, s_tick = (sem("gelu_high"), sem("gelu_low"), sem("mlp_residual"), sem("mlp_out"),
                                            sem("mlp_summed"), sem("wait_carrier2"))
    s_out = [sem("stored0"), sem("stored1")]
    W_LOADS = 6

    @block.sync
    def _(sp):
        sp.dma_start(w1_raw[:], w1.rearrange("(k p) n -> p k n", p=P)).then_inc(s_w, 16)
        sp.dma_start(w2_raw[:], w2.rearrange("(k p) n -> p k n", p=P)).then_inc(s_w, 16)
        for dst, src in ((lns, ln3_s), (lnb, ln3_b), (bias1, b1)):
            sp.dma_start(dst[:], src.rearrange("(m p) -> p m", p=P), allow_slow_non_contiguous=True).then_inc(s_w, 16)
        sp.dma_start(bias2[:], b2.partition_broadcast(P)).then_inc(s_w, 16)

        def step(q):
            if exists(q, 0, NG):
                sp.wait_ge(s_res, q.idx + 1)
                sp.dma_start(out[bass.ds(q.idx * 4, 4)].rearrange("(i n) c s -> (n c) i s", n=2), res[:, q.par]
                             ).then_inc(s_out[q.par], 16)
        run_steps(sp, step, 0, NG - 1, 2, 5)
        for par in range(2):
            sp.wait_ge(s_out[par], 16 * NG // 2)

    @block.gpsimd
    def _(pool):
        nc.gpsimd.memset(ident[:], 0.0).then_inc(s_const, 1)
        nc.gpsimd.memset(neghalf[:], -0.5).then_inc(s_const, 1)
        pool.wait_ge(s_const, 2)
        nc.gpsimd.affine_select(out=ident[:], in_=ident[:], compare_op=ALU.not_equal, fill=1.0, base=0,
                                pattern=[[-1, P]], channel_multiplier=1).then_inc(s_const, 1)
        pool.wait_ge(s_w, 16 * W_LOADS)

        def step(q):
            if exists(q, 2, NG):
                n = q.next(2)
                pool.wait_ge(s_veps, n.idx + 1)
                wait(pool, s_xc, 2 * n.idx)
                nc.gpsimd.tensor_tensor(rstd[:], veps[:], neghalf[:], ALU.pow).then_inc(s_rstd, 1)
            if exists(q, 0, NG):
                wait(pool, s_res, q.idx)
                nc.gpsimd.tensor_tensor(xb[:], x1[:, bass.ds(q.idx * 2, 2)], bc(bias2[:], 1, 2), ALU.add).then_inc(s_xb, 1)

        step(Pair(-2, 0, -1))
        step(Pair(-1, 1, -1))
        run_steps(pool, step, 0, NG - 1, 2, 5)

    @block.scalar
    def _(act):
        act.wait_ge(s_lnf, G)
        nc.scalar.copy(w1_hi[:], w1_raw[:]).then_inc(s_hi, 1)
        nc.scalar.copy(w2_hi[:], w2_raw[:]).then_inc(s_hi, 1)
        act.wait_ge(s_bf, 1)

        def step(q):
            if exists(q, 1, NG):
                n = q.next()
                for m in range(M):
                    if m % 2 == 0:
                        act.wait_ge(s_h, 4 * n.idx + m // 2 + 1)
                    if m == 0:
                        wait(act, s_gl, 4 * n.idx)
                    nc.scalar.activation(gf[:, m], H[:, m // 2, m % 2 * GT:(m % 2 + 1) * GT], ACT.Gelu_apprx_tanh,
                                         bias=bias1[:, m:m + 1]).then_inc(s_g, 1)
                    if m % 2 == 1:
                        act.wait_ge(s_g, 8 * n.idx + m + 1)
                        wait(act, s_o, 2 * (n.idx - 1))
                        nc.scalar.copy(gh[:, n.par, m - 1:m + 1], gf[:, m - 1:m + 1]).then_inc(s_gh, 1)
            if exists(q, 2, NG):
                n = q.next(2)
                act.wait_ge(s_t, n.idx + 1)
                wait(act, s_h, 4 * n.idx)
                nc.scalar.copy(hh[:].rearrange("p k t -> p (k t)"), T).then_inc(s_hh, 1)

        step(Pair(-2, 0, -1))
        step(Pair(-1, 1, -1))
        run_steps(act, step, 0, NG - 1, 2, 5)

    @block.vector
    def _(dve):
        dve.wait_ge(s_w, 16 * W_LOADS)
        dve.wait_ge(s_b, 1)
        nc.vector.tensor_tensor(bias1[:], T[:, 0:M], bias1[:], ALU.add).then_inc(s_bf, 1)
        for kt in range(G):
            nc.vector.tensor_scalar(w1_raw[:, kt], w1_raw[:, kt], lns[:, kt:kt + 1], None, ALU.mult).then_inc(s_lnf, 1)
        for n, (src, hi, lo) in enumerate(((w1_raw, w1_hi, w1_lo), (w2_raw, w2_hi, w2_lo))):
            dve.wait_ge(s_hi, n + 1)
            nc.vector.tensor_tensor(lo[:], src[:], hi[:].bitcast(F32), ALU.subtract).then_inc(s_lo, 1)

        def norm(n):
            wait(dve, s_mv, 2 * n.idx)
            dve.sem_inc(s_tick, 1)
            for k in range(2):
                nc.vector.bn_stats(bnst[:, k], x1[:, n.idx * 2 + k]).then_inc(s_bn, 1)
            dve.wait_ge(s_bn, 2 * n.idx + 2)
            wait(dve, s_xc, 2 * n.idx)
            dve.sem_inc(s_tick, 1)
            for k in range(2):
                nc.vector.bn_aggr(mv[:, k], bnst[:, k]).then_inc(s_mv, 1)
            dve.wait_ge(s_mv, 2 * n.idx + 2)
            wait(dve, s_rstd, n.idx)
            nc.vector.tensor_scalar(veps[:], mv[:, :, 1], EPS, None, ALU.add).then_inc(s_veps, 1)

        def step(q):
            if exists(q, 2, NG):
                norm(q.next(2))
            if exists(q, 1, NG):
                n = q.next()
                for k in range(4):
                    dve.wait_ge(s_gh, 4 * n.idx + k + 1)
                    wait(dve, s_o, 2 * (n.idx - 1))
                    nc.vector.tensor_tensor(gl[:, n.par, 2 * k:2 * k + 2], gf[:, 2 * k:2 * k + 2],
                                            gh[:, n.par, 2 * k:2 * k + 2].bitcast(F32), ALU.subtract).then_inc(s_gl, 1)
                    if k == 0 and exists(q, 2, NG):
                        centre(q.next(2))
            elif exists(q, 2, NG):
                centre(q.next(2))
            if exists(q, 2, NG):
                n = q.next(2)
                dve.wait_ge(s_hh, n.idx + 1)
                wait(dve, s_h, 4 * n.idx)
                nc.vector.tensor_tensor(hl[:].rearrange("p k t -> p (k t)"), T,
                                        hh[:].rearrange("p k t -> p (k t)").bitcast(F32), ALU.subtract).then_inc(s_hl, 1)
            if exists(q, 0, NG):
                dve.wait_ge(s_o, 2 * q.idx + 2)
                dve.wait_ge(s_xb, q.idx + 1)
                wait(dve, s_out[q.par], 16 * q.before)
                nc.vector.tensor_tensor(res[:, q.par].rearrange("p i s -> p (i s)"), O,
                                        xb[:].rearrange("p i s -> p (i s)"), ALU.add).then_inc(s_res, 1)

        def centre(n):
            dve.wait_ge(s_rstd, n.idx + 1)
            wait(dve, s_t, n.idx)
            for k in range(2):
                nc.vector.tensor_scalar(xc[:, k], x1[:, n.idx * 2 + k], mv[:, k, 0:1], rstd[:, k:k + 1], ALU.subtract,
                                        ALU.mult).then_inc(s_xc, 1)

        step(Pair(-2, 0, -1))
        step(Pair(-1, 1, -1))
        run_steps(dve, step, 0, NG - 1, 2, 5)

    @block.tensor
    def _(pe):
        mm = nc.tensor.matmul
        pe.wait_ge(s_w, 16 * W_LOADS)
        for m in range(M):
            for kt in range(G):
                last = mm(T[:, m:m + 1], w1_raw[:, kt, m * P:(m + 1) * P], lnb[:, kt:kt + 1], start=(kt == 0), stop=(kt == G - 1))
        last.then_inc(s_b, 1)
        pe.wait_ge(s_const, 3)
        pe.wait_ge(s_bf, 1)

        def step(q):
            if exists(q, 1, NG):
                n = q.next()
                if isinstance(n.idx, int) and n.idx == 0:
                    pe.wait_ge(s_lo, 2)
                pe.wait_ge(s_hl, n.idx + 1)
                for m in range(M):
                    if m % 2 == 0:
                        wait(pe, s_g, 8 * (n.idx - 1) + m + 2)
                    o = H[:, m // 2, m % 2 * GT:(m % 2 + 1) * GT]
                    for kt in range(G):
                        hi, lo = w1_hi[:, kt, m * P:(m + 1) * P], w1_lo[:, kt, m * P:(m + 1) * P]
                        mm(o, hi, hh[:, kt], start=(kt == 0), stop=False)
                        mm(o, lo, hh[:, kt], start=False, stop=False)
                        last = mm(o, hi, hl[:, kt], start=False, stop=(kt == G - 1))
                    if m % 2 == 1:
                        last.then_inc(s_h, 1)
            if exists(q, 2, NG):
                n = q.next(2)
                pe.wait_ge(s_xc, 2 * n.idx + 2)
                wait(pe, s_hl, n.idx)
                for k in range(2):
                    for kt in range(G):
                        last = nc.tensor.transpose(T[:, kt * GT + k * TOK:kt * GT + (k + 1) * TOK],
                                                   xc[:, k, kt * P:(kt + 1) * P], ident[:])
                last.then_inc(s_t, 1)
            if exists(q, 0, NG):
                pe.wait_ge(s_gl, 4 * q.idx + 4)
                wait(pe, s_res, q.idx)
                for k in range(2):
                    o = O[:, k * D:(k + 1) * D]
                    tok = slice(k * TOK, (k + 1) * TOK)
                    for m in range(M):
                        mm(o, gh[:, q.par, m, tok], w2_hi[:, m], start=(m == 0), stop=False)
                        mm(o, gh[:, q.par, m, tok], w2_lo[:, m], start=False, stop=False)
                        last = mm(o, gl[:, q.par, m, tok], w2_hi[:, m], start=False, stop=(m == M - 1))
                    last.then_inc(s_o, 1)

        step(Pair(-2, 0, -1))
        step(Pair(-1, 1, -1))
        run_steps(pe, step, 0, NG - 1, 2, 5)


def decoder(nc, x, ctx_2048, mask_1x1xSxS2_fc1, mask_Bx1xSxS2_ff1, L0_gamma, L0_beta, L0_Wq, L0_bq, L0_Wkv, L0_bkv,
            L0_Wo, L0_bo, ln1_s, ln1_b, w_qkv, b_qkv, w_ao, b_ao, ln2_s, ln2_b, w_q, b_q, w_kv, b_kv, w_co, b_co,
            ln3_s, ln3_b, w1, b1, w2, b2, out):
    with ExitStack() as kept:
        def enter(stack, make, *args):
            return stack.enter_context(make(*args))

        psum = enter(kept, nc.psum_tensor, "banks", [P, 8, 512], F32)
        x1 = enter(kept, nc.sbuf_tensor, "tokens", [P, NP, D], F32)

        def phase(build, *args):
            with ExitStack() as stack:
                def sb(name, shape, dt):
                    return enter(stack, nc.sbuf_tensor, name, shape, dt)

                def sem(name):
                    return enter(stack, nc.semaphore, name)
                with nc.Block() as block:
                    build(nc, sb, psum, sem, block, *args)

        phase(layer0, x, ctx_2048, L0_gamma, L0_beta, L0_Wq, L0_bq, L0_Wkv, L0_bkv, L0_Wo, L0_bo, x1)
        phase(layer1_attentions, ctx_2048, mask_1x1xSxS2_fc1, mask_Bx1xSxS2_ff1, ln1_s, ln1_b, w_qkv, b_qkv, w_ao,
              b_ao, ln2_s, ln2_b, w_q, b_q, w_kv, b_kv, w_co, b_co, x1)
        phase(layer1_mlp, ln3_s, ln3_b, w1, b1, w2, b2, x1, out)


_INS = ["x", "ctx_2048", "mask_1x1xSxS2_fc1", "mask_Bx1xSxS2_ff1", "L0_xattn_gamma", "L0_xattn_beta", "L0_xattn_Wq",
        "L0_xattn_bq", "L0_xattn_Wkv", "L0_xattn_bkv", "L0_xattn_Wo", "L0_xattn_bo"] + [
        "L1_xattn_" + k for k in ("ln1_s", "ln1_b", "w_qkv", "b_qkv", "w_ao", "b_ao", "ln2_s", "ln2_b", "w_q", "b_q",
                                  "w_kv", "b_kv", "w_co", "b_co", "ln3_s", "ln3_b", "w1", "b1", "w2", "b2")]


def kernel(**inputs):
    import numpy as _np
    import concourse.bacc as _bacc
    from concourse import mybir as _mybir
    from concourse.bass_utils import run_bass_kernel_spmd as _run

    nc = _bacc.Bacc("TRN2", target_bir_lowering=False, num_devices=1)
    arrays, args = {}, []
    for name in _INS:
        a = _np.ascontiguousarray(inputs[name])
        arrays[f"in_{name}"] = a
        args.append(nc.dram_tensor(f"in_{name}", a.shape, _mybir.dt.from_np(a.dtype), kind="ExternalInput").ap())
    args.append(nc.dram_tensor("out", (B, S, D), F32, kind="ExternalOutput").ap())
    decoder(nc, *args)
    r = _run(nc, [arrays], core_ids=[0])
    return r.results[0]["out"]
```

```python
from contextlib import ExitStack

import concourse.bass as bass
from concourse import mybir

F32 = mybir.dt.float32
F32R = mybir.dt.float32r
ALU = mybir.AluOpType
ACT = mybir.ActivationFunctionType
AX = mybir.AxisListType

P = 128
B, S, D = 32, 64, 256
NP = B // 2
H0, C0 = 8, 64
QT, KT = D // P, D // P
SCALE0 = float(C0) ** -0.5
EPS = 1e-5


class Pair:

    def __init__(self, idx, par, before):
        self.idx, self.par, self.before = idx, par, before

    def next(self, n=1):
        off = self.par + n
        return Pair(self.idx + n, off % 2, self.before + off // 2)


def run_steps(eng, step, first, last, loop_first, loop_last):
    idx = first
    while idx <= last:
        if idx == loop_first:
            turns = (loop_last + 1 - loop_first) // 2
            with eng.Fori(0, turns) as t:
                step(Pair(t * 2 + loop_first, 0, t + loop_first // 2))
                step(Pair(t * 2 + loop_first + 1, 1, t + loop_first // 2))
            idx += 2 * turns
        else:
            step(Pair(idx, idx % 2, idx // 2))
            idx += 1


def exists(pair, off, count=NP):
    return not isinstance(pair.idx, int) or 0 <= pair.idx + off < count


def wait(eng, sem, value):
    if not isinstance(value, int) or value > 0:
        eng.wait_ge(sem, value)


def bc(ap, dim, n):
    shape = list(ap.shape)
    return ap.unsqueeze(dim).broadcast_to(shape[:dim] + [n] + shape[dim:])


def layer0(nc, sb, psum, sem, block, x, ctx, gamma, beta, Wq, bq, Wkv, bkv, Wo, bo, x1):
    wq2 = sb("wq2", [C0, H0, 2, C0], F32)
    wk2 = sb("wk2", [C0, H0, 2, C0], F32)
    wv2 = sb("wv2", [C0, H0, 2, C0], F32)
    wo_nat = sb("wo_nat", [C0, H0 * C0], F32)
    wo2 = sb("wo2", [C0, H0, 2, C0], F32)
    bq_sb = sb("bq_sb", [C0, H0], F32)
    bv_sb = sb("bv_sb", [C0, H0], F32)
    gamma2 = sb("gamma2", [P, 1], F32)
    beta2 = sb("beta2", [P, 1], F32)
    bo2 = sb("bo2", [P, 1], F32)
    a_st = sb("a_st", [P, H0, P], F32R)
    qbias = sb("qbias", [P, H0], F32)
    wvo_hi = sb("wvo_hi", [P, H0 * C0], F32R)
    wvo_lo = sb("wvo_lo", [P, H0 * C0], F32R)
    obias = sb("obias", [P, 1], F32)
    ident = sb("ident", [P, P], F32)
    mean64 = sb("mean64", [C0, P], F32)
    neghalf = sb("neghalf", [P, 2], F32)
    xd = sb("xd", [P, 2, 2, D], F32)
    cd = sb("cd", [P, 2, 2, D], F32)
    xp = sb("xp", [P, 2, D], F32)
    bnst = sb("bnst", [P, 2, 6], F32)
    mv = sb("mv", [P, 2, 2], F32)
    mvm = sb("mvm", [P, 2, 2], F32)
    dev = sb("dev", [P, 2], F32)
    dev2 = sb("dev2", [P, 2], F32)
    veps = sb("veps", [P, 2], F32)
    rstd = sb("rstd", [P, 2], F32)
    s1 = sb("s1", [P, 2], F32)
    ms1 = sb("ms1", [P, 2], F32)
    s2 = sb("s2", [P, 2], F32)
    xh = sb("xh", [P, 2, 2, D], F32R)
    xn = sb("xn", [P, 2, D], F32)
    xl = sb("xl", [P, 2, 2, D], F32R)
    cs = sb("cs", [P, 2, 2, D], F32R)
    c1 = sb("c1", [P, 2, 2, D], F32R)
    qh = sb("qh", [P, 2, H0, 2, D], F32R)
    ql = sb("ql", [P, 2, 2, H0, D], F32R)
    vw = sb("vw", [P, 2, 2, KT, H0, C0 + 1], F32)
    pt = sb("pt", [P, 2, KT, D], F32)
    nmax = sb("nmax", [P, 2, H0, QT], F32)
    nmaxt = sb("nmaxt", [H0 * QT, 2, P], F32R)
    rden = sb("rden", [P, 2, 2, QT], F32)
    yn = sb("yn", [P, 2, 4, 2, QT, C0], F32)
    ysum = sb("ysum", [P, 2, 4, QT, C0], F32)
    ot = sb("ot", [P, 2, QT, 2, C0], F32)

    T = [psum[:, 0], psum[:, 1]]
    M = [psum[:, 2], psum[:, 3]]
    J = [psum[:, 4], psum[:, 5]]
    Y = [psum[:, 6], psum[:, 7]]

    STATS = 2 * QT * (C0 + 1)

    s_w, s_const, s_ones = sem("w_loaded"), sem("const_set"), sem("ones_set")
    s_wot, s_wot_ev = sem("wo_transposed"), sem("wo_copied")
    s_fold, s_fold_ev, s_fold_lo = sem("folded"), sem("fold_high"), sem("fold_low")
    s_x = [sem("x_loaded0"), sem("x_loaded1")]
    s_c = [sem("ctx_loaded0"), sem("ctx_loaded1")]
    s_xp = [sem("xres_loaded0"), sem("xres_loaded1")]
    s_bn, s_mv, s_st = sem("bn_done"), sem("row_stats"), sem("sample_stats")
    s_dev, s_dev2, s_veps = sem("dev_done"), sem("dev2_done"), sem("var_eps")
    s_aff, s_xh, s_xn, s_xl = sem("affine"), sem("x_high"), sem("x_norm"), sem("x_low")
    s_cs, s_c1, s_csl = sem("ctx_high"), sem("ctx_high_ones"), sem("ctx_low")
    s_q, s_qh, s_ql = sem("q_projected"), sem("q_high"), sem("q_low")
    s_s, s_max = sem("scores_for_max"), sem("max_taken")
    s_mt, s_mtc, s_row = sem("max_transposed"), sem("max_rounded"), [sem("max_row0"), sem("max_row1")]
    s_v, s_vw = sem("v_projected"), sem("v_copied")
    s_t, s_exp, s_pv = sem("scores"), sem("probs"), sem("weighted")
    s_rden, s_yn, s_ysum = sem("denominators"), sem("normalised"), sem("heads_summed")
    s_tick = sem("wait_carrier")
    s_ot, s_x1 = sem("out_transposed"), sem("x1_ready")

    @block.sync
    def _(sp):
        for copy in range(2):
            sp.dma_start(wq2[:, :, copy], Wq.rearrange("(h o) c -> o h c", o=C0)).then_inc(s_w, 16)
            sp.dma_start(wk2[:, :, copy], Wkv[0:H0 * C0].rearrange("(h o) c -> o h c", o=C0)).then_inc(s_w, 16)
            sp.dma_start(wv2[:, :, copy], Wkv[H0 * C0:].rearrange("(h o) c -> o h c", o=C0)).then_inc(s_w, 16)
            half = slice(64 * copy, 64 * copy + 64)
            sp.dma_start(gamma2[half], gamma.rearrange("(c a) -> c a", a=1)).then_inc(s_w, 16)
            sp.dma_start(beta2[half], beta.rearrange("(c a) -> c a", a=1)).then_inc(s_w, 16)
            sp.dma_start(bo2[half], bo.rearrange("(c a) -> c a", a=1)).then_inc(s_w, 16)
        sp.dma_start(wo_nat[:], Wo).then_inc(s_w, 16)
        sp.dma_start(bq_sb[:], bq.rearrange("(h o) -> o h", o=C0), allow_slow_non_contiguous=True).then_inc(s_w, 16)
        sp.dma_start(bv_sb[:], bkv[H0 * C0:].rearrange("(h o) -> o h", o=C0), allow_slow_non_contiguous=True).then_inc(s_w, 16)

        def load(p):
            for copy in range(2):
                half = slice(64 * copy, 64 * copy + 64)
                sp.dma_start(xd[half, p.par], x[bass.ds(p.idx * 2, 2)].rearrange("n c s -> c n s")
                             ).then_inc(s_x[p.par], 16)
            for copy in range(2):
                half = slice(64 * copy, 64 * copy + 64)
                sp.dma_start(cd[half, p.par], ctx[bass.ds(p.idx * 2, 2)].rearrange("n c s -> c n s")
                             ).then_inc(s_c[p.par], 16)

        def max_row(p, n):
            sp.wait_ge(s_mtc, p.idx * 2 + n + 1)
            sp.dma_start(ql[C0:C0 + 1, p.par, n].rearrange("a h (t q) -> a (h t) q", t=QT).bitcast(F32),
                         nmaxt[:, n].bitcast(F32)).then_inc(s_row[n], 16)

        def step(p):
            if exists(p, 3):
                p3 = p.next(3)
                wait(sp, s_xh, 2 * (p3.idx - 1))
                wait(sp, s_xl, p3.idx - 1)
                wait(sp, s_csl, p3.idx - 1)
                wait(sp, s_c1, p3.idx - 1)
                load(p3)
            if exists(p, 0):
                max_row(p, 1)
                wait(sp, s_x1, p.idx - 1)
                sp.dma_start(xp[:, p.par], x[bass.ds(p.idx * 2, 2)].rearrange("n c s -> (n c) s")
                             ).then_inc(s_xp[p.par], 16)
            if exists(p, 1):
                max_row(p.next(), 0)

        load(Pair(0, 0, 0))
        load(Pair(1, 1, 0))
        step(Pair(-1, 1, -1))
        run_steps(sp, step, 0, NP - 1, 2, NP - 5)

    @block.gpsimd
    def _(pool):
        nc.gpsimd.memset(ident[:], 0.0).then_inc(s_const, 1)
        nc.gpsimd.memset(mean64[:], 1.0 / C0).then_inc(s_const, 1)
        nc.gpsimd.memset(neghalf[:], -0.5).then_inc(s_const, 1)
        nc.gpsimd.memset(vw[:, :, :, :, :, C0:C0 + 1], 1.0).then_inc(s_const, 1)
        pool.wait_ge(s_const, 1)
        nc.gpsimd.affine_select(out=ident[:], in_=ident[:], compare_op=ALU.not_equal, fill=1.0, base=0,
                                pattern=[[-1, P]], channel_multiplier=1).then_inc(s_const, 1)
        pool.wait_ge(s_w, 16 * 15)
        pool.wait_ge(s_const, 5)

        def prepare_x(p):
            pool.wait_ge(s_veps, p.idx + 1)
            wait(pool, s_xh, 2 * p.idx)
            wait(pool, s_xn, 2 * p.idx)
            wait(pool, s_xl, p.idx)
            nc.gpsimd.tensor_tensor(rstd[:], veps[:], neghalf[:], ALU.pow).then_inc(s_aff, 1)
            pool.wait_ge(s_aff, 4 * p.idx + 1)
            nc.gpsimd.tensor_tensor(s1[:], rstd[:], gamma2[:].broadcast_to([P, 2]), ALU.mult).then_inc(s_aff, 1)
            pool.wait_ge(s_aff, 4 * p.idx + 2)
            nc.gpsimd.tensor_tensor(ms1[:], s1[:], mvm[:, :, 0], ALU.mult).then_inc(s_aff, 1)
            pool.wait_ge(s_aff, 4 * p.idx + 3)
            nc.gpsimd.tensor_tensor(s2[:], beta2[:].broadcast_to([P, 2]), ms1[:], ALU.subtract).then_inc(s_aff, 1)
            pool.wait_ge(s_aff, 4 * p.idx + 4)
            pool.sem_inc(s_tick, 1)
            for n in range(2):
                nc.gpsimd.tensor_scalar(xn[:, n], xd[:, p.par, n], s1[:, n:n + 1], s2[:, n:n + 1],
                                        ALU.mult, ALU.add).then_inc(s_xn, 1)
            pool.wait_ge(s_xn, 2 * p.idx + 2)
            pool.wait_ge(s_xh, 2 * p.idx + 2)
            wait(pool, s_q, H0 * (p.idx - 1))
            nc.gpsimd.tensor_tensor(xl[:, p.par], xn[:], xh[:, p.par].bitcast(F32), ALU.subtract).then_inc(s_xl, 1)

        def prepare_context(p):
            pool.wait_ge(s_xl, p.idx + 1)
            pool.wait_ge(s_cs, p.idx + 1)
            nc.gpsimd.tensor_tensor(cs[C0:P, p.par], cd[C0:P, p.par], cs[C0:P, p.par].bitcast(F32),
                                    ALU.subtract).then_inc(s_csl, 1)

        def sum_heads(p, n):
            pool.wait_ge(s_yn, 8 * p.idx + 4 * n + 4)
            c = 6 * p.idx + 3 * n
            yv = yn[:, n].rearrange("p a b t c -> p (a b) t c")
            a = ysum[:, n]
            wait(pool, s_ysum, c)
            nc.gpsimd.tensor_tensor(a, yv[:, 0:4], yv[:, 4:8], ALU.add).then_inc(s_ysum, 1)
            pool.wait_ge(s_ysum, c + 1)
            nc.gpsimd.tensor_tensor(a[:, 0:2], a[:, 0:2], a[:, 2:4], ALU.add).then_inc(s_ysum, 1)
            pool.wait_ge(s_ysum, c + 2)
            wait(pool, s_ot, p.idx - 1)
            nc.gpsimd.tensor_tensor(ot[:, p.par, :, n], a[:, 0], a[:, 1], ALU.add).then_inc(s_ysum, 1)

        def step(p):
            if exists(p, 0):
                sum_heads(p, 0)
            if exists(p, 2):
                prepare_x(p.next(2))
                prepare_context(p.next(2))
                pool.wait_ge(s_csl, p.idx + 3)
            if exists(p, 0):
                sum_heads(p, 1)

        step(Pair(-2, 0, -1))
        step(Pair(-1, 1, -1))
        run_steps(pool, step, 0, NP - 1, 2, NP - 3)

    @block.scalar
    def _(act):
        act.wait_ge(s_fold, 1)
        for b in range(2):
            nc.scalar.activation(a_st[:, 4 * b:4 * b + 4], T[b].rearrange("p (h c) -> p h c", c=P), ACT.Copy,
                                 scale=SCALE0).then_inc(s_fold_ev, 1)
        nc.scalar.copy(wvo_hi[:], M[0]).then_inc(s_fold_ev, 1)
        nc.scalar.activation(qbias[:], M[1][:, 0:H0], ACT.Copy, scale=SCALE0).then_inc(s_fold_ev, 1)

        def prepare_x(p):
            act.wait_ge(s_aff, 4 * p.idx + 4)
            wait(act, s_q, H0 * (p.idx - 1))
            for n in range(2):
                nc.scalar.activation(xh[:, p.par, n], xd[:, p.par, n], ACT.Identity, bias=s2[:, n:n + 1],
                                     scale=s1[:, n:n + 1]).then_inc(s_xh, 1)

        def prepare_context(p):
            act.wait_ge(s_c[p.par], 32 * (p.before + 1))
            wait(act, s_v, 4 * (p.idx - 1))
            wait(act, s_s, 16 * (p.idx - 1))
            wait(act, s_t, 16 * (p.idx - 1))
            nc.scalar.copy(cs[:, p.par], cd[:, p.par]).then_inc(s_cs, 1)
            nc.scalar.copy(c1[0:C0, p.par], cd[0:C0, p.par]).then_inc(s_c1, 1)

        def q_high(p, h):
            act.wait_ge(s_q, H0 * p.idx + h + 1)
            if h == 0:
                wait(act, s_s, 16 * (p.idx - 1))
                wait(act, s_t, 16 * (p.idx - 1))
            nc.scalar.activation(qh[:, p.par, h].rearrange("p n s -> p (n s)"), J[h % 2], ACT.Identity,
                                 bias=qbias[:, h:h + 1]).then_inc(s_qh, 1)

        def v_copy(p, n, kt):
            act.wait_ge(s_v, 4 * p.idx + 2 * n + kt + 1)
            if n == 0 and kt == 0:
                wait(act, s_pv, 16 * (p.idx - 1))
            nc.scalar.copy(vw[:, p.par, n, kt, :, 0:C0], J[kt].rearrange("p (h c) -> p h c", c=C0)
                           ).then_inc(s_vw, 1)

        def exp(p, u):
            act.wait_ge(s_t, 16 * p.idx + u + 1)
            wait(act, s_pv, 16 * p.idx + u - 1)
            nc.scalar.activation(pt[:, u % 2].rearrange("p t q -> p (t q)"), T[u % 2], ACT.Exp
                                 ).then_inc(s_exp, 1)

        def step(p):
            for u in range(16):
                if u < H0 and exists(p, 1):
                    q_high(p.next(), u)
                if exists(p, 0):
                    exp(p, u)
                if u in (11, 12, 13, 14) and exists(p, 1):
                    v_copy(p.next(), (u - 11) // 2, (u - 11) % 2)
                if u == 11 and exists(p, 2):
                    prepare_x(p.next(2))
            if exists(p, 2):
                prepare_context(p.next(2))

        step(Pair(-2, 0, -1))
        step(Pair(-1, 1, -1))
        run_steps(act, step, 0, NP - 1, 2, NP - 3)

    @block.vector
    def _(dve):
        nc.vector.memset(c1[C0:P].bitcast(F32), 0.0).then_inc(s_ones, 1)
        dve.wait_ge(s_ones, 1)
        nc.vector.memset(c1[C0:C0 + 1].bitcast(F32), 1.0).then_inc(s_ones, 1)
        nc.vector.memset(ql[C0:P].bitcast(F32), 0.0).then_inc(s_ones, 1)
        dve.wait_ge(s_wot, 1)
        for copy in range(2):
            nc.vector.tensor_copy(wo2[:, :, copy], J[0][0:C0].rearrange("o (h c) -> o h c", c=C0)).then_inc(s_wot_ev, 1)
        dve.wait_ge(s_fold_ev, 4)
        for b in range(2):
            hi = a_st[C0:P, 4 * b:4 * b + 4]
            nc.vector.scalar_tensor_tensor(hi, T[b][C0:P].rearrange("p (h c) -> p h c", c=P), SCALE0,
                                           hi.bitcast(F32), ALU.mult, ALU.subtract).then_inc(s_fold_lo, 1)
        nc.vector.tensor_tensor(wvo_lo[:], M[0], wvo_hi[:].bitcast(F32), ALU.subtract).then_inc(s_fold_lo, 1)
        nc.vector.tensor_tensor(obias[:], M[1][:, 32:33], bo2[:], ALU.add).then_inc(s_fold_lo, 1)

        def row_stats(p):
            dve.wait_ge(s_x[p.par], 32 * (p.before + 1))
            wait(dve, s_mv, 2 * p.idx)
            for n in range(2):
                nc.vector.bn_stats(bnst[:, n], xd[:, p.par, n]).then_inc(s_bn, 1)
            dve.wait_ge(s_bn, 2 * p.idx + 2)
            wait(dve, s_st, 2 * p.idx)
            wait(dve, s_dev, 2 * p.idx)
            dve.sem_inc(s_tick, 1)
            for n in range(2):
                nc.vector.bn_aggr(mv[:, n], bnst[:, n]).then_inc(s_mv, 1)

        def deviation(p):
            dve.wait_ge(s_st, 2 * p.idx + 1)
            wait(dve, s_aff, 4 * p.idx)
            wait(dve, s_veps, p.idx)
            wait(dve, s_dev2, p.idx)
            nc.vector.tensor_copy(mvm[:], Y[0][:, STATS:STATS + 4].rearrange("p (n k) -> p n k", k=2)).then_inc(s_dev, 1)
            dve.wait_ge(s_dev, 2 * p.idx + 1)
            dve.wait_ge(s_mv, 2 * p.idx + 2)
            nc.vector.tensor_tensor(dev[:], mv[:, :, 0], mvm[:, :, 0], ALU.subtract).then_inc(s_dev, 1)
            dve.wait_ge(s_dev, 2 * p.idx + 2)
            nc.vector.tensor_tensor(dev2[:], dev[:], dev[:], ALU.mult).then_inc(s_dev2, 1)

        def variance(p):
            dve.wait_ge(s_st, 2 * p.idx + 2)
            nc.vector.scalar_tensor_tensor(veps[:], Y[0][:, STATS:STATS + 2], EPS, mvm[:, :, 1], ALU.add, ALU.add
                                           ).then_inc(s_veps, 1)

        def q_low(p, h):
            dve.wait_ge(s_qh, H0 * p.idx + h + 1)
            if h == 0:
                wait(dve, s_t, 16 * (p.idx - 1))
            nc.vector.scalar_tensor_tensor(ql[0:C0, p.par, :, h], J[h % 2][0:C0].rearrange("p (n s) -> p n s", n=2),
                                           qbias[0:C0, h:h + 1], qh[0:C0, p.par, h].bitcast(F32),
                                           ALU.add, ALU.subtract).then_inc(s_ql, 1)

        def maximum(p, k):
            n, h = k // H0, k % H0
            dve.wait_ge(s_s, 16 * p.idx + k + 1)
            if k % H0 == 0:
                wait(dve, s_mt, 2 * (p.idx - 1) + n + 1)
            nc.vector.tensor_reduce(out=nmax[:, n, h], in_=M[k % 2].rearrange("p (t k) -> p t k", t=QT),
                                    op=ALU.max, axis=AX.X, negate=True).then_inc(s_max, 1)

        def round_max(p, n):
            dve.wait_ge(s_mt, 2 * p.idx + n + 1)
            wait(dve, s_row[n], 16 * p.idx)
            nc.vector.tensor_copy(nmaxt[:, n], J[0][0:H0 * QT, 0:P]).then_inc(s_mtc, 1)

        def normalise(p, g):
            n, a = g // 4, g % 4
            dve.wait_ge(s_pv, 16 * p.idx + 2 * g + 2)
            wait(dve, s_yn, 8 * p.idx + g - 1)
            yb = Y[g % 2][:, 0:2 * QT * (C0 + 1)].rearrange("p (b t c) -> p b t c", t=QT, c=C0 + 1)
            nc.vector.reciprocal(rden[:, g % 2], yb[:, :, :, C0]).then_inc(s_rden, 1)
            dve.wait_ge(s_rden, 8 * p.idx + g + 1)
            if a == 0:
                wait(dve, s_ysum, 6 * (p.idx - 1) + 3 * n + 1)
            nc.vector.tensor_tensor(yn[:, n, a], yb[:, :, :, 0:C0], bc(rden[:, g % 2], 3, C0), ALU.mult
                                    ).then_inc(s_yn, 1)

        def residual(p):
            dve.wait_ge(s_ot, p.idx + 1)
            dve.wait_ge(s_xp[p.par], 16 * (p.before + 1))
            nc.vector.scalar_tensor_tensor(x1[:, p.idx], J[1][:, 0:D], obias[:], xp[:, p.par], ALU.add, ALU.add
                                           ).then_inc(s_x1, 1)

        def step(p):
            for u in range(16):
                if u < H0 and exists(p, 1):
                    q_low(p.next(), u)
                if u == 1 and exists(p, 0):
                    round_max(p, 1)
                if u == 4 and exists(p, -1):
                    residual(p.next(-1))
                if u == 0 and exists(p, 2):
                    row_stats(p.next(2))
                if u == 3 and exists(p, 2):
                    deviation(p.next(2))
                if u == 7 and exists(p, 2):
                    variance(p.next(2))
                if u % 2 == 1 and u > 1 and exists(p, 0):
                    normalise(p, u // 2 - 1)
                if u >= 1 and u <= 8 and exists(p, 1):
                    maximum(p.next(), u - 1)
                if u >= 8 and exists(p, 1):
                    maximum(p.next(), u)
                if u == 10 and exists(p, 1):
                    round_max(p.next(), 0)
            if exists(p, 0):
                normalise(p, 7)

        step(Pair(-2, 0, -1))
        step(Pair(-1, 1, -1))
        run_steps(dve, step, 0, NP - 1, 2, NP - 3)
        residual(Pair(NP - 1, (NP - 1) % 2, (NP - 1) // 2))

    @block.tensor
    def _(pe):
        mm = nc.tensor.matmul
        pe.wait_ge(s_w, 16 * 15)
        pe.wait_ge(s_const, 5)
        for h in range(H0):
            last = nc.tensor.transpose(J[0][0:C0, h * C0:(h + 1) * C0], wo_nat[:, h * C0:(h + 1) * C0], ident[0:C0, 0:C0])
        last.then_inc(s_wot, 1)
        for h in range(H0):
            mm(T[h // 4][:, h % 4 * P:(h % 4 + 1) * P], wq2[:, h].rearrange("o a c -> o (a c)"),
               wk2[:, h].rearrange("o a c -> o (a c)"), start=True, stop=True)
            mm(M[1][:, h:h + 1], wk2[:, h].rearrange("o a c -> o (a c)"), bq_sb[:, h:h + 1], start=True, stop=True)
        pe.wait_ge(s_wot_ev, 2)
        for h in range(H0):
            mm(M[0][:, h * C0:(h + 1) * C0], wv2[:, h].rearrange("o a c -> o (a c)"), wo2[:, h, 0], start=True, stop=True)
        for h in range(H0):
            last = mm(M[1][:, 32:33], wo2[:, h].rearrange("o a c -> o (a c)"), bv_sb[:, h:h + 1],
                      start=(h == 0), stop=(h == H0 - 1))
        last.then_inc(s_fold, 1)
        pe.wait_ge(s_fold_lo, 4)
        pe.wait_ge(s_ones, 3)

        def stats(p, k):
            if k == 0:
                pe.wait_ge(s_mv, 2 * p.idx + 2)
                wait(pe, s_veps, p.idx)
                mm(Y[0][:, STATS:STATS + 4], mean64[:], mv[0:C0].rearrange("p n k -> p (n k)"), start=True, stop=True
                   ).then_inc(s_st, 1)
            else:
                pe.wait_ge(s_dev2, p.idx + 1)
                mm(Y[0][:, STATS:STATS + 2], mean64[:], dev2[0:C0], start=True, stop=True).then_inc(s_st, 1)

        def project_q(p, h):
            if h == 0:
                pe.wait_ge(s_xl, p.idx + 1)
                pe.wait_ge(s_xh, 2 * p.idx + 2)
                wait(pe, s_vw, 4 * p.idx)
            else:
                wait(pe, s_ql, H0 * p.idx + h - 1)
            if h == 2:
                wait(pe, s_mtc, 2 * p.idx)
            if h == 5:
                wait(pe, s_x1, p.idx - 1)
            mm(J[h % 2], a_st[:, h], xh[:, p.par].rearrange("p n s -> p (n s)"), start=True, stop=False)
            mm(J[h % 2], a_st[:, h], xl[:, p.par].rearrange("p n s -> p (n s)"), start=False, stop=True
               ).then_inc(s_q, 1)

        def scores_for_max(p, k):
            n, h = k // H0, k % H0
            if k == 0:
                pe.wait_ge(s_csl, p.idx + 1)
            if n == 0:
                pe.wait_ge(s_qh, H0 * p.idx + h + 1)
            wait(pe, s_max, 16 * p.idx + k - 1)
            for qt in range(QT):
                last = mm(M[k % 2][:, qt * D:(qt + 1) * D], qh[:, p.par, h, n, qt * P:(qt + 1) * P], cs[:, p.par, n],
                          start=True, stop=True)
            last.then_inc(s_s, 1)

        def transpose_max(p, n):
            pe.wait_ge(s_max, 16 * p.idx + 8 * n + 8)
            nc.tensor.transpose(J[0][0:H0 * QT, 0:P], nmax[:, n].rearrange("p h t -> p (h t)"), ident[:]
                                ).then_inc(s_mt, 1)

        def project_v(p, n, kt):
            if n == 0 and kt == 0:
                wait(pe, s_mtc, 2 * p.idx + 1)
            if n == 0 and kt == 1:
                wait(pe, s_ql, H0 * p.idx + H0)
            if n == 1:
                pe.wait_ge(s_vw, 4 * p.idx + kt + 1)
            keys = slice(kt * P, (kt + 1) * P)
            mm(J[kt], cs[:, p.par, n, keys], wvo_hi[:], start=True, stop=False)
            mm(J[kt], cs[:, p.par, n, keys], wvo_lo[:], start=False, stop=True).then_inc(s_v, 1)

        def scores(p, u):
            n, h = u // H0, u % H0
            if h == 0:
                pe.wait_ge(s_row[n], 16 * (p.idx + 1))
            if u == 0:
                pe.wait_ge(s_c1, p.idx + 1)
                pe.wait_ge(s_ql, H0 * (p.idx + 1))
            wait(pe, s_exp, 16 * p.idx + u - 1)
            for kt in range(KT):
                keys = slice(kt * P, (kt + 1) * P)
                out = T[u % 2][:, kt * D:(kt + 1) * D]
                mm(out, cs[:, p.par, n, keys], qh[:, p.par, h, n], start=True, stop=False)
                last = mm(out, c1[:, p.par, n, keys], ql[:, p.par, n, h], start=False, stop=True)
            last.then_inc(s_t, 1)

        def weigh(p, u):
            n, h = u // H0, u % H0
            pe.wait_ge(s_exp, 16 * p.idx + u + 1)
            if u == 0:
                pe.wait_ge(s_vw, 4 * p.idx + 4)
                wait(pe, s_veps, p.idx + 2 if exists(p, 1) else NP)
            if u % 2 == 0:
                wait(pe, s_yn, 8 * p.idx + u // 2 - 1)
            for qt in range(QT):
                at = (u % 2 * QT + qt) * (C0 + 1)
                out = Y[u // 2 % 2][:, at:at + C0 + 1]
                for kt in range(KT):
                    last = mm(out, pt[:, u % 2, kt, qt * P:(qt + 1) * P], vw[:, p.par, n, kt, h],
                              start=(kt == 0), stop=(kt == KT - 1))
            last.then_inc(s_pv, 1)

        def transpose_out(p):
            pe.wait_ge(s_ysum, 6 * p.idx + 6)
            for qt in range(QT):
                last = nc.tensor.transpose(J[1][:, qt * P:(qt + 1) * P],
                                           ot[:, p.par, qt].rearrange("q n c -> q (n c)"), ident[:])
            last.then_inc(s_ot, 1)

        def step(p):
            for u in range(16):
                if u < H0 and exists(p, 1):
                    project_q(p.next(), u)
                if u == 1 and exists(p, 0):
                    if exists(p, 1):
                        pe.wait_ge(s_ql, H0 * (p.idx + 1) + 1)
                    pe.wait_ge(s_vw, 4 * (p.idx + 1))
                    transpose_max(p, 1)
                if u == 2 and exists(p, 2):
                    stats(p.next(2), 0)
                if u == 6 and exists(p, 2):
                    stats(p.next(2), 1)
                if u == 4 and exists(p, -1):
                    if exists(p, 1):
                        pe.wait_ge(s_ql, H0 * (p.idx + 1) + 4)
                    pe.wait_ge(s_vw, 4 * (p.idx + 1))
                    transpose_out(p.next(-1))
                if exists(p, 0):
                    scores(p, u)
                    if u > 0:
                        weigh(p, u - 1)
                if u >= 1 and u <= 8 and exists(p, 1):
                    scores_for_max(p.next(), u - 1)
                if u >= 8 and exists(p, 1):
                    scores_for_max(p.next(), u)
                if u == 10 and exists(p, 1):
                    pe.wait_ge(s_ql, H0 * (p.idx + 2))
                    transpose_max(p.next(), 0)
                if u in (11, 12, 13, 14) and exists(p, 1):
                    project_v(p.next(), (u - 11) // 2, (u - 11) % 2)
            if exists(p, 0):
                weigh(p, 15)

        step(Pair(-2, 0, -1))
        step(Pair(-1, 1, -1))
        run_steps(pe, step, 0, NP - 1, 2, NP - 3)
        pe.wait_ge(s_x1, NP - 1)
        transpose_out(Pair(NP - 1, (NP - 1) % 2, (NP - 1) // 2))
    return s_x1


NH, HD = 16, D // 16
G = D // P
FF = 4 * D
SCALE1 = float(HD) ** -0.5
TOK = 2 * S


class Attention:

    def __init__(self, name, sb, sem, cross):
        cols = 2 * D if cross else D
        self.cross = cross
        self.bnst = sb(name + "_bnst", [P, 6], F32)
        self.mv = sb(name + "_mv", [P, 2], F32)
        self.veps = sb(name + "_veps", [P, 1], F32)
        self.rstd = sb(name + "_rstd", [P, 1], F32)
        self.xc = sb(name + "_xc", [P, D], F32)
        self.hh = sb(name + "_hh", [P, cols], F32R)
        self.hl = sb(name + "_hl", [P, cols], F32R)
        self.qs = sb(name + "_qs", [P, G, TOK], F32)
        self.q8 = sb(name + "_q8", [P, G, 2, 8, S], F32)
        self.kT = sb(name + "_kT", [P, G, TOK], F32)
        self.vz = sb(name + "_vz", [P, 2, 2, D], F32)
        self.t = sb(name + "_t", [P, 2, 8, S], F32)
        self.nmax = sb(name + "_nmax", [P, 2, 8], F32)
        self.den = sb(name + "_den", [P, 2, 8], F32)
        self.rden = sb(name + "_rden", [P, 2, 8], F32)
        self.pT = sb(name + "_pT", [P, 8, P], F32)
        self.yh = sb(name + "_yh", [P, G, TOK], F32R)
        self.yl = sb(name + "_yl", [P, G, TOK], F32R)
        self.xb = sb(name + "_xb", [P, D], F32)
        self.done = {what: sem(name + "_" + what) for what in (
            "bnst", "mv", "veps", "rstd", "xc", "transposed", "hh", "hl", "qk", "qs", "q8_g0", "q8_g1", "kT", "v",
            "vz", "s", "masked", "mask_added", "nmax", "shifted", "exp", "den", "rden", "probs", "p_transposed",
            "pT", "y", "yh", "yl", "o", "xb", "x")}


def split_weight(nc, sb, name, shape):
    return (sb(name + "_raw", shape, F32), sb(name + "_high", shape, F32R), sb(name + "_low", shape, F32R))


def layer1_attentions(nc, sb, psum, sem, block, ctx, self_mask, cross_mask, ln1_s, ln1_b, w_qkv, b_qkv, w_ao, b_ao,
                      ln2_s, ln2_b, w_q, b_q, w_kv, b_kv, w_co, b_co, x1):
    SELF = Attention("self", sb, sem, False)
    CROSS = Attention("cross", sb, sem, True)
    wqkv_raw, wqkv_hi, wqkv_lo = split_weight(nc, sb, "w_qkv", [P, G, 3 * D])
    wao_raw, wao_hi, wao_lo = split_weight(nc, sb, "w_ao", [P, G, D])
    wcq_raw, wcq_hi, wcq_lo = split_weight(nc, sb, "w_q", [P, G, D])
    wkv_raw, wkv_hi, wkv_lo = split_weight(nc, sb, "w_kv", [P, G, 2 * D])
    wco_raw, wco_hi, wco_lo = split_weight(nc, sb, "w_co", [P, G, D])
    lns = sb("ln_scales", [P, 2, G], F32)
    lnb = sb("ln_biases", [P, 2, G], F32)
    bias1 = sb("bias_self", [P, 3 * G], F32)
    bias2 = sb("bias_cross", [P, 3 * G], F32)
    bias_out = sb("bias_out", [P, 2, D], F32)
    ident = sb("ident1", [P, P], F32)
    mask8 = sb("mask8", [P, 8], F32)
    m_self = sb("m_self", [P, S], F32)
    ma_self = sb("ma_self", [P, S], F32)
    m_cross = sb("m_cross", [P, 2, S], F32)
    ma_cross = sb("ma_cross", [P, 2, S], F32)
    ctok = sb("ctx_tokens", [P, D], F32)
    neghalf = sb("neghalf1", [P, 1], F32)

    SB = psum[:, 0:2]
    PB = psum[:, 2:4]
    QK, V, T = psum[:, 4], psum[:, 5], psum[:, 6]
    YO = psum[:, 7]

    s_w, s_const = sem("w1_loaded"), sem("const1_set")
    s_lnf, s_hi, s_lo = sem("ln_folded"), sem("w1_high"), sem("w1_low")
    s_b, s_bf = sem("bias_product"), sem("bias_folded")
    s_ctx, s_cm, s_ma = sem("ctx_tokens_loaded"), sem("cross_mask_loaded"), sem("cross_mask_term")
    s_tick = sem("wait_carrier1")
    W_LOADS = 5 + 4 + 3 + 2 + 2

    def columns(v):
        return v.rearrange("(m p) -> p m", p=P)

    def in_steps(eng, half):
        def step(i):
            half(SELF, f2=at(i, 0), b1=at(i, -1), f1=at(i, -2), sm=at(i, -3), b2=at(i, -4))
            half(CROSS, f2=at(i, -2), b1=at(i, -3), f1=at(i, 1), sm=at(i, 0), b2=at(i, -1))
        for i in range(-1, 5):
            step(i)
        with eng.Fori(5, NP - 1) as i:
            step(i)
        for i in range(NP - 1, NP + 4):
            step(i)

    def at(i, off):
        if isinstance(i, int) and not 0 <= i + off < NP:
            return None
        return i + off

    def before(a, p):
        n = p + 3 if a.cross else p - 2
        return n if not isinstance(n, int) else max(0, min(n, NP))

    def other(a):
        return SELF if a.cross else CROSS

    @block.sync
    def _(sp):
        for dst, src in ((wqkv_raw, w_qkv), (wao_raw, w_ao), (wcq_raw, w_q), (wkv_raw, w_kv), (wco_raw, w_co)):
            sp.dma_start(dst[:], src.rearrange("(k p) n -> p k n", p=P)).then_inc(s_w, 16)
        for n, (s_in, b_in) in enumerate(((ln1_s, ln1_b), (ln2_s, ln2_b))):
            sp.dma_start(lns[:, n], columns(s_in), allow_slow_non_contiguous=True).then_inc(s_w, 16)
            sp.dma_start(lnb[:, n], columns(b_in), allow_slow_non_contiguous=True).then_inc(s_w, 16)
        sp.dma_start(bias1[:], columns(b_qkv), allow_slow_non_contiguous=True).then_inc(s_w, 16)
        sp.dma_start(bias2[:, 0:G], columns(b_q), allow_slow_non_contiguous=True).then_inc(s_w, 16)
        sp.dma_start(bias2[:, G:3 * G], columns(b_kv), allow_slow_non_contiguous=True).then_inc(s_w, 16)
        for n, bias in enumerate((b_ao, b_co)):
            sp.dma_start(bias_out[:, n], bias.partition_broadcast(P)).then_inc(s_w, 16)
        for h2 in range(2):
            sp.dma_start(m_self[S * h2:S * h2 + S], self_mask[0, 0]).then_inc(s_w, 16)

        def load(p):
            wait(sp, CROSS.done["transposed"], p)
            sp.dma_start(ctok[:], ctx[bass.ds(p * 2, 2)].rearrange("n t f -> (n t) f")).then_inc(s_ctx, 16)
            wait(sp, CROSS.done["masked"], 2 * p)
            wait(sp, s_ma, p)
            for h2 in range(2):
                sp.dma_start(m_cross[S * h2:S * h2 + S],
                             cross_mask[bass.ds(p * 2, 2), 0].rearrange("n q k -> q n k")).then_inc(s_cm, 16)
        load(0)
        load(1)
        with sp.Fori(2, NP) as p:
            load(p)

    @block.gpsimd
    def _(pool):
        nc.gpsimd.memset(ident[:], 0.0).then_inc(s_const, 1)
        nc.gpsimd.memset(mask8[:], 1.0).then_inc(s_const, 1)
        nc.gpsimd.memset(neghalf[:], -0.5).then_inc(s_const, 1)
        for a in (SELF, CROSS):
            nc.gpsimd.memset(a.vz[:], 0.0).then_inc(s_const, 1)
        pool.wait_ge(s_const, 5)
        nc.gpsimd.affine_select(out=ident[:], in_=ident[:], compare_op=ALU.not_equal, fill=1.0, base=0,
                                pattern=[[-1, P]], channel_multiplier=1).then_inc(s_const, 1)
        nc.gpsimd.affine_select(out=mask8[:], in_=mask8[:], compare_op=ALU.is_ge, fill=0.0, base=0,
                                pattern=[[-HD, 8]], channel_multiplier=1).then_inc(s_const, 1)
        pool.wait_ge(s_const, 7)
        nc.gpsimd.affine_select(out=mask8[:], in_=mask8[:], compare_op=ALU.is_ge, fill=0.0, base=HD - 1,
                                pattern=[[HD, 8]], channel_multiplier=-1).then_inc(s_const, 1)
        pool.wait_ge(s_const, 8)
        pool.wait_ge(s_w, 16 * W_LOADS)
        nc.gpsimd.tensor_scalar(ma_self[:], m_self[:], 1e4, -1e4, ALU.mult, ALU.add).then_inc(s_const, 1)
        pool.wait_ge(s_const, 9)

        def half(a, f2, b1, f1, sm, b2):
            done, o = a.done, other(a)
            if sm is not None:
                for n in range(2):
                    pool.wait_ge(o.done["masked"], 2 * sm + n + 1)
                    if o.cross and n == 0:
                        pool.wait_ge(s_ma, sm + 1)
                    term = ma_cross[:, n] if o.cross else ma_self[:]
                    nc.gpsimd.tensor_tensor(o.t[:, n], o.t[:, n], bc(term, 1, 8), ALU.add
                                            ).then_inc(o.done["mask_added"], 1)
            if f1 is not None:
                pool.wait_ge(o.done["veps"], f1 + 1)
                wait(pool, o.done["xc"], f1)
                nc.gpsimd.tensor_tensor(o.rstd[:], o.veps[:], neghalf[:], ALU.pow).then_inc(o.done["rstd"], 1)
            if f2 is not None:
                pool.wait_ge(done["qs"], 2 * f2 + 2)
                wait(pool, done["s"], 2 * f2)
                for n in range(2):
                    q_n = bc(a.qs[:, 1, S * n:S * n + S], 1, 8)
                    nc.gpsimd.tensor_tensor(a.q8[:, 1, n], q_n, bc(mask8[:], 2, S), ALU.mult).then_inc(done["q8_g1"], 1)
                if a.cross:
                    pool.wait_ge(s_cm, 32 * (f2 + 1))
                    wait(pool, done["mask_added"], 2 * f2)
                    pool.sem_inc(s_tick, 1)
                    nc.gpsimd.tensor_scalar(ma_cross[:], m_cross[:], 1e4, -1e4, ALU.mult, ALU.add).then_inc(s_ma, 1)
            if b1 is not None:
                wait(pool, done["x"], b1)
                if a.cross:
                    pool.wait_ge(SELF.done["x"], b1 + 1)
                nc.gpsimd.tensor_tensor(a.xb[:], x1[:, b1], bias_out[:, 1 if a.cross else 0], ALU.add
                                        ).then_inc(done["xb"], 1)

        in_steps(pool, half)

    @block.scalar
    def _(act):
        act.wait_ge(s_lnf, 4)
        for src, hi in ((wqkv_raw, wqkv_hi), (wao_raw, wao_hi), (wcq_raw, wcq_hi), (wkv_raw, wkv_hi), (wco_raw, wco_hi)):
            nc.scalar.copy(hi[:], src[:]).then_inc(s_hi, 1)
        act.wait_ge(s_bf, 4)
        act.wait_ge(s_const, 9)

        def half(a, f2, b1, f1, sm, b2):
            done, o, bias = a.done, other(a), (bias2 if a.cross else bias1)
            if f2 is not None:
                act.wait_ge(done["qk"], f2 + 1)
                wait(act, done["q8_g0"], 2 * f2)
                wait(act, done["q8_g1"], 2 * f2)
                for g in range(G):
                    nc.scalar.activation(a.qs[:, g], QK[:, g * TOK:(g + 1) * TOK], ACT.Identity, bias=bias[:, g:g + 1],
                                         scale=SCALE1).then_inc(done["qs"], 1)
                wait(act, done["s"], 2 * f2)
                for g in range(G):
                    nc.scalar.activation(a.kT[:, g], QK[:, (G + g) * TOK:(G + g + 1) * TOK], ACT.Identity,
                                         bias=bias[:, G + g:G + g + 1]).then_inc(done["kT"], 1)
            if sm is not None:
                for n in range(2):
                    act.wait_ge(o.done["shifted"], 2 * sm + n + 1)
                    nc.scalar.activation(o.t[:, n], o.t[:, n], ACT.Exp).then_inc(o.done["exp"], 1)
            if b1 is not None:
                for n in range(2):
                    act.wait_ge(done["p_transposed"], 2 * b1 + n + 1)
                    if n == 0:
                        wait(act, done["y"], b1)
                    nc.scalar.copy(a.pT[:, 4 * n:4 * n + 4].rearrange("p a q -> p (a q)"), PB[:, n]).then_inc(done["pT"], 1)
            if f1 is not None:
                act.wait_ge(o.done["transposed"], f1 + 1)
                wait(act, o.done["v"], f1)
                nc.scalar.copy(o.hh[:], T[:, 0:o.hh.shape[1]]).then_inc(o.done["hh"], 1)
            if b1 is not None:
                act.wait_ge(done["y"], b1 + 1)
                wait(act, done["o"], b1)
                wait(act, done["yl"], 2 * b1)
                for g in range(G):
                    nc.scalar.activation(a.yh[:, g], YO[:, g * TOK:(g + 1) * TOK], ACT.Identity,
                                         bias=bias[:, 2 * G + g:2 * G + g + 1]).then_inc(done["yh"], 1)
            if f2 is not None:
                act.wait_ge(done["v"], f2 + 1)
                wait(act, done["y"], f2)
                for n in range(2):
                    for hp2 in range(2):
                        src = V[S * n:S * n + S, 0:D].rearrange("k (gj a h d) -> k gj a h d", a=2, h=2, d=HD)[:, :, hp2]
                        dst = a.vz[S * hp2:S * hp2 + S, n].rearrange("k h (gj a c d) -> k gj a c h d", a=2, c=2, d=HD)
                        for h2 in range(2):
                            nc.scalar.copy(dst[:, :, hp2, h2, h2], src[:, :, h2]).then_inc(done["vz"], 1)

        in_steps(act, half)

    @block.vector
    def _(dve):
        dve.wait_ge(s_w, 16 * W_LOADS)
        dve.wait_ge(s_b, 1)
        nc.vector.tensor_tensor(bias1[:], T[:, 0:3 * G], bias1[:], ALU.add).then_inc(s_bf, 1)
        nc.vector.tensor_tensor(bias2[:, 0:G], T[:, 16:16 + G], bias2[:, 0:G], ALU.add).then_inc(s_bf, 1)
        dve.wait_ge(s_bf, 2)
        nc.vector.tensor_scalar(bias1[:, 0:G], bias1[:, 0:G], SCALE1, None, ALU.mult).then_inc(s_bf, 1)
        nc.vector.tensor_scalar(bias2[:, 0:G], bias2[:, 0:G], SCALE1, None, ALU.mult).then_inc(s_bf, 1)
        for n, w in enumerate((wqkv_raw, wcq_raw)):
            for kt in range(G):
                nc.vector.tensor_scalar(w[:, kt], w[:, kt], lns[:, n, kt:kt + 1], None, ALU.mult).then_inc(s_lnf, 1)
        for n, (src, hi, lo) in enumerate(((wqkv_raw, wqkv_hi, wqkv_lo), (wao_raw, wao_hi, wao_lo),
                                           (wcq_raw, wcq_hi, wcq_lo), (wkv_raw, wkv_hi, wkv_lo),
                                           (wco_raw, wco_hi, wco_lo))):
            dve.wait_ge(s_hi, n + 1)
            nc.vector.tensor_tensor(lo[:], src[:], hi[:].bitcast(F32), ALU.subtract).then_inc(s_lo, 1)
        dve.wait_ge(s_const, 9)

        def half(a, f2, b1, f1, sm, b2):
            done, o, bias = a.done, other(a), (bias2 if a.cross else bias1)
            odone = o.done
            if f1 is not None:
                if o.cross:
                    dve.wait_ge(SELF.done["x"], f1 + 1)
                wait(dve, odone["mv"], f1)
                dve.sem_inc(s_tick, 1)
                nc.vector.bn_stats(o.bnst[:], x1[:, f1]).then_inc(odone["bnst"], 1)
                dve.wait_ge(odone["bnst"], f1 + 1)
                wait(dve, odone["xc"], f1)
                dve.sem_inc(s_tick, 1)
                nc.vector.bn_aggr(o.mv[:], o.bnst[:]).then_inc(odone["mv"], 1)
                dve.wait_ge(odone["mv"], f1 + 1)
                wait(dve, odone["rstd"], f1)
                nc.vector.tensor_scalar(o.veps[:], o.mv[:, 1:2], EPS, None, ALU.add).then_inc(odone["veps"], 1)
            if sm is not None:
                for n in range(2):
                    dve.wait_ge(odone["mask_added"], 2 * sm + n + 1)
                    wait(dve, odone["shifted"], 2 * sm)
                    nc.vector.tensor_reduce(out=o.nmax[:, n], in_=o.t[:, n], op=ALU.max, axis=AX.X, negate=True
                                            ).then_inc(odone["nmax"], 1)
                    dve.wait_ge(odone["nmax"], 2 * sm + n + 1)
                    nc.vector.tensor_tensor(o.t[:, n], o.t[:, n], bc(o.nmax[:, n], 2, S), ALU.add
                                            ).then_inc(odone["shifted"], 1)
            if f1 is not None:
                dve.wait_ge(odone["rstd"], f1 + 1)
                wait(dve, odone["transposed"], f1)
                nc.vector.tensor_scalar(o.xc[:], x1[:, f1], o.mv[:, 0:1], o.rstd[:], ALU.subtract, ALU.mult
                                        ).then_inc(odone["xc"], 1)
            if f2 is not None:
                dve.wait_ge(done["qs"], 2 * f2 + 1)
                wait(dve, done["s"], 2 * f2)
                for n in range(2):
                    q_n = bc(a.qs[:, 0, S * n:S * n + S], 1, 8)
                    nc.vector.tensor_tensor(a.q8[:, 0, n], q_n, bc(mask8[:], 2, S), ALU.mult).then_inc(done["q8_g0"], 1)
            if b2 is not None:
                dve.wait_ge(odone["o"], b2 + 1)
                dve.wait_ge(odone["xb"], b2 + 1)
                nc.vector.tensor_tensor(x1[:, b2], YO[:, D:2 * D], o.xb[:], ALU.add).then_inc(odone["x"], 1)
            if sm is not None:
                for n in range(2):
                    dve.wait_ge(odone["exp"], 2 * sm + n + 1)
                    wait(dve, odone["rden"], sm)
                    nc.vector.tensor_reduce(out=o.den[:, n], in_=o.t[:, n], op=ALU.add, axis=AX.X
                                            ).then_inc(odone["den"], 1)
                dve.wait_ge(odone["den"], 2 * sm + 2)
                wait(dve, odone["probs"], 2 * sm)
                nc.vector.reciprocal(o.rden[:], o.den[:]).then_inc(odone["rden"], 1)
                dve.wait_ge(odone["rden"], sm + 1)
                for n in range(2):
                    nc.vector.tensor_tensor(o.t[:, n], o.t[:, n], bc(o.rden[:, n], 2, S), ALU.mult
                                            ).then_inc(odone["probs"], 1)
            if f1 is not None:
                dve.wait_ge(odone["hh"], f1 + 1)
                wait(dve, odone["v"], f1)
                nc.vector.tensor_tensor(o.hl[:], T[:, 0:o.hl.shape[1]], o.hh[:].bitcast(F32), ALU.subtract
                                        ).then_inc(odone["hl"], 1)
            if b1 is not None:
                for g in range(G):
                    dve.wait_ge(done["yh"], 2 * b1 + 2)
                    wait(dve, done["o"], b1)
                    nc.vector.scalar_tensor_tensor(a.yl[:, g], YO[:, g * TOK:(g + 1) * TOK],
                                                   bias[:, 2 * G + g:2 * G + g + 1], a.yh[:, g].bitcast(F32),
                                                   ALU.add, ALU.subtract).then_inc(done["yl"], 1)
            if f2 is not None:
                wait(dve, done["p_transposed"], 2 * f2)
                for n in range(2):
                    dve.wait_ge(done["s"], 2 * f2 + n + 1)
                    if a.cross and n == 0:
                        dve.wait_ge(s_cm, 32 * (f2 + 1))
                    mask = m_cross[:, n] if a.cross else m_self[:]
                    nc.vector.tensor_tensor(a.t[:, n], SB[:, n].rearrange("p (h k) -> p h k", k=S), bc(mask, 1, 8),
                                            ALU.mult).then_inc(done["masked"], 1)

        in_steps(dve, half)

    @block.tensor
    def _(pe):
        mm = nc.tensor.matmul
        pe.wait_ge(s_w, 16 * W_LOADS)
        pe.wait_ge(s_const, 9)
        for m in range(3 * G):
            for kt in range(G):
                mm(T[:, m:m + 1], wqkv_raw[:, kt, m * P:(m + 1) * P], lnb[:, 0, kt:kt + 1], start=(kt == 0), stop=(kt == G - 1))
        for m in range(G):
            for kt in range(G):
                last = mm(T[:, 16 + m:17 + m], wcq_raw[:, kt, m * P:(m + 1) * P], lnb[:, 1, kt:kt + 1],
                          start=(kt == 0), stop=(kt == G - 1))
        last.then_inc(s_b, 1)
        pe.wait_ge(s_lo, 5)
        pe.wait_ge(s_bf, 4)

        def three(out, pairs):
            n = len(pairs)
            for k, ((lh, ll), (rh, rl)) in enumerate(pairs):
                mm(out, lh, rh, start=(k == 0), stop=False)
                mm(out, ll, rh, start=False, stop=False)
                last = mm(out, lh, rl, start=False, stop=(k == n - 1))
            return last

        def half(a, f2, b1, f1, sm, b2):
            done, o = a.done, other(a)
            if f2 is not None:
                pe.wait_ge(done["hl"], f2 + 1)
                wait(pe, o.done["kT"], 2 * before(a, f2))
                wait(pe, done["kT"], 2 * f2)
                for m in range(2 * G):
                    pairs = []
                    for kt in range(G):
                        src = D if a.cross and m >= G else 0
                        cols = slice(src + kt * TOK, src + (kt + 1) * TOK)
                        if not a.cross:
                            w = (wqkv_hi[:, kt, m * P:(m + 1) * P], wqkv_lo[:, kt, m * P:(m + 1) * P])
                        elif m < G:
                            w = (wcq_hi[:, kt, m * P:(m + 1) * P], wcq_lo[:, kt, m * P:(m + 1) * P])
                        else:
                            w = (wkv_hi[:, kt, (m - G) * P:(m - G + 1) * P], wkv_lo[:, kt, (m - G) * P:(m - G + 1) * P])
                        pairs.append((w, (a.hh[:, cols], a.hl[:, cols])))
                    last = three(QK[:, m * TOK:(m + 1) * TOK], pairs)
                last.then_inc(done["qk"], 1)
            if b2 is not None:
                pe.wait_ge(o.done["yl"], 2 * b2 + 2)
                hi, lo = (wco_hi, wco_lo) if o.cross else (wao_hi, wao_lo)
                pairs = [((o.yh[:, g], o.yl[:, g]), (hi[:, g], lo[:, g])) for g in range(G)]
                three(YO[:, D:2 * D], pairs).then_inc(o.done["o"], 1)
            if b1 is not None:
                wait(pe, o.done["pT"], 2 * before(a, b1))
                wait(pe, done["pT"], 2 * b1)
                for n in range(2):
                    pe.wait_ge(done["probs"], 2 * b1 + n + 1)
                    for k in range(4):
                        last = nc.tensor.transpose(PB[:, n, k * P:(k + 1) * P],
                                                   a.t[:, n, 2 * k:2 * k + 2].rearrange("p h k -> p (h k)"), ident[:])
                    last.then_inc(done["p_transposed"], 1)
            if f2 is not None:
                wait(pe, o.done["vz"], 8 * before(a, f2))
                wait(pe, done["vz"], 8 * f2)
                pairs = []
                for kt in range(G):
                    src = D if a.cross else 0
                    cols = slice(src + kt * TOK, src + (kt + 1) * TOK)
                    w = (wkv_hi[:, kt, D:2 * D], wkv_lo[:, kt, D:2 * D]) if a.cross else \
                        (wqkv_hi[:, kt, 2 * D:3 * D], wqkv_lo[:, kt, 2 * D:3 * D])
                    pairs.append(((a.hh[:, cols], a.hl[:, cols]), w))
                three(V[:, 0:D], pairs).then_inc(done["v"], 1)
            if f1 is not None:
                wait(pe, done["hl"], before(o, f1))
                wait(pe, o.done["hl"], f1)
                if o.cross:
                    pe.wait_ge(s_ctx, 16 * (f1 + 1))
                    for kt in range(G):
                        nc.tensor.transpose(T[:, D + kt * TOK:D + (kt + 1) * TOK], ctok[:, kt * P:(kt + 1) * P], ident[:])
                pe.wait_ge(o.done["xc"], f1 + 1)
                for kt in range(G):
                    last = nc.tensor.transpose(T[:, kt * TOK:(kt + 1) * TOK], o.xc[:, kt * P:(kt + 1) * P], ident[:])
                last.then_inc(o.done["transposed"], 1)
            if b1 is not None:
                pe.wait_ge(done["pT"], 2 * b1 + 2)
                pe.wait_ge(done["vz"], 8 * b1 + 8)
                wait(pe, o.done["x"], before(a, b1))
                wait(pe, done["x"], b1)
                for n in range(2):
                    for g in range(G):
                        for jj in range(2):
                            for h2 in range(2):
                                at_f = g * P + jj * S
                                last = mm(YO[S * jj:S * jj + S, g * TOK + n * S:g * TOK + (n + 1) * S],
                                          a.vz[:, n, h2, at_f:at_f + S], a.pT[:, 4 * n + 2 * g + jj, h2 * S:(h2 + 1) * S],
                                          start=(h2 == 0), stop=(h2 == 1))
                last.then_inc(done["y"], 1)
            if f2 is not None:
                pe.wait_ge(done["kT"], 2 * f2 + 2)
                wait(pe, o.done["masked"], 2 * before(a, f2))
                wait(pe, done["masked"], 2 * f2)
                for g in range(G):
                    for n in range(2):
                        pe.wait_ge(done["q8_g1" if g else "q8_g0"], 2 * f2 + n + 1)
                        for r in range(4):
                            hp = 4 * g + r
                            last = mm(SB[:, n, hp * S:(hp + 1) * S],
                                      a.q8[:, g, n, 2 * r:2 * r + 2].rearrange("p h q -> p (h q)"),
                                      a.kT[:, g, n * S:(n + 1) * S], start=True, stop=True)
                        if g == G - 1:
                            last.then_inc(done["s"], 1)

        in_steps(pe, half)


def layer1_mlp(nc, sb, psum, sem, block, ln3_s, ln3_b, w1, b1, w2, b2, x1, out):
    NG, GT = NP // 2, 2 * TOK
    M = FF // P
    w1_raw, w1_hi, w1_lo = split_weight(nc, sb, "w1", [P, G, FF])
    w2_raw, w2_hi, w2_lo = split_weight(nc, sb, "w2", [P, M, D])
    lns = sb("ln3_scale", [P, G], F32)
    lnb = sb("ln3_bias", [P, G], F32)
    bias1 = sb("bias_hidden", [P, M], F32)
    bias2 = sb("bias_mlp", [P, D], F32)
    ident = sb("ident2", [P, P], F32)
    neghalf = sb("neghalf2", [P, 2], F32)
    bnst = sb("mlp_bnst", [P, 2, 6], F32)
    mv = sb("mlp_mv", [P, 2, 2], F32)
    veps = sb("mlp_veps", [P, 2], F32)
    rstd = sb("mlp_rstd", [P, 2], F32)
    xc = sb("mlp_xc", [P, 2, D], F32)
    xb = sb("mlp_xb", [P, 2, D], F32)
    hh = sb("mlp_hh", [P, G, GT], F32R)
    hl = sb("mlp_hl", [P, G, GT], F32R)
    gf = sb("mlp_gelu", [P, M, GT], F32)
    gh = sb("mlp_gelu_high", [P, 2, M, GT], F32R)
    gl = sb("mlp_gelu_low", [P, 2, M, GT], F32R)
    res = sb("mlp_result", [P, 2, 2, D], F32)

    H = psum[:, 0:4]
    T, O = psum[:, 4], psum[:, 5]

    s_w, s_const = sem("w2_loaded"), sem("const2_set")
    s_b, s_bf, s_lnf, s_hi, s_lo = (sem("bias1_product"), sem("bias1_folded"), sem("ln3_folded"), sem("w2_high"),
                                    sem("w2_low"))
    s_bn, s_mv, s_veps, s_rstd, s_xc = (sem("mlp_bn"), sem("mlp_mean_var"), sem("mlp_var_eps"), sem("mlp_rstd_done"),
                                        sem("mlp_centred"))
    s_t, s_hh, s_hl, s_h, s_g = (sem("mlp_transposed"), sem("mlp_high"), sem("mlp_low"), sem("mlp_hidden"),
                                 sem("mlp_gelu_done"))
    s_gh, s_gl, s_xb, s_o, s_res, s_tick = (sem("gelu_high"), sem("gelu_low"), sem("mlp_residual"), sem("mlp_out"),
                                            sem("mlp_summed"), sem("wait_carrier2"))
    s_out = [sem("stored0"), sem("stored1")]
    W_LOADS = 6

    @block.sync
    def _(sp):
        sp.dma_start(w1_raw[:], w1.rearrange("(k p) n -> p k n", p=P)).then_inc(s_w, 16)
        sp.dma_start(w2_raw[:], w2.rearrange("(k p) n -> p k n", p=P)).then_inc(s_w, 16)
        for dst, src in ((lns, ln3_s), (lnb, ln3_b), (bias1, b1)):
            sp.dma_start(dst[:], src.rearrange("(m p) -> p m", p=P), allow_slow_non_contiguous=True).then_inc(s_w, 16)
        sp.dma_start(bias2[:], b2.partition_broadcast(P)).then_inc(s_w, 16)

        def step(q):
            if exists(q, 0, NG):
                sp.wait_ge(s_res, q.idx + 1)
                sp.dma_start(out[bass.ds(q.idx * 4, 4)].rearrange("(i n) c s -> (n c) i s", n=2), res[:, q.par]
                             ).then_inc(s_out[q.par], 16)
        run_steps(sp, step, 0, NG - 1, 2, 5)
        for par in range(2):
            sp.wait_ge(s_out[par], 16 * NG // 2)

    @block.gpsimd
    def _(pool):
        nc.gpsimd.memset(ident[:], 0.0).then_inc(s_const, 1)
        nc.gpsimd.memset(neghalf[:], -0.5).then_inc(s_const, 1)
        pool.wait_ge(s_const, 2)
        nc.gpsimd.affine_select(out=ident[:], in_=ident[:], compare_op=ALU.not_equal, fill=1.0, base=0,
                                pattern=[[-1, P]], channel_multiplier=1).then_inc(s_const, 1)
        pool.wait_ge(s_w, 16 * W_LOADS)

        def step(q):
            if exists(q, 2, NG):
                n = q.next(2)
                pool.wait_ge(s_veps, n.idx + 1)
                wait(pool, s_xc, 2 * n.idx)
                nc.gpsimd.tensor_tensor(rstd[:], veps[:], neghalf[:], ALU.pow).then_inc(s_rstd, 1)
            if exists(q, 0, NG):
                wait(pool, s_res, q.idx)
                nc.gpsimd.tensor_tensor(xb[:], x1[:, bass.ds(q.idx * 2, 2)], bc(bias2[:], 1, 2), ALU.add).then_inc(s_xb, 1)

        step(Pair(-2, 0, -1))
        step(Pair(-1, 1, -1))
        run_steps(pool, step, 0, NG - 1, 2, 5)

    @block.scalar
    def _(act):
        act.wait_ge(s_lnf, G)
        nc.scalar.copy(w1_hi[:], w1_raw[:]).then_inc(s_hi, 1)
        nc.scalar.copy(w2_hi[:], w2_raw[:]).then_inc(s_hi, 1)
        act.wait_ge(s_bf, 1)

        def step(q):
            if exists(q, 1, NG):
                n = q.next()
                for m in range(M):
                    if m % 2 == 0:
                        act.wait_ge(s_h, 4 * n.idx + m // 2 + 1)
                    if m == 0:
                        wait(act, s_gl, 4 * n.idx)
                    nc.scalar.activation(gf[:, m], H[:, m // 2, m % 2 * GT:(m % 2 + 1) * GT], ACT.Gelu_apprx_tanh,
                                         bias=bias1[:, m:m + 1]).then_inc(s_g, 1)
                    if m % 2 == 1:
                        act.wait_ge(s_g, 8 * n.idx + m + 1)
                        wait(act, s_o, 2 * (n.idx - 1))
                        nc.scalar.copy(gh[:, n.par, m - 1:m + 1], gf[:, m - 1:m + 1]).then_inc(s_gh, 1)
            if exists(q, 2, NG):
                n = q.next(2)
                act.wait_ge(s_t, n.idx + 1)
                wait(act, s_h, 4 * n.idx)
                nc.scalar.copy(hh[:].rearrange("p k t -> p (k t)"), T).then_inc(s_hh, 1)

        step(Pair(-2, 0, -1))
        step(Pair(-1, 1, -1))
        run_steps(act, step, 0, NG - 1, 2, 5)

    @block.vector
    def _(dve):
        dve.wait_ge(s_w, 16 * W_LOADS)
        dve.wait_ge(s_b, 1)
        nc.vector.tensor_tensor(bias1[:], T[:, 0:M], bias1[:], ALU.add).then_inc(s_bf, 1)
        for kt in range(G):
            nc.vector.tensor_scalar(w1_raw[:, kt], w1_raw[:, kt], lns[:, kt:kt + 1], None, ALU.mult).then_inc(s_lnf, 1)
        for n, (src, hi, lo) in enumerate(((w1_raw, w1_hi, w1_lo), (w2_raw, w2_hi, w2_lo))):
            dve.wait_ge(s_hi, n + 1)
            nc.vector.tensor_tensor(lo[:], src[:], hi[:].bitcast(F32), ALU.subtract).then_inc(s_lo, 1)

        def norm(n):
            wait(dve, s_mv, 2 * n.idx)
            dve.sem_inc(s_tick, 1)
            for k in range(2):
                nc.vector.bn_stats(bnst[:, k], x1[:, n.idx * 2 + k]).then_inc(s_bn, 1)
            dve.wait_ge(s_bn, 2 * n.idx + 2)
            wait(dve, s_xc, 2 * n.idx)
            dve.sem_inc(s_tick, 1)
            for k in range(2):
                nc.vector.bn_aggr(mv[:, k], bnst[:, k]).then_inc(s_mv, 1)
            dve.wait_ge(s_mv, 2 * n.idx + 2)
            wait(dve, s_rstd, n.idx)
            nc.vector.tensor_scalar(veps[:], mv[:, :, 1], EPS, None, ALU.add).then_inc(s_veps, 1)

        def step(q):
            if exists(q, 2, NG):
                norm(q.next(2))
            if exists(q, 1, NG):
                n = q.next()
                for k in range(4):
                    dve.wait_ge(s_gh, 4 * n.idx + k + 1)
                    wait(dve, s_o, 2 * (n.idx - 1))
                    nc.vector.tensor_tensor(gl[:, n.par, 2 * k:2 * k + 2], gf[:, 2 * k:2 * k + 2],
                                            gh[:, n.par, 2 * k:2 * k + 2].bitcast(F32), ALU.subtract).then_inc(s_gl, 1)
                    if k == 0 and exists(q, 2, NG):
                        centre(q.next(2))
            elif exists(q, 2, NG):
                centre(q.next(2))
            if exists(q, 2, NG):
                n = q.next(2)
                dve.wait_ge(s_hh, n.idx + 1)
                wait(dve, s_h, 4 * n.idx)
                nc.vector.tensor_tensor(hl[:].rearrange("p k t -> p (k t)"), T,
                                        hh[:].rearrange("p k t -> p (k t)").bitcast(F32), ALU.subtract).then_inc(s_hl, 1)
            if exists(q, 0, NG):
                dve.wait_ge(s_o, 2 * q.idx + 2)
                dve.wait_ge(s_xb, q.idx + 1)
                wait(dve, s_out[q.par], 16 * q.before)
                nc.vector.tensor_tensor(res[:, q.par].rearrange("p i s -> p (i s)"), O,
                                        xb[:].rearrange("p i s -> p (i s)"), ALU.add).then_inc(s_res, 1)

        def centre(n):
            dve.wait_ge(s_rstd, n.idx + 1)
            wait(dve, s_t, n.idx)
            for k in range(2):
                nc.vector.tensor_scalar(xc[:, k], x1[:, n.idx * 2 + k], mv[:, k, 0:1], rstd[:, k:k + 1], ALU.subtract,
                                        ALU.mult).then_inc(s_xc, 1)

        step(Pair(-2, 0, -1))
        step(Pair(-1, 1, -1))
        run_steps(dve, step, 0, NG - 1, 2, 5)

    @block.tensor
    def _(pe):
        mm = nc.tensor.matmul
        pe.wait_ge(s_w, 16 * W_LOADS)
        for m in range(M):
            for kt in range(G):
                last = mm(T[:, m:m + 1], w1_raw[:, kt, m * P:(m + 1) * P], lnb[:, kt:kt + 1], start=(kt == 0), stop=(kt == G - 1))
        last.then_inc(s_b, 1)
        pe.wait_ge(s_const, 3)
        pe.wait_ge(s_bf, 1)

        def step(q):
            if exists(q, 1, NG):
                n = q.next()
                if isinstance(n.idx, int) and n.idx == 0:
                    pe.wait_ge(s_lo, 2)
                pe.wait_ge(s_hl, n.idx + 1)
                for m in range(M):
                    if m % 2 == 0:
                        wait(pe, s_g, 8 * (n.idx - 1) + m + 2)
                    o = H[:, m // 2, m % 2 * GT:(m % 2 + 1) * GT]
                    for kt in range(G):
                        hi, lo = w1_hi[:, kt, m * P:(m + 1) * P], w1_lo[:, kt, m * P:(m + 1) * P]
                        mm(o, hi, hh[:, kt], start=(kt == 0), stop=False)
                        mm(o, lo, hh[:, kt], start=False, stop=False)
                        last = mm(o, hi, hl[:, kt], start=False, stop=(kt == G - 1))
                    if m % 2 == 1:
                        last.then_inc(s_h, 1)
            if exists(q, 2, NG):
                n = q.next(2)
                pe.wait_ge(s_xc, 2 * n.idx + 2)
                wait(pe, s_hl, n.idx)
                for k in range(2):
                    for kt in range(G):
                        last = nc.tensor.transpose(T[:, kt * GT + k * TOK:kt * GT + (k + 1) * TOK],
                                                   xc[:, k, kt * P:(kt + 1) * P], ident[:])
                last.then_inc(s_t, 1)
            if exists(q, 0, NG):
                pe.wait_ge(s_gl, 4 * q.idx + 4)
                wait(pe, s_res, q.idx)
                for k in range(2):
                    o = O[:, k * D:(k + 1) * D]
                    tok = slice(k * TOK, (k + 1) * TOK)
                    for m in range(M):
                        mm(o, gh[:, q.par, m, tok], w2_hi[:, m], start=(m == 0), stop=False)
                        mm(o, gh[:, q.par, m, tok], w2_lo[:, m], start=False, stop=False)
                        last = mm(o, gl[:, q.par, m, tok], w2_hi[:, m], start=False, stop=(m == M - 1))
                    last.then_inc(s_o, 1)

        step(Pair(-2, 0, -1))
        step(Pair(-1, 1, -1))
        run_steps(pe, step, 0, NG - 1, 2, 5)


def decoder(nc, x, ctx_2048, mask_1x1xSxS2_fc1, mask_Bx1xSxS2_ff1, L0_gamma, L0_beta, L0_Wq, L0_bq, L0_Wkv, L0_bkv,
            L0_Wo, L0_bo, ln1_s, ln1_b, w_qkv, b_qkv, w_ao, b_ao, ln2_s, ln2_b, w_q, b_q, w_kv, b_kv, w_co, b_co,
            ln3_s, ln3_b, w1, b1, w2, b2, out):
    with ExitStack() as kept:
        def enter(stack, make, *args):
            return stack.enter_context(make(*args))

        psum = enter(kept, nc.psum_tensor, "banks", [P, 8, 512], F32)
        x1 = enter(kept, nc.sbuf_tensor, "tokens", [P, NP, D], F32)

        def phase(build, *args):
            with ExitStack() as stack:
                def sb(name, shape, dt):
                    return enter(stack, nc.sbuf_tensor, name, shape, dt)

                def sem(name):
                    return enter(stack, nc.semaphore, name)
                with nc.Block() as block:
                    build(nc, sb, psum, sem, block, *args)

        phase(layer0, x, ctx_2048, L0_gamma, L0_beta, L0_Wq, L0_bq, L0_Wkv, L0_bkv, L0_Wo, L0_bo, x1)
        phase(layer1_attentions, ctx_2048, mask_1x1xSxS2_fc1, mask_Bx1xSxS2_ff1, ln1_s, ln1_b, w_qkv, b_qkv, w_ao,
              b_ao, ln2_s, ln2_b, w_q, b_q, w_kv, b_kv, w_co, b_co, x1)
        phase(layer1_mlp, ln3_s, ln3_b, w1, b1, w2, b2, x1, out)


_INS = ["x", "ctx_2048", "mask_1x1xSxS2_fc1", "mask_Bx1xSxS2_ff1", "L0_xattn_gamma", "L0_xattn_beta", "L0_xattn_Wq",
        "L0_xattn_bq", "L0_xattn_Wkv", "L0_xattn_bkv", "L0_xattn_Wo", "L0_xattn_bo"] + [
        "L1_xattn_" + k for k in ("ln1_s", "ln1_b", "w_qkv", "b_qkv", "w_ao", "b_ao", "ln2_s", "ln2_b", "w_q", "b_q",
                                  "w_kv", "b_kv", "w_co", "b_co", "ln3_s", "ln3_b", "w1", "b1", "w2", "b2")]


def kernel(**inputs):
    import numpy as _np
    import concourse.bacc as _bacc
    from concourse import mybir as _mybir
    from concourse.bass_utils import run_bass_kernel_spmd as _run

    nc = _bacc.Bacc("TRN2", target_bir_lowering=False, num_devices=1)
    arrays, args = {}, []
    for name in _INS:
        a = _np.ascontiguousarray(inputs[name])
        arrays[f"in_{name}"] = a
        args.append(nc.dram_tensor(f"in_{name}", a.shape, _mybir.dt.from_np(a.dtype), kind="ExternalInput").ap())
    args.append(nc.dram_tensor("out", (B, S, D), F32, kind="ExternalOutput").ap())
    decoder(nc, *args)
    r = _run(nc, [arrays], core_ids=[0])
    return r.results[0]["out"]
```

```python
from contextlib import ExitStack

import concourse.bass as bass
from concourse import mybir

F32 = mybir.dt.float32
F32R = mybir.dt.float32r
ALU = mybir.AluOpType
ACT = mybir.ActivationFunctionType
AX = mybir.AxisListType

P = 128
B, S, D = 32, 64, 256
NP = B // 2
H0, C0 = 8, 64
QT, KT = D // P, D // P
SCALE0 = float(C0) ** -0.5
EPS = 1e-5


class Pair:

    def __init__(self, idx, par, before):
        self.idx, self.par, self.before = idx, par, before

    def next(self, n=1):
        off = self.par + n
        return Pair(self.idx + n, off % 2, self.before + off // 2)


def run_steps(eng, step, first, last, loop_first, loop_last):
    idx = first
    while idx <= last:
        if idx == loop_first:
            turns = (loop_last + 1 - loop_first) // 2
            with eng.Fori(0, turns) as t:
                step(Pair(t * 2 + loop_first, 0, t + loop_first // 2))
                step(Pair(t * 2 + loop_first + 1, 1, t + loop_first // 2))
            idx += 2 * turns
        else:
            step(Pair(idx, idx % 2, idx // 2))
            idx += 1


def exists(pair, off, count=NP):
    return not isinstance(pair.idx, int) or 0 <= pair.idx + off < count


def wait(eng, sem, value):
    if not isinstance(value, int) or value > 0:
        eng.wait_ge(sem, value)


def bc(ap, dim, n):
    shape = list(ap.shape)
    return ap.unsqueeze(dim).broadcast_to(shape[:dim] + [n] + shape[dim:])


def layer0(nc, sb, psum, sem, block, x, ctx, gamma, beta, Wq, bq, Wkv, bkv, Wo, bo, x1, w_att):
    wq2 = sb("wq2", [C0, H0, 2, C0], F32)
    wk2 = sb("wk2", [C0, H0, 2, C0], F32)
    wv2 = sb("wv2", [C0, H0, 2, C0], F32)
    wo_nat = sb("wo_nat", [C0, H0 * C0], F32)
    wo2 = sb("wo2", [C0, H0, 2, C0], F32)
    bq_sb = sb("bq_sb", [C0, H0], F32)
    bv_sb = sb("bv_sb", [C0, H0], F32)
    gamma2 = sb("gamma2", [P, 1], F32)
    beta2 = sb("beta2", [P, 1], F32)
    bo2 = sb("bo2", [P, 1], F32)
    a_st = sb("a_st", [P, H0, P], F32R)
    qbias = sb("qbias", [P, H0], F32)
    wvo_hi = sb("wvo_hi", [P, H0 * C0], F32R)
    wvo_lo = sb("wvo_lo", [P, H0 * C0], F32R)
    obias = sb("obias", [P, 1], F32)
    ident = sb("ident", [P, P], F32)
    mean64 = sb("mean64", [C0, P], F32)
    neghalf = sb("neghalf", [P, 2], F32)
    xd = sb("xd", [P, 2, 2, D], F32)
    cd = sb("cd", [P, 2, 2, D], F32)
    xp = sb("xp", [P, 2, D], F32)
    bnst = sb("bnst", [P, 2, 6], F32)
    mv = sb("mv", [P, 2, 2], F32)
    mvm = sb("mvm", [P, 2, 2], F32)
    dev = sb("dev", [P, 2], F32)
    dev2 = sb("dev2", [P, 2], F32)
    veps = sb("veps", [P, 2], F32)
    rstd = sb("rstd", [P, 2], F32)
    s1 = sb("s1", [P, 2], F32)
    ms1 = sb("ms1", [P, 2], F32)
    s2 = sb("s2", [P, 2], F32)
    xh = sb("xh", [P, 2, 2, D], F32R)
    xn = sb("xn", [P, 2, D], F32)
    xl = sb("xl", [P, 2, 2, D], F32R)
    cs = sb("cs", [P, 2, 2, D], F32R)
    c1 = sb("c1", [P, 2, 2, D], F32R)
    qh = sb("qh", [P, 2, H0, 2, D], F32R)
    ql = sb("ql", [P, 2, 2, H0, D], F32R)
    vw = sb("vw", [P, 2, 2, KT, H0, C0 + 1], F32)
    pt = sb("pt", [P, 2, KT, D], F32)
    nmax = sb("nmax", [P, 2, H0, QT], F32)
    nmaxt = sb("nmaxt", [H0 * QT, 2, P], F32R)
    rden = sb("rden", [P, 2, 2, QT], F32)
    yn = sb("yn", [P, 2, 4, 2, QT, C0], F32)
    ysum = sb("ysum", [P, 2, 4, QT, C0], F32)
    ot = sb("ot", [P, 2, QT, 2, C0], F32)

    T = [psum[:, 0], psum[:, 1]]
    M = [psum[:, 2], psum[:, 3]]
    J = [psum[:, 4], psum[:, 5]]
    Y = [psum[:, 6], psum[:, 7]]

    STATS = 2 * QT * (C0 + 1)

    MAX_UNITS = [[], [], [0], [1], [2], [3], [4], [5], [6], [7, 8], [9], [10], [11], [12], [13], [14, 15]]

    s_zeros = sem("zeros_set")
    s_wqk, s_w, s_const, s_ones = sem("wq_wk_loaded"), sem("w_loaded"), sem("const_set"), sem("ones_set")
    s_wot, s_wot_ev = sem("wo_transposed"), sem("wo_copied")
    s_fold, s_fold_ev, s_fold_lo = sem("folded"), sem("fold_high"), sem("fold_low")
    s_x = [sem("x_loaded0"), sem("x_loaded1")]
    s_c = [sem("ctx_loaded0"), sem("ctx_loaded1")]
    s_xp = [sem("xres_loaded0"), sem("xres_loaded1")]
    s_bn, s_mv, s_st = sem("bn_done"), sem("row_stats"), sem("sample_stats")
    s_dev, s_dev2, s_veps = sem("dev_done"), sem("dev2_done"), sem("var_eps")
    s_aff, s_xh, s_xn, s_xl = sem("affine"), sem("x_high"), sem("x_norm"), sem("x_low")
    s_cs, s_c1, s_csl = sem("ctx_high"), sem("ctx_high_ones"), sem("ctx_low")
    s_q, s_qh, s_ql = sem("q_projected"), sem("q_high"), sem("q_low")
    s_s, s_max = sem("scores_for_max"), sem("max_taken")
    s_mt, s_mtc, s_row = sem("max_transposed"), sem("max_rounded"), [sem("max_row0"), sem("max_row1")]
    s_v, s_vw = sem("v_projected"), sem("v_copied")
    s_t, s_exp, s_pv = sem("scores"), sem("probs"), sem("weighted")
    s_rden, s_yn, s_ysum = sem("denominators"), sem("normalised"), sem("heads_summed")
    s_tick = sem("wait_carrier")
    s_ot, s_x1 = sem("out_transposed"), sem("x1_ready")

    @block.sync
    def _(sp):
        for copy in range(2):
            sp.dma_start(wq2[:, :, copy], Wq.rearrange("(h o) c -> o h c", o=C0)).then_inc(s_wqk, 16)
            sp.dma_start(wk2[:, :, copy], Wkv[0:H0 * C0].rearrange("(h o) c -> o h c", o=C0)).then_inc(s_wqk, 16)
        sp.dma_start(bq_sb[:], bq.rearrange("(h o) -> o h", o=C0), allow_slow_non_contiguous=True).then_inc(s_wqk, 16)

        def load(p):
            for copy in range(2):
                half = slice(64 * copy, 64 * copy + 64)
                sp.dma_start(xd[half, p.par], x[bass.ds(p.idx * 2, 2)].rearrange("n c s -> c n s")
                             ).then_inc(s_x[p.par], 16)
            for copy in range(2):
                half = slice(64 * copy, 64 * copy + 64)
                sp.dma_start(cd[half, p.par], ctx[bass.ds(p.idx * 2, 2)].rearrange("n c s -> c n s")
                             ).then_inc(s_c[p.par], 16)

        def max_row(p, n):
            sp.wait_ge(s_mtc, p.idx * 2 + n + 1)
            sp.dma_start(ql[C0:C0 + 1, p.par, n].rearrange("a h (t q) -> a (h t) q", t=QT).bitcast(F32),
                         nmaxt[:, n].bitcast(F32)).then_inc(s_row[n], 16)

        def step(p):
            if exists(p, 0):
                max_row(p, 1)
                wait(sp, s_x1, p.idx - 1)
                sp.dma_start(xp[:, p.par], x[bass.ds(p.idx * 2, 2)].rearrange("n c s -> (n c) s")
                             ).then_inc(s_xp[p.par], 16)
            if exists(p, 3):
                p3 = p.next(3)
                wait(sp, s_xh, 2 * (p3.idx - 1))
                wait(sp, s_xl, p3.idx - 1)
                wait(sp, s_csl, p3.idx - 1)
                wait(sp, s_c1, p3.idx - 1)
                load(p3)
            if exists(p, 1):
                max_row(p.next(), 0)

        load(Pair(0, 0, 0))
        sp.dma_start(wo_nat[:], Wo).then_inc(s_w, 16)
        for copy in range(2):
            sp.dma_start(wv2[:, :, copy], Wkv[H0 * C0:].rearrange("(h o) c -> o h c", o=C0)).then_inc(s_w, 16)
            half = slice(64 * copy, 64 * copy + 64)
            sp.dma_start(gamma2[half], gamma.rearrange("(c a) -> c a", a=1)).then_inc(s_w, 16)
            sp.dma_start(beta2[half], beta.rearrange("(c a) -> c a", a=1)).then_inc(s_w, 16)
            sp.dma_start(bo2[half], bo.rearrange("(c a) -> c a", a=1)).then_inc(s_w, 16)
        sp.dma_start(bv_sb[:], bkv[H0 * C0:].rearrange("(h o) -> o h", o=C0), allow_slow_non_contiguous=True).then_inc(s_w, 16)
        load(Pair(1, 1, 0))
        sp.wait_ge(s_zeros, 1)
        sp.wait_ge(s_ones, 3)
        w_att.load(sp)
        step(Pair(-1, 1, -1))
        run_steps(sp, step, 0, NP - 1, 2, NP - 5)

    @block.gpsimd
    def _(pool):
        nc.gpsimd.memset(ident[:], 0.0).then_inc(s_const, 1)
        nc.gpsimd.memset(mean64[:], 1.0 / C0).then_inc(s_const, 1)
        nc.gpsimd.memset(neghalf[:], -0.5).then_inc(s_const, 1)
        nc.gpsimd.memset(vw[:, :, :, :, :, C0:C0 + 1], 1.0).then_inc(s_const, 1)
        pool.wait_ge(s_const, 1)
        nc.gpsimd.affine_select(out=ident[:], in_=ident[:], compare_op=ALU.not_equal, fill=1.0, base=0,
                                pattern=[[-1, P]], channel_multiplier=1).then_inc(s_const, 1)
        pool.wait_ge(s_const, 5)
        nc.gpsimd.memset(ql[C0:P, 0].bitcast(F32), 0.0).then_inc(s_zeros, 1)
        pool.wait_ge(s_zeros, 1)
        pool.wait_ge(s_w, 16 * 10)

        def prepare_x(p):
            pool.wait_ge(s_veps, p.idx + 1)
            wait(pool, s_xh, 2 * p.idx)
            wait(pool, s_xn, 2 * p.idx)
            wait(pool, s_xl, p.idx)
            nc.gpsimd.tensor_tensor(rstd[:], veps[:], neghalf[:], ALU.pow).then_inc(s_aff, 1)
            pool.wait_ge(s_aff, 4 * p.idx + 1)
            nc.gpsimd.tensor_tensor(s1[:], rstd[:], gamma2[:].broadcast_to([P, 2]), ALU.mult).then_inc(s_aff, 1)
            pool.wait_ge(s_aff, 4 * p.idx + 2)
            nc.gpsimd.tensor_tensor(ms1[:], s1[:], mvm[:, :, 0], ALU.mult).then_inc(s_aff, 1)
            pool.wait_ge(s_aff, 4 * p.idx + 3)
            nc.gpsimd.tensor_tensor(s2[:], beta2[:].broadcast_to([P, 2]), ms1[:], ALU.subtract).then_inc(s_aff, 1)
            pool.wait_ge(s_aff, 4 * p.idx + 4)
            pool.sem_inc(s_tick, 1)
            for n in range(2):
                nc.gpsimd.tensor_scalar(xn[:, n], xd[:, p.par, n], s1[:, n:n + 1], s2[:, n:n + 1],
                                        ALU.mult, ALU.add).then_inc(s_xn, 1)
            pool.wait_ge(s_xn, 2 * p.idx + 2)
            pool.wait_ge(s_xh, 2 * p.idx + 2)
            wait(pool, s_q, H0 * (p.idx - 1))
            nc.gpsimd.tensor_tensor(xl[:, p.par], xn[:], xh[:, p.par].bitcast(F32), ALU.subtract).then_inc(s_xl, 1)

        def prepare_context(p):
            pool.wait_ge(s_xl, p.idx + 1)
            pool.wait_ge(s_cs, p.idx + 1)
            nc.gpsimd.tensor_tensor(cs[C0:P, p.par], cd[C0:P, p.par], cs[C0:P, p.par].bitcast(F32),
                                    ALU.subtract).then_inc(s_csl, 1)

        def sum_heads(p, n):
            pool.wait_ge(s_yn, 8 * p.idx + 4 * n + 4)
            c = 6 * p.idx + 3 * n
            yv = yn[:, n].rearrange("p a b t c -> p (a b) t c")
            a = ysum[:, n]
            wait(pool, s_ysum, c)
            nc.gpsimd.tensor_tensor(a, yv[:, 0:4], yv[:, 4:8], ALU.add).then_inc(s_ysum, 1)
            pool.wait_ge(s_ysum, c + 1)
            nc.gpsimd.tensor_tensor(a[:, 0:2], a[:, 0:2], a[:, 2:4], ALU.add).then_inc(s_ysum, 1)
            pool.wait_ge(s_ysum, c + 2)
            wait(pool, s_ot, p.idx - 1)
            nc.gpsimd.tensor_tensor(ot[:, p.par, :, n], a[:, 0], a[:, 1], ALU.add).then_inc(s_ysum, 1)

        def step(p):
            if exists(p, 1):
                prepare_context(p.next())
                pool.wait_ge(s_csl, p.idx + 2)
            if exists(p, -1):
                sum_heads(p.next(-1), 1)
            if exists(p, 0):
                sum_heads(p, 0)
            if exists(p, 2):
                prepare_x(p.next(2))

        step(Pair(-2, 0, -1))
        step(Pair(-1, 1, -1))
        run_steps(pool, step, 0, NP - 1, 4, NP - 3)
        sum_heads(Pair(NP - 1, (NP - 1) % 2, (NP - 1) // 2), 1)

    @block.scalar
    def _(act):
        act.wait_ge(s_fold, 1)
        for b in range(2):
            nc.scalar.activation(a_st[:, 4 * b:4 * b + 4], T[b].rearrange("p (h c) -> p h c", c=P), ACT.Copy,
                                 scale=SCALE0).then_inc(s_fold_ev, 1)
        nc.scalar.activation(qbias[:], M[1][:, 0:H0], ACT.Copy, scale=SCALE0).then_inc(s_fold_ev, 1)

        def prepare_x(p):
            act.wait_ge(s_aff, 4 * p.idx + 4)
            wait(act, s_q, H0 * (p.idx - 1))
            for n in range(2):
                nc.scalar.activation(xh[:, p.par, n], xd[:, p.par, n], ACT.Identity, bias=s2[:, n:n + 1],
                                     scale=s1[:, n:n + 1]).then_inc(s_xh, 1)

        def context_high(p):
            act.wait_ge(s_c[p.par], 32 * (p.before + 1))
            wait(act, s_v, 4 * (p.idx - 1))
            wait(act, s_s, 16 * (p.idx - 1))
            wait(act, s_t, 16 * (p.idx - 1))
            nc.scalar.copy(cs[:, p.par], cd[:, p.par]).then_inc(s_cs, 1)

        def context_ones(p):
            nc.scalar.copy(c1[0:C0, p.par], cd[0:C0, p.par]).then_inc(s_c1, 1)

        def q_high(p, h):
            act.wait_ge(s_q, H0 * p.idx + h + 1)
            if h == 0:
                wait(act, s_s, 16 * (p.idx - 1))
                wait(act, s_t, 16 * (p.idx - 1))
            nc.scalar.activation(qh[:, p.par, h].rearrange("p n s -> p (n s)"), J[h % 2], ACT.Identity,
                                 bias=qbias[:, h:h + 1]).then_inc(s_qh, 1)

        def v_copy(p, n, kt):
            act.wait_ge(s_v, 4 * p.idx + 2 * n + 2 - kt)
            if n == 0 and kt == 1:
                wait(act, s_pv, 16 * (p.idx - 1))
            nc.scalar.copy(vw[:, p.par, n, kt, :, 0:C0], J[kt].rearrange("p (h c) -> p h c", c=C0)
                           ).then_inc(s_vw, 1)

        def exp(p, u):
            act.wait_ge(s_t, 16 * p.idx + u + 1)
            wait(act, s_pv, 16 * p.idx + u - 1)
            nc.scalar.activation(pt[:, u % 2].rearrange("p t q -> p (t q)"), T[u % 2], ACT.Exp
                                 ).then_inc(s_exp, 1)

        def step(p):
            for u in range(16):
                if u < H0 and exists(p, 1):
                    q_high(p.next(), u)
                if exists(p, 0):
                    exp(p, u)
                if u == 0 and exists(p, 1):
                    context_high(p.next())
                if u == 1 and exists(p, 1):
                    context_ones(p.next())
                if u in (11, 12, 13, 14) and exists(p, 1):
                    v_copy(p.next(), (u - 11) // 2, 1 - (u - 11) % 2)
                if u == 11 and exists(p, 2):
                    prepare_x(p.next(2))

        step(Pair(-2, 0, -1))
        act.wait_ge(s_fold, 2)
        nc.scalar.copy(wvo_hi[:], M[0]).then_inc(s_fold_ev, 1)
        step(Pair(-1, 1, -1))
        run_steps(act, step, 0, NP - 1, 2, NP - 3)

    @block.vector
    def _(dve):
        nc.vector.memset(c1[C0:P].bitcast(F32), 0.0).then_inc(s_ones, 1)
        dve.wait_ge(s_ones, 1)
        nc.vector.memset(c1[C0:C0 + 1].bitcast(F32), 1.0).then_inc(s_ones, 1)
        nc.vector.memset(ql[C0:P, 1].bitcast(F32), 0.0).then_inc(s_ones, 1)
        def row_stats(p):
            dve.wait_ge(s_x[p.par], 32 * (p.before + 1))
            wait(dve, s_mv, 2 * p.idx)
            for n in range(2):
                nc.vector.bn_stats(bnst[:, n], xd[:, p.par, n]).then_inc(s_bn, 1)
            dve.wait_ge(s_bn, 2 * p.idx + 2)
            wait(dve, s_st, 2 * p.idx)
            wait(dve, s_dev, 2 * p.idx)
            dve.sem_inc(s_tick, 1)
            for n in range(2):
                nc.vector.bn_aggr(mv[:, n], bnst[:, n]).then_inc(s_mv, 1)

        def deviation(p):
            dve.wait_ge(s_st, 2 * p.idx + 1)
            wait(dve, s_aff, 4 * p.idx)
            wait(dve, s_veps, p.idx)
            wait(dve, s_dev2, p.idx)
            nc.vector.tensor_copy(mvm[:], Y[0][:, STATS:STATS + 4].rearrange("p (n k) -> p n k", k=2)).then_inc(s_dev, 1)
            dve.wait_ge(s_dev, 2 * p.idx + 1)
            dve.wait_ge(s_mv, 2 * p.idx + 2)
            nc.vector.tensor_tensor(dev[:], mv[:, :, 0], mvm[:, :, 0], ALU.subtract).then_inc(s_dev, 1)
            dve.wait_ge(s_dev, 2 * p.idx + 2)
            nc.vector.tensor_tensor(dev2[:], dev[:], dev[:], ALU.mult).then_inc(s_dev2, 1)

        def variance(p):
            dve.wait_ge(s_st, 2 * p.idx + 2)
            nc.vector.scalar_tensor_tensor(veps[:], Y[0][:, STATS:STATS + 2], EPS, mvm[:, :, 1], ALU.add, ALU.add
                                           ).then_inc(s_veps, 1)

        def q_low(p, h):
            dve.wait_ge(s_qh, H0 * p.idx + h + 1)
            if h == 0:
                wait(dve, s_t, 16 * (p.idx - 1))
            nc.vector.scalar_tensor_tensor(ql[0:C0, p.par, :, h], J[h % 2][0:C0].rearrange("p (n s) -> p n s", n=2),
                                           qbias[0:C0, h:h + 1], qh[0:C0, p.par, h].bitcast(F32),
                                           ALU.add, ALU.subtract).then_inc(s_ql, 1)

        def maximum(p, k):
            n, h = k // H0, k % H0
            dve.wait_ge(s_s, 16 * p.idx + k + 1)
            if k % H0 == 0:
                wait(dve, s_mt, 2 * (p.idx - 1) + n + 1)
            nc.vector.tensor_reduce(out=nmax[:, n, h], in_=M[k % 2].rearrange("p (t k) -> p t k", t=QT),
                                    op=ALU.max, axis=AX.X, negate=True).then_inc(s_max, 1)

        def round_max(p, n):
            dve.wait_ge(s_mt, 2 * p.idx + n + 1)
            wait(dve, s_row[n], 16 * p.idx)
            nc.vector.tensor_copy(nmaxt[:, n], J[0][0:H0 * QT, 0:P]).then_inc(s_mtc, 1)

        def normalise(p, g):
            n, a = g // 4, g % 4
            dve.wait_ge(s_pv, 16 * p.idx + 2 * g + 2)
            wait(dve, s_yn, 8 * p.idx + g - 1)
            yb = Y[g % 2][:, 0:2 * QT * (C0 + 1)].rearrange("p (b t c) -> p b t c", t=QT, c=C0 + 1)
            nc.vector.reciprocal(rden[:, g % 2], yb[:, :, :, C0]).then_inc(s_rden, 1)
            dve.wait_ge(s_rden, 8 * p.idx + g + 1)
            if a == 0:
                wait(dve, s_ysum, 6 * (p.idx - 1) + 3 * n + 1)
            nc.vector.tensor_tensor(yn[:, n, a], yb[:, :, :, 0:C0], bc(rden[:, g % 2], 3, C0), ALU.mult
                                    ).then_inc(s_yn, 1)

        def residual(p):
            dve.wait_ge(s_ot, p.idx + 1)
            dve.wait_ge(s_xp[p.par], 16 * (p.before + 1))
            nc.vector.scalar_tensor_tensor(x1[:, p.idx], J[1][:, 0:D], obias[:], xp[:, p.par], ALU.add, ALU.add
                                           ).then_inc(s_x1, 1)

        def step(p):
            for u in range(16):
                if u == 1 and exists(p, 0):
                    round_max(p, 1)
                if u < H0 and exists(p, 1):
                    q_low(p.next(), u)
                if u == 0 and exists(p, -1):
                    normalise(p.next(-1), 7)
                if u == 9 and exists(p, -1):
                    residual(p.next(-1))
                if u == 12 and exists(p, 3):
                    row_stats(p.next(3))
                if u == 3 and exists(p, 2):
                    deviation(p.next(2))
                if u == 7 and exists(p, 2):
                    variance(p.next(2))
                if u % 2 == 1 and u > 1 and exists(p, 0):
                    normalise(p, u // 2 - 1)
                for k in MAX_UNITS[u]:
                    if exists(p, 1):
                        maximum(p.next(), k)
                if u == 11 and exists(p, 1):
                    round_max(p.next(), 0)

        row_stats(Pair(0, 0, 0))
        dve.wait_ge(s_fold_ev, 3)
        for b in range(2):
            hi = a_st[C0:P, 4 * b:4 * b + 4]
            nc.vector.scalar_tensor_tensor(hi, T[b][C0:P].rearrange("p (h c) -> p h c", c=P), SCALE0,
                                           hi.bitcast(F32), ALU.mult, ALU.subtract).then_inc(s_fold_lo, 1)
        dve.wait_ge(s_wot, 1)
        for copy in range(2):
            nc.vector.tensor_copy(wo2[:, :, copy], J[0][0:C0].rearrange("o (h c) -> o h c", c=C0)).then_inc(s_wot_ev, 1)
        step(Pair(-2, 0, -1))
        dve.wait_ge(s_fold_ev, 4)
        nc.vector.tensor_tensor(wvo_lo[:], M[0], wvo_hi[:].bitcast(F32), ALU.subtract).then_inc(s_fold_lo, 1)
        nc.vector.tensor_tensor(obias[:], Y[1][:, 0:1], bo2[:], ALU.add).then_inc(s_fold_lo, 1)
        step(Pair(-1, 1, -1))
        run_steps(dve, step, 0, NP - 1, 2, NP - 5)
        normalise(Pair(NP - 1, (NP - 1) % 2, (NP - 1) // 2), 7)
        residual(Pair(NP - 1, (NP - 1) % 2, (NP - 1) // 2))

    @block.tensor
    def _(pe):
        mm = nc.tensor.matmul
        pe.wait_ge(s_wqk, 16 * 5)
        for h in range(H0):
            mm(T[h // 4][:, h % 4 * P:(h % 4 + 1) * P], wq2[:, h].rearrange("o a c -> o (a c)"),
               wk2[:, h].rearrange("o a c -> o (a c)"), start=True, stop=True)
            last = mm(M[1][:, h:h + 1], wk2[:, h].rearrange("o a c -> o (a c)"), bq_sb[:, h:h + 1], start=True, stop=True)
        last.then_inc(s_fold, 1)
        pe.wait_ge(s_w, 16 * 10)
        pe.wait_ge(s_const, 5)
        for h in range(H0):
            last = nc.tensor.transpose(J[0][0:C0, h * C0:(h + 1) * C0], wo_nat[:, h * C0:(h + 1) * C0], ident[0:C0, 0:C0])
        last.then_inc(s_wot, 1)

        def stats(p, k):
            if k == 0:
                pe.wait_ge(s_mv, 2 * p.idx + 2)
                wait(pe, s_veps, p.idx)
                mm(Y[0][:, STATS:STATS + 4], mean64[:], mv[0:C0].rearrange("p n k -> p (n k)"), start=True, stop=True
                   ).then_inc(s_st, 1)
            else:
                pe.wait_ge(s_dev2, p.idx + 1)
                mm(Y[0][:, STATS:STATS + 2], mean64[:], dev2[0:C0], start=True, stop=True).then_inc(s_st, 1)

        def project_q(p, h):
            if h == 0:
                pe.wait_ge(s_xl, p.idx + 1)
                pe.wait_ge(s_xh, 2 * p.idx + 2)
                wait(pe, s_vw, 4 * p.idx)
            else:
                wait(pe, s_ql, H0 * p.idx + h - 1)
            if h == 2:
                wait(pe, s_mtc, 2 * p.idx)
            mm(J[h % 2], a_st[:, h], xh[:, p.par].rearrange("p n s -> p (n s)"), start=True, stop=False)
            mm(J[h % 2], a_st[:, h], xl[:, p.par].rearrange("p n s -> p (n s)"), start=False, stop=True
               ).then_inc(s_q, 1)

        def scores_for_max(p, k):
            n, h = k // H0, k % H0
            if k == 0:
                pe.wait_ge(s_csl, p.idx + 1)
            if n == 0:
                pe.wait_ge(s_qh, H0 * p.idx + h + 1)
            wait(pe, s_max, 16 * p.idx + k - 1)
            for qt in range(QT):
                last = mm(M[k % 2][:, qt * D:(qt + 1) * D], qh[:, p.par, h, n, qt * P:(qt + 1) * P], cs[:, p.par, n],
                          start=True, stop=True)
            last.then_inc(s_s, 1)

        def transpose_max(p, n):
            pe.wait_ge(s_max, 16 * p.idx + 8 * n + 8)
            nc.tensor.transpose(J[0][0:H0 * QT, 0:P], nmax[:, n].rearrange("p h t -> p (h t)"), ident[:]
                                ).then_inc(s_mt, 1)

        def project_v(p, n, kt):
            if n == 0 and kt == 0:
                wait(pe, s_mtc, 2 * p.idx + 1)
            if n == 0 and kt == 1:
                wait(pe, s_ql, H0 * p.idx + H0)
                wait(pe, s_x1, p.idx - 1)
            if n == 1:
                pe.wait_ge(s_vw, 4 * p.idx + 2 - kt)
            keys = slice(kt * P, (kt + 1) * P)
            mm(J[kt], cs[:, p.par, n, keys], wvo_hi[:], start=True, stop=False)
            mm(J[kt], cs[:, p.par, n, keys], wvo_lo[:], start=False, stop=True).then_inc(s_v, 1)

        def scores(p, u):
            n, h = u // H0, u % H0
            if h == 0:
                pe.wait_ge(s_row[n], 16 * (p.idx + 1))
            if u == 0:
                pe.wait_ge(s_c1, p.idx + 1)
                pe.wait_ge(s_ql, H0 * (p.idx + 1))
            wait(pe, s_exp, 16 * p.idx + u - 1)
            for kt in range(KT):
                keys = slice(kt * P, (kt + 1) * P)
                out = T[u % 2][:, kt * D:(kt + 1) * D]
                mm(out, cs[:, p.par, n, keys], qh[:, p.par, h, n], start=True, stop=False)
                last = mm(out, c1[:, p.par, n, keys], ql[:, p.par, n, h], start=False, stop=True)
            last.then_inc(s_t, 1)

        def weigh(p, u):
            n, h = u // H0, u % H0
            pe.wait_ge(s_exp, 16 * p.idx + u + 1)
            if u == 0:
                pe.wait_ge(s_vw, 4 * p.idx + 4)
                wait(pe, s_veps, p.idx + 2 if exists(p, 1) else NP)
            if u % 2 == 0:
                wait(pe, s_yn, 8 * p.idx + u // 2 - 1)
            for qt in range(QT):
                at = (u % 2 * QT + qt) * (C0 + 1)
                out = Y[u // 2 % 2][:, at:at + C0 + 1]
                for kt in range(KT):
                    last = mm(out, pt[:, u % 2, kt, qt * P:(qt + 1) * P], vw[:, p.par, n, kt, h],
                              start=(kt == 0), stop=(kt == KT - 1))
            last.then_inc(s_pv, 1)

        def transpose_out(p):
            pe.wait_ge(s_ysum, 6 * p.idx + 6)
            for qt in range(QT):
                last = nc.tensor.transpose(J[1][:, qt * P:(qt + 1) * P],
                                           ot[:, p.par, qt].rearrange("q n c -> q (n c)"), ident[:])
            last.then_inc(s_ot, 1)

        def step(p):
            for u in range(16):
                if u < H0 and exists(p, 1):
                    project_q(p.next(), u)
                if u == 0 and exists(p, -1):
                    weigh(p.next(-1), 15)
                if u == 1 and exists(p, 0):
                    if exists(p, 1):
                        pe.wait_ge(s_ql, H0 * (p.idx + 1) + 1)
                    pe.wait_ge(s_vw, 4 * (p.idx + 1))
                    transpose_max(p, 1)
                if u == 2 and exists(p, 2):
                    stats(p.next(2), 0)
                if u == 6 and exists(p, 2):
                    stats(p.next(2), 1)
                if u == 9 and exists(p, -1):
                    pe.wait_ge(s_ql, H0 * (p.idx + 2 if exists(p, 1) else NP))
                    pe.wait_ge(s_vw, 4 * (p.idx + 1))
                    transpose_out(p.next(-1))
                if exists(p, 0):
                    scores(p, u)
                    if u > 0:
                        weigh(p, u - 1)
                for k in MAX_UNITS[u]:
                    if exists(p, 1):
                        scores_for_max(p.next(), k)
                if u == 11 and exists(p, 1):
                    pe.wait_ge(s_ql, H0 * (p.idx + 2))
                    transpose_max(p.next(), 0)
                if u in (11, 12, 13, 14) and exists(p, 1):
                    project_v(p.next(), (u - 11) // 2, 1 - (u - 11) % 2)

        step(Pair(-2, 0, -1))
        pe.wait_ge(s_wot_ev, 2)
        for h in range(H0):
            mm(M[0][:, h * C0:(h + 1) * C0], wv2[:, h].rearrange("o a c -> o (a c)"), wo2[:, h, 0], start=True, stop=True)
        for h in range(H0):
            last = mm(Y[1][:, 0:1], wo2[:, h].rearrange("o a c -> o (a c)"), bv_sb[:, h:h + 1],
                      start=(h == 0), stop=(h == H0 - 1))
        last.then_inc(s_fold, 1)
        pe.wait_ge(s_fold_lo, 4)
        pe.wait_ge(s_ones, 3)
        pe.wait_ge(s_zeros, 1)
        step(Pair(-1, 1, -1))
        run_steps(pe, step, 0, NP - 1, 2, NP - 3)
        weigh(Pair(NP - 1, (NP - 1) % 2, (NP - 1) // 2), 15)
        pe.wait_ge(s_x1, NP - 1)
        transpose_out(Pair(NP - 1, (NP - 1) % 2, (NP - 1) // 2))


NH, HD = 16, D // 16
G = D // P
FF = 4 * D
SCALE1 = float(HD) ** -0.5
TOK = 2 * S


class Attention:

    def __init__(self, name, sb, sem, cross):
        cols = 2 * D if cross else D
        self.cross = cross
        self.bnst = sb(name + "_bnst", [P, 6], F32)
        self.mv = sb(name + "_mv", [P, 2], F32)
        self.veps = sb(name + "_veps", [P, 1], F32)
        self.rstd = sb(name + "_rstd", [P, 1], F32)
        self.xc = sb(name + "_xc", [P, D], F32)
        self.hh = sb(name + "_hh", [P, cols], F32R)
        self.hl = sb(name + "_hl", [P, cols], F32R)
        self.qs = sb(name + "_qs", [P, G, TOK], F32)
        self.q8 = sb(name + "_q8", [P, G, 2, 8, S], F32)
        self.kT = sb(name + "_kT", [P, G, TOK], F32)
        self.vz = sb(name + "_vz", [P, 2, 2, D], F32)
        self.t = sb(name + "_t", [P, 2, 8, S], F32)
        self.nmax = sb(name + "_nmax", [P, 2, 8], F32)
        self.den = sb(name + "_den", [P, 2, 8], F32)
        self.rden = sb(name + "_rden", [P, 2, 8], F32)
        self.pT = sb(name + "_pT", [P, 8, P], F32)
        self.yh = sb(name + "_yh", [P, G, TOK], F32R)
        self.yl = sb(name + "_yl", [P, G, TOK], F32R)
        self.xb = sb(name + "_xb", [P, D], F32)
        self.done = {what: sem(name + "_" + what) for what in (
            "bnst", "mv", "veps", "rstd", "xc", "transposed", "hh", "hl", "qk", "qs", "q8_g0", "q8_g1", "kT", "v",
            "vz", "s", "masked", "mask_added", "nmax", "shifted", "exp", "den", "rden", "probs", "p_transposed",
            "pT", "y", "yh", "yl", "o", "xb", "x")}


def columns(v):
    return v.rearrange("(m p) -> p m", p=P)


class AttentionWeights:

    def __init__(self, sb, sem, self_mask, ln1_s, ln1_b, w_qkv, b_qkv, w_ao, b_ao, ln2_s, ln2_b, w_q, b_q, w_kv,
                 b_kv, w_co, b_co):
        self.qkv = sb("w_qkv_raw", [P, G, 3 * D], F32)
        self.ao = sb("w_ao_raw", [P, G, D], F32)
        self.cq = sb("w_q_raw", [P, G, D], F32)
        self.kv = sb("w_kv_raw", [P, G, 2 * D], F32)
        self.co = sb("w_co_raw", [P, G, D], F32)
        self.lns = sb("ln_scales", [P, 2, G], F32)
        self.lnb = sb("ln_biases", [P, 2, G], F32)
        self.bias_self = sb("bias_self", [P, 3 * G], F32)
        self.bias_cross = sb("bias_cross", [P, 3 * G], F32)
        self.bias_out = sb("bias_out", [P, 2, D], F32)
        self.m_self = sb("m_self", [P, S], F32)
        self.loaded = sem("w1_loaded")
        self.loads = [(dst[:], src.rearrange("(k p) n -> p k n", p=P)) for dst, src in (
            (self.qkv, w_qkv), (self.ao, w_ao), (self.cq, w_q), (self.kv, w_kv), (self.co, w_co))]
        self.loads += [(self.lns[:, 0], columns(ln1_s)), (self.lns[:, 1], columns(ln2_s)),
                       (self.lnb[:, 0], columns(ln1_b)), (self.lnb[:, 1], columns(ln2_b)),
                       (self.bias_self[:], columns(b_qkv)), (self.bias_cross[:, 0:G], columns(b_q)),
                       (self.bias_cross[:, G:3 * G], columns(b_kv))]
        self.loads += [(self.bias_out[:, n], bias.partition_broadcast(P)) for n, bias in enumerate((b_ao, b_co))]
        self.loads += [(self.m_self[S * h2:S * h2 + S], self_mask[0, 0]) for h2 in range(2)]

    def load(self, sp):
        for dst, src in self.loads:
            sp.dma_start(dst, src, allow_slow_non_contiguous=True).then_inc(self.loaded, 16)


class MlpWeights:

    def __init__(self, sb, sem, psum, ln3_s, ln3_b, w1, b1, w2, b2):
        self.w1_raw = sb("w1_raw", [P, G, FF], F32)
        self.w1_hi = sb("w1_high", [P, G, FF], F32R)
        self.w1_lo = sb("w1_low", [P, G, FF], F32R)
        self.w2_raw = sb("w2_raw", [P, FF // P, D], F32)
        self.w2_hi = sb("w2_high", [P, FF // P, D], F32R)
        self.w2_lo = sb("w2_low", [P, FF // P, D], F32R)
        self.lns = sb("ln3_scale", [P, G], F32)
        self.lnb = sb("ln3_bias", [P, G], F32)
        self.bias1 = sb("bias_hidden", [P, FF // P], F32)
        self.bias2 = sb("bias_mlp", [P, D], F32)
        self.product = psum[:, 6, 0:FF // P]
        self.loaded, self.high, self.low = sem("w2_loaded"), sem("w2_high"), sem("w2_low")
        self.multiplied = sem("bias1_product")
        self.loads = [(self.w1_raw[:], w1.rearrange("(k p) n -> p k n", p=P)),
                      (self.w2_raw[:], w2.rearrange("(k p) n -> p k n", p=P)),
                      (self.lns[:], columns(ln3_s)), (self.lnb[:], columns(ln3_b)), (self.bias1[:], columns(b1)),
                      (self.bias2[:], b2.partition_broadcast(P))]
        self.pieces = [(self.w1_raw[:, kt], self.w1_hi[:, kt], self.w1_lo[:, kt], self.lns[:, kt:kt + 1])
                       for kt in range(G)]
        self.pieces += [(self.w2_raw[:, m:m + 4], self.w2_hi[:, m:m + 4], self.w2_lo[:, m:m + 4], None)
                        for m in range(0, FF // P, 4)]

    def load(self, sp):
        for dst, src in self.loads:
            sp.dma_start(dst, src, allow_slow_non_contiguous=True).then_inc(self.loaded, 16)


def split_high(nc, raw, hi, scale):
    if scale is None:
        return nc.scalar.copy(hi, raw)
    return nc.scalar.activation(hi, raw, ACT.Copy, scale=scale)


def split_low(nc, raw, hi, lo, scale):
    if scale is None:
        return nc.vector.tensor_tensor(lo, raw, hi.bitcast(F32), ALU.subtract)
    return nc.vector.scalar_tensor_tensor(lo, raw, scale, hi.bitcast(F32), ALU.mult, ALU.subtract)


def layer1_attentions(nc, sb, psum, sem, block, ctx, cross_mask, w, w_mlp, x1):
    SELF = Attention("self", sb, sem, False)
    CROSS = Attention("cross", sb, sem, True)
    wqkv_hi, wqkv_lo = sb("w_qkv_high", [P, G, 3 * D], F32R), sb("w_qkv_low", [P, G, 3 * D], F32R)
    wao_hi, wao_lo = sb("w_ao_high", [P, G, D], F32R), sb("w_ao_low", [P, G, D], F32R)
    wcq_hi, wcq_lo = sb("w_q_high", [P, G, D], F32R), sb("w_q_low", [P, G, D], F32R)
    wkv_hi, wkv_lo = sb("w_kv_high", [P, G, 2 * D], F32R), sb("w_kv_low", [P, G, 2 * D], F32R)
    wco_hi, wco_lo = sb("w_co_high", [P, G, D], F32R), sb("w_co_low", [P, G, D], F32R)
    bias1, bias2, bias_out, m_self = w.bias_self, w.bias_cross, w.bias_out, w.m_self
    pieces = [(w.qkv[:, kt], wqkv_hi[:, kt], wqkv_lo[:, kt], w.lns[:, 0, kt:kt + 1]) for kt in range(G)]
    pieces += [(w.ao[:], wao_hi[:], wao_lo[:], None)]
    pieces += [(w.cq[:, kt], wcq_hi[:, kt], wcq_lo[:, kt], w.lns[:, 1, kt:kt + 1]) for kt in range(G)]
    pieces += [(w.kv[:], wkv_hi[:], wkv_lo[:], None), (w.co[:], wco_hi[:], wco_lo[:], None)]
    ident = sb("ident1", [P, P], F32)
    mask8 = sb("mask8", [P, 8], F32)
    ma_self = sb("ma_self", [P, S], F32)
    m_cross = sb("m_cross", [P, 2, S], F32)
    ma_cross = sb("ma_cross", [P, 2, S], F32)
    ctok = sb("ctx_tokens", [P, D], F32)
    neghalf = sb("neghalf1", [P, 1], F32)

    SB = psum[:, 0:2]
    PB = psum[:, 2:4]
    QK, V, T = psum[:, 4], psum[:, 5], psum[:, 6]
    YO = psum[:, 7]

    s_const, s_hi, s_lo = sem("const1_set"), sem("w1_high"), sem("w1_low")
    s_b, s_bf, s_vz0 = sem("bias_product"), sem("bias_folded"), sem("vz_zeroed")
    s_ctx, s_cm, s_ma = sem("ctx_tokens_loaded"), sem("cross_mask_loaded"), sem("cross_mask_term")
    s_tick = sem("wait_carrier1")

    def in_steps(eng, half, after):
        def step(i):
            half(SELF, f2=at(i, 0), b1=at(i, -1), f1=at(i, -2), sm=at(i, -3), b2=at(i, -4))
            half(CROSS, f2=at(i, -2), b1=at(i, -3), f1=at(i, 1), sm=at(i, 0), b2=at(i, -1))
        for i in range(-1, 5):
            step(i)
            after(i)
        with eng.Fori(5, NP - 1) as i:
            step(i)
        for i in range(NP - 1, NP + 4):
            step(i)
            after(i)

    def at(i, off):
        if isinstance(i, int) and not 0 <= i + off < NP:
            return None
        return i + off

    def before(a, p):
        n = p + 3 if a.cross else p - 2
        return n if not isinstance(n, int) else max(0, min(n, NP))

    def other(a):
        return SELF if a.cross else CROSS

    @block.sync
    def _(sp):
        def load(p):
            wait(sp, CROSS.done["transposed"], p)
            sp.dma_start(ctok[:], ctx[bass.ds(p * 2, 2)].rearrange("n t f -> (n t) f")).then_inc(s_ctx, 16)
            wait(sp, CROSS.done["masked"], 2 * p)
            wait(sp, s_ma, p)
            for h2 in range(2):
                sp.dma_start(m_cross[S * h2:S * h2 + S],
                             cross_mask[bass.ds(p * 2, 2), 0].rearrange("n q k -> q n k")).then_inc(s_cm, 16)
        load(0)
        w_mlp.load(sp)
        load(1)
        with sp.Fori(2, NP) as p:
            load(p)

    @block.gpsimd
    def _(pool):
        nc.gpsimd.memset(ident[:], 0.0).then_inc(s_const, 1)
        nc.gpsimd.memset(mask8[:], 1.0).then_inc(s_const, 1)
        nc.gpsimd.memset(neghalf[:], -0.5).then_inc(s_const, 1)
        pool.wait_ge(s_const, 3)
        nc.gpsimd.affine_select(out=ident[:], in_=ident[:], compare_op=ALU.not_equal, fill=1.0, base=0,
                                pattern=[[-1, P]], channel_multiplier=1).then_inc(s_const, 1)
        nc.gpsimd.affine_select(out=mask8[:], in_=mask8[:], compare_op=ALU.is_ge, fill=0.0, base=0,
                                pattern=[[-HD, 8]], channel_multiplier=1).then_inc(s_const, 1)
        pool.wait_ge(s_const, 5)
        nc.gpsimd.affine_select(out=mask8[:], in_=mask8[:], compare_op=ALU.is_ge, fill=0.0, base=HD - 1,
                                pattern=[[HD, 8]], channel_multiplier=-1).then_inc(s_const, 1)
        pool.wait_ge(w.loaded, 16 * len(w.loads))
        nc.gpsimd.tensor_scalar(ma_self[:], m_self[:], 1e4, -1e4, ALU.mult, ALU.add).then_inc(s_const, 1)

        def after(i):
            if i == -1:
                for a in (SELF, CROSS):
                    nc.gpsimd.memset(a.vz[:], 0.0).then_inc(s_vz0, 1)
                pool.wait_ge(s_const, 7)

        def half(a, f2, b1, f1, sm, b2):
            done, o = a.done, other(a)
            if sm is not None:
                for n in range(2):
                    pool.wait_ge(o.done["masked"], 2 * sm + n + 1)
                    if o.cross and n == 0:
                        pool.wait_ge(s_ma, sm + 1)
                    term = ma_cross[:, n] if o.cross else ma_self[:]
                    nc.gpsimd.tensor_tensor(o.t[:, n], o.t[:, n], bc(term, 1, 8), ALU.add
                                            ).then_inc(o.done["mask_added"], 1)
            if f1 is not None:
                pool.wait_ge(o.done["veps"], f1 + 1)
                wait(pool, o.done["xc"], f1)
                nc.gpsimd.tensor_tensor(o.rstd[:], o.veps[:], neghalf[:], ALU.pow).then_inc(o.done["rstd"], 1)
            if f2 is not None:
                pool.wait_ge(done["qs"], 2 * f2 + 2)
                wait(pool, done["s"], 2 * f2)
                for n in range(2):
                    q_n = bc(a.qs[:, 1, S * n:S * n + S], 1, 8)
                    nc.gpsimd.tensor_tensor(a.q8[:, 1, n], q_n, bc(mask8[:], 2, S), ALU.mult).then_inc(done["q8_g1"], 1)
                if a.cross:
                    pool.wait_ge(s_cm, 32 * (f2 + 1))
                    wait(pool, done["mask_added"], 2 * f2)
                    pool.sem_inc(s_tick, 1)
                    nc.gpsimd.tensor_scalar(ma_cross[:], m_cross[:], 1e4, -1e4, ALU.mult, ALU.add).then_inc(s_ma, 1)
            if b1 is not None:
                wait(pool, done["x"], b1)
                if a.cross:
                    pool.wait_ge(SELF.done["x"], b1 + 1)
                nc.gpsimd.tensor_tensor(a.xb[:], x1[:, b1], bias_out[:, 1 if a.cross else 0], ALU.add
                                        ).then_inc(done["xb"], 1)

        in_steps(pool, half, after)

    @block.scalar
    def _(act):
        def split(first, last):
            for raw, hi, _, scale in pieces[first:last]:
                split_high(nc, raw, hi, scale).then_inc(s_hi, 1)

        act.wait_ge(w.loaded, 16 * len(w.loads))
        split(0, 2)

        def after(i):
            if i == -1:
                split(2, 3)
                act.wait_ge(s_bf, 4)
                act.wait_ge(s_vz0, 2)
            if i == 0:
                split(3, 7)
            if i == NP:
                act.wait_ge(w_mlp.loaded, 16 * len(w_mlp.loads))
            if NP <= i < NP + 4:
                raw, hi, _, scale = w_mlp.pieces[i - NP]
                split_high(nc, raw, hi, scale).then_inc(w_mlp.high, 1)

        def half(a, f2, b1, f1, sm, b2):
            done, o, bias = a.done, other(a), (bias2 if a.cross else bias1)
            if f2 is not None:
                act.wait_ge(done["qk"], f2 + 1)
                wait(act, done["q8_g0"], 2 * f2)
                wait(act, done["q8_g1"], 2 * f2)
                for g in range(G):
                    nc.scalar.activation(a.qs[:, g], QK[:, g * TOK:(g + 1) * TOK], ACT.Identity, bias=bias[:, g:g + 1],
                                         scale=SCALE1).then_inc(done["qs"], 1)
                wait(act, done["s"], 2 * f2)
                for g in range(G):
                    nc.scalar.activation(a.kT[:, g], QK[:, (G + g) * TOK:(G + g + 1) * TOK], ACT.Identity,
                                         bias=bias[:, G + g:G + g + 1]).then_inc(done["kT"], 1)
            if b1 is not None:
                for n in range(2):
                    act.wait_ge(done["p_transposed"], 2 * b1 + n + 1)
                    if n == 0:
                        wait(act, done["y"], b1)
                    nc.scalar.copy(a.pT[:, 4 * n:4 * n + 4].rearrange("p a q -> p (a q)"), PB[:, n]).then_inc(done["pT"], 1)
            if sm is not None:
                act.wait_ge(o.done["shifted"], sm + 1)
                nc.scalar.activation(o.t[:, 0], o.t[:, 0], ACT.Exp).then_inc(o.done["exp"], 1)
                act.wait_ge(o.done["nmax"], 2 * sm + 2)
                wait(act, o.done["rden"], 2 * sm)
                for h in range(8):
                    last = nc.scalar.activation(o.t[:, 1, h], o.t[:, 1, h], ACT.Exp, bias=o.nmax[:, 1, h:h + 1],
                                                accum_out=o.den[:, 1, h:h + 1])
                last.then_inc(o.done["exp"], 1)
            if f1 is not None:
                act.wait_ge(o.done["transposed"], f1 + 1)
                wait(act, o.done["v"], f1)
                nc.scalar.copy(o.hh[:], T[:, 0:o.hh.shape[1]]).then_inc(o.done["hh"], 1)
            if b1 is not None:
                act.wait_ge(done["y"], b1 + 1)
                wait(act, done["o"], b1)
                wait(act, done["yl"], 2 * b1)
                for g in range(G):
                    nc.scalar.activation(a.yh[:, g], YO[:, g * TOK:(g + 1) * TOK], ACT.Identity,
                                         bias=bias[:, 2 * G + g:2 * G + g + 1]).then_inc(done["yh"], 1)
            if f2 is not None:
                act.wait_ge(done["v"], f2 + 1)
                wait(act, done["y"], f2)
                for n in range(2):
                    for hp2 in range(2):
                        src = V[S * n:S * n + S, 0:D].rearrange("k (gj a h d) -> k gj a h d", a=2, h=2, d=HD)[:, :, hp2]
                        dst = a.vz[S * hp2:S * hp2 + S, n].rearrange("k h (gj a c d) -> k gj a c h d", a=2, c=2, d=HD)
                        for h2 in range(2):
                            nc.scalar.copy(dst[:, :, hp2, h2, h2], src[:, :, h2]).then_inc(done["vz"], 1)

        in_steps(act, half, after)

    @block.vector
    def _(dve):
        def split(first, last):
            for n in range(first, last):
                raw, hi, lo, scale = pieces[n]
                dve.wait_ge(s_hi, n + 1)
                split_low(nc, raw, hi, lo, scale).then_inc(s_lo, 1)

        dve.wait_ge(w.loaded, 16 * len(w.loads))
        split(0, 2)
        dve.wait_ge(s_const, 7)

        def after(i):
            if i == -1:
                split(2, 3)
                dve.wait_ge(s_b, 1)
                nc.vector.tensor_tensor(bias1[:], V[:, 0:3 * G], bias1[:], ALU.add).then_inc(s_bf, 1)
                nc.vector.tensor_tensor(bias2[:, 0:G], V[:, 16:16 + G], bias2[:, 0:G], ALU.add).then_inc(s_bf, 1)
                dve.wait_ge(s_bf, 2)
                nc.vector.tensor_scalar(bias1[:, 0:G], bias1[:, 0:G], SCALE1, None, ALU.mult).then_inc(s_bf, 1)
                nc.vector.tensor_scalar(bias2[:, 0:G], bias2[:, 0:G], SCALE1, None, ALU.mult).then_inc(s_bf, 1)
                dve.wait_ge(s_bf, 4)
            if i == 0:
                split(3, 7)
            if NP <= i < NP + 4:
                raw, hi, lo, scale = w_mlp.pieces[i - NP]
                dve.wait_ge(w_mlp.high, i - NP + 1)
                split_low(nc, raw, hi, lo, scale).then_inc(w_mlp.low, 1)

        def half(a, f2, b1, f1, sm, b2):
            done, o, bias = a.done, other(a), (bias2 if a.cross else bias1)
            odone = o.done
            if f1 is not None:
                if o.cross:
                    dve.wait_ge(SELF.done["x"], f1 + 1)
                wait(dve, odone["mv"], f1)
                dve.sem_inc(s_tick, 1)
                nc.vector.bn_stats(o.bnst[:], x1[:, f1]).then_inc(odone["bnst"], 1)
                dve.wait_ge(odone["bnst"], f1 + 1)
                wait(dve, odone["xc"], f1)
                dve.sem_inc(s_tick, 1)
                nc.vector.bn_aggr(o.mv[:], o.bnst[:]).then_inc(odone["mv"], 1)
                dve.wait_ge(odone["mv"], f1 + 1)
                wait(dve, odone["rstd"], f1)
                nc.vector.tensor_scalar(o.veps[:], o.mv[:, 1:2], EPS, None, ALU.add).then_inc(odone["veps"], 1)
            if sm is not None:
                for n in range(2):
                    dve.wait_ge(odone["mask_added"], 2 * sm + n + 1)
                    wait(dve, odone["exp"], 2 * sm)
                    if n == 0:
                        wait(dve, odone["shifted"], sm)
                    nc.vector.tensor_reduce(out=o.nmax[:, n], in_=o.t[:, n], op=ALU.max, axis=AX.X, negate=True
                                            ).then_inc(odone["nmax"], 1)
                    if n == 0:
                        dve.wait_ge(odone["nmax"], 2 * sm + 1)
                        nc.vector.tensor_tensor(o.t[:, 0], o.t[:, 0], bc(o.nmax[:, 0], 2, S), ALU.add
                                                ).then_inc(odone["shifted"], 1)
            if b2 is not None:
                dve.wait_ge(odone["o"], b2 + 1)
                dve.wait_ge(odone["xb"], b2 + 1)
                nc.vector.tensor_tensor(x1[:, b2], YO[:, D:2 * D], o.xb[:], ALU.add).then_inc(odone["x"], 1)
            if f1 is not None:
                dve.wait_ge(odone["rstd"], f1 + 1)
                wait(dve, odone["transposed"], f1)
                nc.vector.tensor_scalar(o.xc[:], x1[:, f1], o.mv[:, 0:1], o.rstd[:], ALU.subtract, ALU.mult
                                        ).then_inc(odone["xc"], 1)
            if f2 is not None:
                dve.wait_ge(done["qs"], 2 * f2 + 1)
                wait(dve, done["s"], 2 * f2)
                for n in range(2):
                    q_n = bc(a.qs[:, 0, S * n:S * n + S], 1, 8)
                    nc.vector.tensor_tensor(a.q8[:, 0, n], q_n, bc(mask8[:], 2, S), ALU.mult).then_inc(done["q8_g0"], 1)
            if sm is not None:
                dve.wait_ge(odone["exp"], 2 * sm + 1)
                wait(dve, odone["rden"], 2 * sm)
                nc.vector.tensor_reduce(out=o.den[:, 0], in_=o.t[:, 0], op=ALU.add, axis=AX.X).then_inc(odone["den"], 1)
                dve.wait_ge(odone["den"], sm + 1)
                for n in range(2):
                    dve.wait_ge(odone["exp"], 2 * sm + n + 1)
                    wait(dve, odone["probs"], 2 * sm)
                    nc.vector.reciprocal(o.rden[:, n], o.den[:, n]).then_inc(odone["rden"], 1)
                    dve.wait_ge(odone["rden"], 2 * sm + n + 1)
                    nc.vector.tensor_tensor(o.t[:, n], o.t[:, n], bc(o.rden[:, n], 2, S), ALU.mult
                                            ).then_inc(odone["probs"], 1)
            if f1 is not None:
                dve.wait_ge(odone["hh"], f1 + 1)
                wait(dve, odone["v"], f1)
                nc.vector.tensor_tensor(o.hl[:], T[:, 0:o.hl.shape[1]], o.hh[:].bitcast(F32), ALU.subtract
                                        ).then_inc(odone["hl"], 1)
            if b1 is not None:
                for g in range(G):
                    dve.wait_ge(done["yh"], 2 * b1 + 2)
                    wait(dve, done["o"], b1)
                    nc.vector.scalar_tensor_tensor(a.yl[:, g], YO[:, g * TOK:(g + 1) * TOK],
                                                   bias[:, 2 * G + g:2 * G + g + 1], a.yh[:, g].bitcast(F32),
                                                   ALU.add, ALU.subtract).then_inc(done["yl"], 1)
            if f2 is not None:
                wait(dve, done["p_transposed"], 2 * f2)
                for n in range(2):
                    dve.wait_ge(done["s"], 2 * f2 + n + 1)
                    if a.cross and n == 0:
                        dve.wait_ge(s_cm, 32 * (f2 + 1))
                    mask = m_cross[:, n] if a.cross else m_self[:]
                    nc.vector.tensor_tensor(a.t[:, n], SB[:, n].rearrange("p (h k) -> p h k", k=S), bc(mask, 1, 8),
                                            ALU.mult).then_inc(done["masked"], 1)

        in_steps(dve, half, after)

    @block.tensor
    def _(pe):
        mm = nc.tensor.matmul
        pe.wait_ge(w.loaded, 16 * len(w.loads))

        for at_col, raw, n, blocks in ((0, w.qkv, 0, 3 * G), (16, w.cq, 1, G)):
            for m in range(blocks):
                for kt in range(G):
                    last = mm(V[:, at_col + m:at_col + m + 1], raw[:, kt, m * P:(m + 1) * P],
                              w.lnb[:, n, kt:kt + 1], start=(kt == 0), stop=(kt == G - 1))
        last.then_inc(s_b, 1)
        pe.wait_ge(s_const, 7)

        def after(i):
            if i == -1:
                pe.wait_ge(s_lo, 3)
                pe.wait_ge(s_bf, 4)
            if i == 1:
                pe.wait_ge(s_lo, 7)
            if i == NP + 1:
                pe.wait_ge(w_mlp.loaded, 16 * len(w_mlp.loads))
                pe.wait_ge(CROSS.done["hl"], NP)
                for m in range(FF // P):
                    for kt in range(G):
                        last = mm(w_mlp.product[:, m:m + 1], w_mlp.w1_raw[:, kt, m * P:(m + 1) * P],
                                  w_mlp.lnb[:, kt:kt + 1], start=(kt == 0), stop=(kt == G - 1))
                last.then_inc(w_mlp.multiplied, 1)

        def three(out, pairs):
            n = len(pairs)
            for k, ((lh, ll), (rh, rl)) in enumerate(pairs):
                mm(out, lh, rh, start=(k == 0), stop=False)
                mm(out, ll, rh, start=False, stop=False)
                last = mm(out, lh, rl, start=False, stop=(k == n - 1))
            return last

        def half(a, f2, b1, f1, sm, b2):
            done, o = a.done, other(a)
            if f2 is not None:
                pe.wait_ge(done["hl"], f2 + 1)
                wait(pe, o.done["kT"], 2 * before(a, f2))
                wait(pe, done["kT"], 2 * f2)
                for m in range(2 * G):
                    pairs = []
                    for kt in range(G):
                        src = D if a.cross and m >= G else 0
                        cols = slice(src + kt * TOK, src + (kt + 1) * TOK)
                        if not a.cross:
                            wt = (wqkv_hi[:, kt, m * P:(m + 1) * P], wqkv_lo[:, kt, m * P:(m + 1) * P])
                        elif m < G:
                            wt = (wcq_hi[:, kt, m * P:(m + 1) * P], wcq_lo[:, kt, m * P:(m + 1) * P])
                        else:
                            wt = (wkv_hi[:, kt, (m - G) * P:(m - G + 1) * P], wkv_lo[:, kt, (m - G) * P:(m - G + 1) * P])
                        pairs.append((wt, (a.hh[:, cols], a.hl[:, cols])))
                    last = three(QK[:, m * TOK:(m + 1) * TOK], pairs)
                last.then_inc(done["qk"], 1)
            if b2 is not None:
                pe.wait_ge(o.done["yl"], 2 * b2 + 2)
                hi, lo = (wco_hi, wco_lo) if o.cross else (wao_hi, wao_lo)
                pairs = [((o.yh[:, g], o.yl[:, g]), (hi[:, g], lo[:, g])) for g in range(G)]
                three(YO[:, D:2 * D], pairs).then_inc(o.done["o"], 1)
            if b1 is not None:
                wait(pe, o.done["pT"], 2 * before(a, b1))
                wait(pe, done["pT"], 2 * b1)
                for n in range(2):
                    pe.wait_ge(done["probs"], 2 * b1 + n + 1)
                    for k in range(4):
                        last = nc.tensor.transpose(PB[:, n, k * P:(k + 1) * P],
                                                   a.t[:, n, 2 * k:2 * k + 2].rearrange("p h k -> p (h k)"), ident[:])
                    last.then_inc(done["p_transposed"], 1)
            if f2 is not None:
                wait(pe, o.done["vz"], 8 * before(a, f2))
                wait(pe, done["vz"], 8 * f2)
                pairs = []
                for kt in range(G):
                    src = D if a.cross else 0
                    cols = slice(src + kt * TOK, src + (kt + 1) * TOK)
                    wt = (wkv_hi[:, kt, D:2 * D], wkv_lo[:, kt, D:2 * D]) if a.cross else \
                        (wqkv_hi[:, kt, 2 * D:3 * D], wqkv_lo[:, kt, 2 * D:3 * D])
                    pairs.append(((a.hh[:, cols], a.hl[:, cols]), wt))
                three(V[:, 0:D], pairs).then_inc(done["v"], 1)
            if f1 is not None:
                wait(pe, done["hl"], before(o, f1))
                wait(pe, o.done["hl"], f1)
                if o.cross:
                    pe.wait_ge(s_ctx, 16 * (f1 + 1))
                    for kt in range(G):
                        nc.tensor.transpose(T[:, D + kt * TOK:D + (kt + 1) * TOK], ctok[:, kt * P:(kt + 1) * P], ident[:])
                pe.wait_ge(o.done["xc"], f1 + 1)
                for kt in range(G):
                    last = nc.tensor.transpose(T[:, kt * TOK:(kt + 1) * TOK], o.xc[:, kt * P:(kt + 1) * P], ident[:])
                last.then_inc(o.done["transposed"], 1)
            if b1 is not None:
                pe.wait_ge(done["vz"], 8 * b1 + 8)
                wait(pe, o.done["x"], before(a, b1))
                wait(pe, done["x"], b1)
                for n in range(2):
                    pe.wait_ge(done["pT"], 2 * b1 + n + 1)
                    for g in range(G):
                        for jj in range(2):
                            for h2 in range(2):
                                at_f = g * P + jj * S
                                last = mm(YO[S * jj:S * jj + S, g * TOK + n * S:g * TOK + (n + 1) * S],
                                          a.vz[:, n, h2, at_f:at_f + S], a.pT[:, 4 * n + 2 * g + jj, h2 * S:(h2 + 1) * S],
                                          start=(h2 == 0), stop=(h2 == 1))
                last.then_inc(done["y"], 1)
            if f2 is not None:
                pe.wait_ge(done["kT"], 2 * f2 + 2)
                wait(pe, o.done["masked"], 2 * before(a, f2))
                wait(pe, done["masked"], 2 * f2)
                for g in range(G):
                    for n in range(2):
                        pe.wait_ge(done["q8_g1" if g else "q8_g0"], 2 * f2 + n + 1)
                        for r in range(4):
                            hp = 4 * g + r
                            last = mm(SB[:, n, hp * S:(hp + 1) * S],
                                      a.q8[:, g, n, 2 * r:2 * r + 2].rearrange("p h q -> p (h q)"),
                                      a.kT[:, g, n * S:(n + 1) * S], start=True, stop=True)
                        if g == G - 1:
                            last.then_inc(done["s"], 1)

        in_steps(pe, half, after)


def layer1_mlp(nc, sb, psum, sem, block, w, x1, out):
    NG, GT = NP // 2, 2 * TOK
    M = FF // P
    w1_hi, w1_lo, w2_hi, w2_lo, bias1, bias2 = w.w1_hi, w.w1_lo, w.w2_hi, w.w2_lo, w.bias1, w.bias2
    ident = sb("ident2", [P, P], F32)
    neghalf = sb("neghalf2", [P, 2], F32)
    bnst = sb("mlp_bnst", [P, 2, 6], F32)
    mv = sb("mlp_mv", [P, 2, 2], F32)
    veps = sb("mlp_veps", [P, 2], F32)
    rstd = sb("mlp_rstd", [P, 2], F32)
    xc = sb("mlp_xc", [P, 2, D], F32)
    xb = sb("mlp_xb", [P, 2, D], F32)
    hh = sb("mlp_hh", [P, G, GT], F32R)
    hl = sb("mlp_hl", [P, G, GT], F32R)
    gf = sb("mlp_gelu", [P, M, GT], F32)
    gh = sb("mlp_gelu_high", [P, 2, M, GT], F32R)
    gl = sb("mlp_gelu_low", [P, 2, M, GT], F32R)
    res = sb("mlp_result", [P, 2, 2, D], F32)

    H = psum[:, 0:4]
    T, O = psum[:, 4], psum[:, 5]

    s_const, s_bf = sem("const2_set"), sem("bias1_folded")
    s_bn, s_mv, s_veps, s_rstd, s_xc = (sem("mlp_bn"), sem("mlp_mean_var"), sem("mlp_var_eps"), sem("mlp_rstd_done"),
                                        sem("mlp_centred"))
    s_t, s_hh, s_hl, s_h, s_g = (sem("mlp_transposed"), sem("mlp_high"), sem("mlp_low"), sem("mlp_hidden"),
                                 sem("mlp_gelu_done"))
    s_gh, s_gl, s_xb, s_o, s_res, s_tick = (sem("gelu_high"), sem("gelu_low"), sem("mlp_residual"), sem("mlp_out"),
                                            sem("mlp_summed"), sem("wait_carrier2"))
    s_out = [sem("stored0"), sem("stored1")]

    @block.sync
    def _(sp):
        def step(q):
            if exists(q, 0, NG):
                sp.wait_ge(s_res, q.idx + 1)
                sp.dma_start(out[bass.ds(q.idx * 4, 4)].rearrange("(i n) c s -> (n c) i s", n=2), res[:, q.par]
                             ).then_inc(s_out[q.par], 16)
        run_steps(sp, step, 0, NG - 1, 2, 5)
        for par in range(2):
            sp.wait_ge(s_out[par], 16 * NG // 2)

    @block.gpsimd
    def _(pool):
        nc.gpsimd.memset(ident[:], 0.0).then_inc(s_const, 1)
        nc.gpsimd.memset(neghalf[:], -0.5).then_inc(s_const, 1)
        pool.wait_ge(s_const, 2)
        nc.gpsimd.affine_select(out=ident[:], in_=ident[:], compare_op=ALU.not_equal, fill=1.0, base=0,
                                pattern=[[-1, P]], channel_multiplier=1).then_inc(s_const, 1)
        pool.wait_ge(s_const, 3)
        pool.wait_ge(w.loaded, 16 * len(w.loads))

        def step(q):
            if exists(q, 2, NG):
                n = q.next(2)
                pool.wait_ge(s_veps, n.idx + 1)
                wait(pool, s_xc, 2 * n.idx)
                nc.gpsimd.tensor_tensor(rstd[:], veps[:], neghalf[:], ALU.pow).then_inc(s_rstd, 1)
            if exists(q, 0, NG):
                wait(pool, s_res, q.idx)
                nc.gpsimd.tensor_tensor(xb[:], x1[:, bass.ds(q.idx * 2, 2)], bc(bias2[:], 1, 2), ALU.add).then_inc(s_xb, 1)

        step(Pair(-2, 0, -1))
        step(Pair(-1, 1, -1))
        run_steps(pool, step, 0, NG - 1, 2, 5)

    @block.scalar
    def _(act):
        act.wait_ge(s_bf, 1)

        def step(q):
            if exists(q, 1, NG):
                n = q.next()
                for m in range(M):
                    if m % 2 == 0:
                        act.wait_ge(s_h, 4 * n.idx + m // 2 + 1)
                    if m == 0:
                        wait(act, s_gl, 4 * n.idx)
                    nc.scalar.activation(gf[:, m], H[:, m // 2, m % 2 * GT:(m % 2 + 1) * GT], ACT.Gelu_apprx_tanh,
                                         bias=bias1[:, m:m + 1]).then_inc(s_g, 1)
                    if m % 2 == 1:
                        act.wait_ge(s_g, 8 * n.idx + m + 1)
                        wait(act, s_o, 2 * (n.idx - 1))
                        nc.scalar.copy(gh[:, n.par, m - 1:m + 1], gf[:, m - 1:m + 1]).then_inc(s_gh, 1)
            if exists(q, 2, NG):
                n = q.next(2)
                act.wait_ge(s_t, n.idx + 1)
                wait(act, s_h, 4 * n.idx)
                nc.scalar.copy(hh[:].rearrange("p k t -> p (k t)"), T).then_inc(s_hh, 1)

        step(Pair(-2, 0, -1))
        step(Pair(-1, 1, -1))
        run_steps(act, step, 0, NG - 1, 2, 5)

    @block.vector
    def _(dve):
        dve.wait_ge(w.multiplied, 1)
        nc.vector.tensor_tensor(bias1[:], w.product, bias1[:], ALU.add).then_inc(s_bf, 1)

        def norm(n):
            wait(dve, s_mv, 2 * n.idx)
            dve.sem_inc(s_tick, 1)
            for k in range(2):
                nc.vector.bn_stats(bnst[:, k], x1[:, n.idx * 2 + k]).then_inc(s_bn, 1)
            dve.wait_ge(s_bn, 2 * n.idx + 2)
            wait(dve, s_xc, 2 * n.idx)
            dve.sem_inc(s_tick, 1)
            for k in range(2):
                nc.vector.bn_aggr(mv[:, k], bnst[:, k]).then_inc(s_mv, 1)
            dve.wait_ge(s_mv, 2 * n.idx + 2)
            wait(dve, s_rstd, n.idx)
            nc.vector.tensor_scalar(veps[:], mv[:, :, 1], EPS, None, ALU.add).then_inc(s_veps, 1)

        def step(q):
            if exists(q, 2, NG):
                norm(q.next(2))
            if exists(q, 1, NG):
                n = q.next()
                for k in range(4):
                    dve.wait_ge(s_gh, 4 * n.idx + k + 1)
                    wait(dve, s_o, 2 * (n.idx - 1))
                    nc.vector.tensor_tensor(gl[:, n.par, 2 * k:2 * k + 2], gf[:, 2 * k:2 * k + 2],
                                            gh[:, n.par, 2 * k:2 * k + 2].bitcast(F32), ALU.subtract).then_inc(s_gl, 1)
                    if k == 0 and exists(q, 2, NG):
                        centre(q.next(2))
            elif exists(q, 2, NG):
                centre(q.next(2))
            if exists(q, 2, NG):
                n = q.next(2)
                dve.wait_ge(s_hh, n.idx + 1)
                wait(dve, s_h, 4 * n.idx)
                nc.vector.tensor_tensor(hl[:].rearrange("p k t -> p (k t)"), T,
                                        hh[:].rearrange("p k t -> p (k t)").bitcast(F32), ALU.subtract).then_inc(s_hl, 1)
            if exists(q, 0, NG):
                dve.wait_ge(s_o, 2 * q.idx + 2)
                dve.wait_ge(s_xb, q.idx + 1)
                wait(dve, s_out[q.par], 16 * q.before)
                nc.vector.tensor_tensor(res[:, q.par].rearrange("p i s -> p (i s)"), O,
                                        xb[:].rearrange("p i s -> p (i s)"), ALU.add).then_inc(s_res, 1)

        def centre(n):
            dve.wait_ge(s_rstd, n.idx + 1)
            wait(dve, s_t, n.idx)
            for k in range(2):
                nc.vector.tensor_scalar(xc[:, k], x1[:, n.idx * 2 + k], mv[:, k, 0:1], rstd[:, k:k + 1], ALU.subtract,
                                        ALU.mult).then_inc(s_xc, 1)

        step(Pair(-2, 0, -1))
        step(Pair(-1, 1, -1))
        run_steps(dve, step, 0, NG - 1, 2, 5)

    @block.tensor
    def _(pe):
        mm = nc.tensor.matmul
        pe.wait_ge(s_const, 3)
        pe.wait_ge(w.low, len(w.pieces))

        def step(q):
            if exists(q, 1, NG):
                n = q.next()
                pe.wait_ge(s_hl, n.idx + 1)
                for m in range(M):
                    if m % 2 == 0:
                        wait(pe, s_g, 8 * (n.idx - 1) + m + 2)
                    o = H[:, m // 2, m % 2 * GT:(m % 2 + 1) * GT]
                    for kt in range(G):
                        hi, lo = w1_hi[:, kt, m * P:(m + 1) * P], w1_lo[:, kt, m * P:(m + 1) * P]
                        mm(o, hi, hh[:, kt], start=(kt == 0), stop=False)
                        mm(o, lo, hh[:, kt], start=False, stop=False)
                        last = mm(o, hi, hl[:, kt], start=False, stop=(kt == G - 1))
                    if m % 2 == 1:
                        last.then_inc(s_h, 1)
            if exists(q, 2, NG):
                n = q.next(2)
                pe.wait_ge(s_xc, 2 * n.idx + 2)
                wait(pe, s_hl, n.idx)
                for k in range(2):
                    for kt in range(G):
                        last = nc.tensor.transpose(T[:, kt * GT + k * TOK:kt * GT + (k + 1) * TOK],
                                                   xc[:, k, kt * P:(kt + 1) * P], ident[:])
                last.then_inc(s_t, 1)
            if exists(q, 0, NG):
                pe.wait_ge(s_gl, 4 * q.idx + 4)
                wait(pe, s_res, q.idx)
                for k in range(2):
                    o = O[:, k * D:(k + 1) * D]
                    tok = slice(k * TOK, (k + 1) * TOK)
                    for m in range(M):
                        mm(o, gh[:, q.par, m, tok], w2_hi[:, m], start=(m == 0), stop=False)
                        mm(o, gh[:, q.par, m, tok], w2_lo[:, m], start=False, stop=False)
                        last = mm(o, gl[:, q.par, m, tok], w2_hi[:, m], start=False, stop=(m == M - 1))
                    last.then_inc(s_o, 1)

        step(Pair(-2, 0, -1))
        step(Pair(-1, 1, -1))
        run_steps(pe, step, 0, NG - 1, 2, 5)


def decoder(nc, x, ctx_2048, mask_1x1xSxS2_fc1, mask_Bx1xSxS2_ff1, L0_gamma, L0_beta, L0_Wq, L0_bq, L0_Wkv, L0_bkv,
            L0_Wo, L0_bo, ln1_s, ln1_b, w_qkv, b_qkv, w_ao, b_ao, ln2_s, ln2_b, w_q, b_q, w_kv, b_kv, w_co, b_co,
            ln3_s, ln3_b, w1, b1, w2, b2, out):
    with ExitStack() as kept:
        def enter(stack, make, *args):
            return stack.enter_context(make(*args))

        psum = enter(kept, nc.psum_tensor, "banks", [P, 8, 512], F32)
        x1 = enter(kept, nc.sbuf_tensor, "tokens", [P, NP, D], F32)

        def phase(build, *args):
            with ExitStack() as stack:
                def sb(name, shape, dt):
                    return enter(stack, nc.sbuf_tensor, name, shape, dt)

                def sem(name):
                    return enter(stack, nc.semaphore, name)
                with nc.Block() as block:
                    build(nc, sb, psum, sem, block, *args)

        with ExitStack() as raw:
            w_att = AttentionWeights(
                lambda *args: enter(raw, nc.sbuf_tensor, *args), lambda name: enter(kept, nc.semaphore, name),
                mask_1x1xSxS2_fc1, ln1_s, ln1_b, w_qkv, b_qkv, w_ao, b_ao, ln2_s, ln2_b, w_q, b_q, w_kv, b_kv, w_co, b_co)
            phase(layer0, x, ctx_2048, L0_gamma, L0_beta, L0_Wq, L0_bq, L0_Wkv, L0_bkv, L0_Wo, L0_bo, x1, w_att)
            with ExitStack() as both:
                w_mlp = MlpWeights(
                    lambda *args: enter(both, nc.sbuf_tensor, *args), lambda name: enter(kept, nc.semaphore, name),
                    psum, ln3_s, ln3_b, w1, b1, w2, b2)
                phase(layer1_attentions, ctx_2048, mask_Bx1xSxS2_ff1, w_att, w_mlp, x1)
                phase(layer1_mlp, w_mlp, x1, out)


_INS = ["x", "ctx_2048", "mask_1x1xSxS2_fc1", "mask_Bx1xSxS2_ff1", "L0_xattn_gamma", "L0_xattn_beta", "L0_xattn_Wq",
        "L0_xattn_bq", "L0_xattn_Wkv", "L0_xattn_bkv", "L0_xattn_Wo", "L0_xattn_bo"] + [
        "L1_xattn_" + k for k in ("ln1_s", "ln1_b", "w_qkv", "b_qkv", "w_ao", "b_ao", "ln2_s", "ln2_b", "w_q", "b_q",
                                  "w_kv", "b_kv", "w_co", "b_co", "ln3_s", "ln3_b", "w1", "b1", "w2", "b2")]


def kernel(**inputs):
    import numpy as _np
    import concourse.bacc as _bacc
    from concourse import mybir as _mybir
    from concourse.bass_utils import run_bass_kernel_spmd as _run

    nc = _bacc.Bacc("TRN2", target_bir_lowering=False, num_devices=1)
    arrays, args = {}, []
    for name in _INS:
        a = _np.ascontiguousarray(inputs[name])
        arrays[f"in_{name}"] = a
        args.append(nc.dram_tensor(f"in_{name}", a.shape, _mybir.dt.from_np(a.dtype), kind="ExternalInput").ap())
    args.append(nc.dram_tensor("out", (B, S, D), F32, kind="ExternalOutput").ap())
    decoder(nc, *args)
    r = _run(nc, [arrays], core_ids=[0])
    return r.results[0]["out"]
```
